# Optimizing a Trainium2 kernel written in Bass

```python
import numpy as np
import jax
import jax.numpy as jnp

def _softmax(x, axis=-1):
    return jax.nn.softmax(x, axis=axis)

def _gelu(x):
    return jax.nn.gelu(x, approximate=True)

def _silu(x):
    return jax.nn.silu(x)

def _sigmoid(x):
    return jax.nn.sigmoid(x)

def _layernorm(x, axis=-1, eps=1e-05):
    m = jnp.mean(x, axis=axis, keepdims=True)
    v = jnp.var(x, axis=axis, keepdims=True)
    return (x - m) / jnp.sqrt(v + eps)

def _scatter_add(tgt, idx, src, axis=0):
    return tgt.at[idx].add(src)

def _segment_sum(src, seg, n):
    return jax.ops.segment_sum(src, seg, n)
kernel_name = 'mk_macaron_d2_jaxref_r8_79d56a'

def setup_inputs(seed: int=0):
    np.random.seed(seed)
    _w = jnp.asarray

    def _L0_attn_setup():
        import jax, jax.numpy as jnp
        import numpy as np
        B, S, DIM = (2, 256, 128)
        H, DH = (16, 64)
        WIN = 64
        key = jax.random.key(seed)
        k1, k2, k3 = jax.random.split(key, 3)
        x = jax.random.normal(k1, (B, S, DIM), dtype=jnp.float32)
        Wqkv = jax.random.normal(k2, (DIM, 3 * H * DH), dtype=jnp.float32) * DIM ** (-0.5)
        Wout = jax.random.normal(k3, (H * DH, DIM), dtype=jnp.float32) * (H * DH) ** (-0.5)
        return {'x': x, 'Wqkv': Wqkv, 'Wout': Wout}
    _L0_attn_in = _L0_attn_setup()

    def _L0_ffn_setup():
        import jax, jax.numpy as jnp
        import numpy as np
        TOP_K = 2

        def _mlp(x, w_fc, w_proj):
            return jnp.square(jax.nn.relu(x @ w_fc.T)) @ w_proj.T
        key = jax.random.key(seed)
        ks = jax.random.split(key, 6)
        B, S, D, E = (4, 256, 128, 8)
        d_ff = 4 * D
        x = jax.random.normal(ks[0], (B, S, D), dtype=jnp.float32)
        router_w = jax.random.normal(ks[1], (E, D), dtype=jnp.float32) * 0.02
        w_fc = jax.random.normal(ks[2], (E, d_ff, D), dtype=jnp.float32) * 0.02
        w_proj = jax.random.normal(ks[3], (E, D, d_ff), dtype=jnp.float32) * 0.02
        shared_fc = jax.random.normal(ks[4], (d_ff, D), dtype=jnp.float32) * 0.02
        shared_proj = jax.random.normal(ks[5], (D, d_ff), dtype=jnp.float32) * 0.02
        return {'x': x, 'router_w': router_w, 'w_fc': w_fc, 'w_proj': w_proj, 'shared_fc': shared_fc, 'shared_proj': shared_proj}
    _L0_ffn_in = _L0_ffn_setup()

    def _L1_attn_setup():
        import jax, jax.numpy as jnp
        import numpy as np
        D_MODEL = 128
        N_HEADS = 16
        N_GROUPS = 4
        CONTEXT_LEN = 64
        D_H = D_MODEL // N_HEADS
        GROUP_SIZE = N_HEADS // N_GROUPS
        B, S = (4, 256)
        key = jax.random.key(seed)
        ks = jax.random.split(key, 9)
        s = 0.02
        return {'x': jax.random.normal(ks[0], (B, S, D_MODEL), dtype=jnp.float32), 'Wq': jax.random.normal(ks[1], (D_MODEL, D_MODEL), dtype=jnp.float32) * s, 'bq': jax.random.normal(ks[2], (D_MODEL,), dtype=jnp.float32) * s, 'Wk': jax.random.normal(ks[3], (D_MODEL, N_GROUPS * D_H), dtype=jnp.float32) * s, 'bk': jax.random.normal(ks[4], (N_GROUPS * D_H,), dtype=jnp.float32) * s, 'Wv': jax.random.normal(ks[5], (D_MODEL, N_GROUPS * D_H), dtype=jnp.float32) * s, 'bv': jax.random.normal(ks[6], (N_GROUPS * D_H,), dtype=jnp.float32) * s, 'Wo': jax.random.normal(ks[7], (D_MODEL, D_MODEL), dtype=jnp.float32) * s, 'bo': jax.random.normal(ks[8], (D_MODEL,), dtype=jnp.float32) * s}
    _L1_attn_in = _L1_attn_setup()

    def _L1_ffn_setup():
        import jax, jax.numpy as jnp
        import numpy as np
        TOP_K = 8
        key = jax.random.key(seed)
        ks = jax.random.split(key, 6)
        B, S, D, F, E = (2, 128, 128, 64, 64)
        x = jax.random.normal(ks[0], (B, S, D), dtype=jnp.float32)
        centroids = jax.random.normal(ks[1], (E, D), dtype=jnp.float32) * 0.05
        expert_biases = jnp.zeros((E,), dtype=jnp.float32)
        Ws_up = jax.random.normal(ks[2], (D, F), dtype=jnp.float32) / np.sqrt(D)
        Ws_down = jax.random.normal(ks[3], (F, D), dtype=jnp.float32) / np.sqrt(F)
        W_up = jax.random.normal(ks[4], (E, D, F), dtype=jnp.float32) / np.sqrt(D)
        W_down = jax.random.normal(ks[5], (E, F, D), dtype=jnp.float32) / np.sqrt(F)
        return {'x': x, 'centroids': centroids, 'expert_biases': expert_biases, 'Ws_up': Ws_up, 'Ws_down': Ws_down, 'W_up': W_up, 'W_down': W_down}
    _L1_ffn_in = _L1_ffn_setup()
    _d = {'L0_attn_x': _L0_attn_in['x'], 'L0_attn_Wqkv': _L0_attn_in['Wqkv'], 'L0_attn_Wout': _L0_attn_in['Wout'], 'L0_ffn_router_w': _L0_ffn_in['router_w'], 'L0_ffn_w_fc': _L0_ffn_in['w_fc'], 'L0_ffn_w_proj': _L0_ffn_in['w_proj'], 'L0_ffn_shared_fc': _L0_ffn_in['shared_fc'], 'L0_ffn_shared_proj': _L0_ffn_in['shared_proj'], 'L1_attn_Wq': _L1_attn_in['Wq'], 'L1_attn_bq': _L1_attn_in['bq'], 'L1_attn_Wk': _L1_attn_in['Wk'], 'L1_attn_bk': _L1_attn_in['bk'], 'L1_attn_Wv': _L1_attn_in['Wv'], 'L1_attn_bv': _L1_attn_in['bv'], 'L1_attn_Wo': _L1_attn_in['Wo'], 'L1_attn_bo': _L1_attn_in['bo'], 'L1_ffn_centroids': _L1_ffn_in['centroids'], 'L1_ffn_expert_biases': _L1_ffn_in['expert_biases'], 'L1_ffn_Ws_up': _L1_ffn_in['Ws_up'], 'L1_ffn_Ws_down': _L1_ffn_in['Ws_down'], 'L1_ffn_W_up': _L1_ffn_in['W_up'], 'L1_ffn_W_down': _L1_ffn_in['W_down']}
    _x0 = _d['L0_attn_x']
    _d['L0_attn_x'] = jax.random.normal(jax.random.fold_in(jax.random.key(seed), 1), (16, 256, 128), dtype=_x0.dtype)
    del _x0
    return _d

def reference(L0_attn_x, L0_attn_Wqkv, L0_attn_Wout, L0_ffn_router_w, L0_ffn_w_fc, L0_ffn_w_proj, L0_ffn_shared_fc, L0_ffn_shared_proj, L1_attn_Wq, L1_attn_bq, L1_attn_Wk, L1_attn_bk, L1_attn_Wv, L1_attn_bv, L1_attn_Wo, L1_attn_bo, L1_ffn_centroids, L1_ffn_expert_biases, L1_ffn_Ws_up, L1_ffn_Ws_down, L1_ffn_W_up, L1_ffn_W_down):

    def _L0_attn_ref(x, Wqkv, Wout):
        import jax, jax.numpy as jnp
        import numpy as np
        B, S, DIM = (2, 256, 128)
        H, DH = (16, 64)
        WIN = 64
        b, s, _ = x.shape
        qkv = jnp.einsum('bsd,de->bse', x, Wqkv)
        q, k, v = jnp.split(qkv, 3, axis=-1)
        q = q.reshape(b, s, H, DH).transpose(0, 2, 1, 3)
        k = k.reshape(b, s, H, DH).transpose(0, 2, 1, 3)
        v = v.reshape(b, s, H, DH).transpose(0, 2, 1, 3)
        scale = DH ** (-0.5)
        scores = jnp.einsum('bhsd,bhtd->bhst', q, k) * scale
        i = jnp.arange(s)[:, None]
        j = jnp.arange(s)[None, :]
        mask = (j >= i - WIN + 1) & (j <= i)
        mask_value = -jnp.finfo(scores.dtype).max
        scores = jnp.where(mask[None, None], scores, mask_value)
        attn = jax.nn.softmax(scores, axis=-1)
        out = jnp.einsum('bhst,bhtd->bhsd', attn, v)
        out = out.transpose(0, 2, 1, 3).reshape(b, s, H * DH)
        return jnp.einsum('bse,ed->bsd', out, Wout)

    def _L0_ffn_ref(x, router_w, w_fc, w_proj, shared_fc, shared_proj):
        import jax, jax.numpy as jnp
        import numpy as np
        TOP_K = 2

        def _mlp(x, w_fc, w_proj):
            return jnp.square(jax.nn.relu(x @ w_fc.T)) @ w_proj.T
        B, S, D = x.shape
        E = router_w.shape[0]
        T = B * S
        flat = x.reshape(T, D)
        logits = flat @ router_w.T
        probs = jax.nn.softmax(logits.astype(jnp.float32), axis=-1)
        topk_p, topk_i = jax.lax.top_k(probs, TOP_K)
        topk_w = (topk_p / jnp.maximum(topk_p.sum(-1, keepdims=True), 1e-09)).astype(flat.dtype)
        combine = jnp.zeros((T, E), dtype=flat.dtype)
        combine = combine.at[jnp.arange(T)[:, None], topk_i].add(topk_w)
        out = jnp.zeros_like(flat)
        for e in range(E):
            out = out + _mlp(flat, w_fc[e], w_proj[e]) * combine[:, e:e + 1]
        out = out + _mlp(flat, shared_fc, shared_proj)
        return out.reshape(B, S, D)

    def _L1_attn_ref(x, Wq, bq, Wk, bk, Wv, bv, Wo, bo):
        import jax, jax.numpy as jnp
        import numpy as np
        D_MODEL = 128
        N_HEADS = 16
        N_GROUPS = 4
        CONTEXT_LEN = 64
        D_H = D_MODEL // N_HEADS
        GROUP_SIZE = N_HEADS // N_GROUPS
        B, S = (4, 256)
        b, s = (x.shape[0], x.shape[1])
        q = (x @ Wq + bq).reshape(b, s, N_GROUPS, GROUP_SIZE, D_H)
        q = jnp.transpose(q, (0, 2, 3, 1, 4))
        k = jnp.transpose((x @ Wk + bk).reshape(b, s, N_GROUPS, D_H), (0, 2, 1, 3))
        v = jnp.transpose((x @ Wv + bv).reshape(b, s, N_GROUPS, D_H), (0, 2, 1, 3))
        scores = jnp.einsum('bghqd,bgkd->bghqk', q, k) / jnp.sqrt(jnp.float32(D_H))
        i = jnp.arange(s)
        j = jnp.arange(s)
        upper = (i - CONTEXT_LEN)[:, None] >= j[None, :]
        lower = i[:, None] < j[None, :]
        mask = upper | lower
        scores = jnp.where(mask, jnp.float32(-1000000000.0), scores)
        att = jax.nn.softmax(scores, axis=-1)
        out = jnp.einsum('bghqk,bgkd->bghqd', att, v)
        out = jnp.transpose(out, (0, 3, 1, 2, 4)).reshape(b, s, D_MODEL)
        return out @ Wo + bo

    def _L1_ffn_ref(x, centroids, expert_biases, Ws_up, Ws_down, W_up, W_down):
        import jax, jax.numpy as jnp
        import numpy as np
        TOP_K = 8
        B, S, D = x.shape
        E = centroids.shape[0]
        T = B * S
        xf = x.reshape(T, D)
        shared = jax.nn.silu(xf @ Ws_up) @ Ws_down
        aff = xf @ centroids.T
        biased = aff + expert_biases
        _, idx = jax.lax.top_k(biased, TOP_K)
        sel = jnp.take_along_axis(aff, idx, axis=1)
        w = jax.nn.sigmoid(sel)
        w = w / (jnp.sum(w, axis=-1, keepdims=True) + 1e-08)
        cw = jnp.zeros((T, E), dtype=x.dtype).at[jnp.arange(T)[:, None], idx].add(w)
        h = jax.nn.silu(jnp.einsum('td,edf->etf', xf, W_up))
        y = jnp.einsum('etf,efd->etd', h, W_down)
        routed = jnp.einsum('etd,te->td', y, cw)
        return (shared + routed).reshape(B, S, D)
    x = L0_attn_x
    x = x + 0.5 * _L0_ffn_ref(_layernorm(x, axis=-1), L0_ffn_router_w, L0_ffn_w_fc, L0_ffn_w_proj, L0_ffn_shared_fc, L0_ffn_shared_proj)
    x = x + _L0_attn_ref(_layernorm(x, axis=-1), L0_attn_Wqkv, L0_attn_Wout)
    x = x + 0.5 * _L0_ffn_ref(_layernorm(x, axis=-1), L0_ffn_router_w, L0_ffn_w_fc, L0_ffn_w_proj, L0_ffn_shared_fc, L0_ffn_shared_proj)
    x = x + 0.5 * _L1_ffn_ref(_layernorm(x, axis=-1), L1_ffn_centroids, L1_ffn_expert_biases, L1_ffn_Ws_up, L1_ffn_Ws_down, L1_ffn_W_up, L1_ffn_W_down)
    x = x + _L1_attn_ref(_layernorm(x, axis=-1), L1_attn_Wq, L1_attn_bq, L1_attn_Wk, L1_attn_bk, L1_attn_Wv, L1_attn_bv, L1_attn_Wo, L1_attn_bo)
    x = x + 0.5 * _L1_ffn_ref(_layernorm(x, axis=-1), L1_ffn_centroids, L1_ffn_expert_biases, L1_ffn_Ws_up, L1_ffn_Ws_down, L1_ffn_W_up, L1_ffn_W_down)
    return x

_drawn_inputs = setup_inputs


def setup_inputs(seed=0):
    import zlib

    import numpy as np

    out = dict(_drawn_inputs(seed))
    spreads = {'L1_ffn_expert_biases': (0.0, 0.1)}
    factors = {'L1_attn_Wq': 8.0,
     'L1_attn_bq': 8.0,
     'L1_attn_Wk': 8.0,
     'L1_attn_bk': 64.0,
     'L1_attn_Wv': 3.87,
     'L1_attn_bv': 6.82,
     'L1_attn_Wo': 3.808,
     'L1_attn_bo': 2.762}
    for name, (base, spread) in spreads.items():
        noise = np.random.default_rng([zlib.crc32(name.encode()), seed]).standard_normal(out[name].shape)
        drawn = base * np.exp(spread * noise) if base else spread * noise
        out[name] = jnp.asarray(drawn.astype(out[name].dtype))
    for name, factor in factors.items():
        out[name] = (out[name] * factor).astype(out[name].dtype)
    return out
```

```python
from contextlib import ExitStack

import concourse.bass as bass
from concourse import mybir

ALU = mybir.AluOpType
ACT = mybir.ActivationFunctionType
F32 = mybir.dt.float32
F32R = mybir.dt.float32r
BF16 = mybir.dt.bfloat16
U32 = mybir.dt.uint32
AX_X = mybir.AxisListType.X

P = 128
D = 128
TILES = 32
GT = 4
GROUPS = TILES // GT
BT = 2
BATCHES = TILES // BT
N = GT * P

E0, FF0 = 8, 512
E1, FF1, TOPK1 = 64, 64, 8
NC0 = (E0 + 1) * FF0 // P
SH0 = FF0 // P
NC1 = 1 + E1 * FF1 // P
H0, DH0 = 16, 64
H1, KV1, DH1 = 16, 4, 8
WINDOW = 64
LAG = 4
UPB = 3
RING = 6
HR = 3
EPS = 1e-5
MASKED = -1e30
PIECE = 768

PHASES = ("F0", "A0", "F0", "F1", "A1", "F1")
ITEMS = {"F0": GROUPS, "F1": GROUPS, "A0": BATCHES, "A1": BATCHES}


class Signal:

    def __init__(self, sem, **per):
        self.sem, self.per = sem, per

    def at(self, ph, it, k):
        base = sum(self.per.get(q, 0) * ITEMS[q] for q in PHASES[:ph])
        return it * self.per.get(PHASES[ph], 0) + (base + k)

    def past(self, ph, it, k):
        return not isinstance(it, int) or it * self.per[PHASES[ph]] + k > 0


class Attention:

    def __init__(self, kind, heads_a_chunk, dh, jobs):
        self.kind, self.heads_a_chunk, self.dh = kind, heads_a_chunk, dh
        self.rows = P // heads_a_chunk
        self.chunks = HEADS // heads_a_chunk
        self.scale = dh ** -0.5
        self.jobs = jobs
        assert len(jobs) % 2 == 0

    def before(self, item, index):
        back = 0
        while item >= -1:
            index -= 2
            if index < 0:
                index += len(self.jobs)
                back += 1
                item = {3: 2, 2: 1, 1: 1, 0: -1, -1: -2}[item]
                if item == -2:
                    return None
            _, name, number = self.jobs[index]
            if (item not in (-1, 0) or name in NEXT) and (item < 2 or name not in NEXT):
                return back, name, number


HEADS = 16
NEXT = ("XT", "QK", "V")
A0 = Attention("A0", 2, DH0, [
    (0, "OT", 0), (1, "OT", 1), (3, "XT", 0), (5, "QK", 0), (6, "OT", 2), (7, "OT", 3), (8, "QK", 1),
    (9, "Y", 0), (10, "QK", 2), (10, "V", 0), (11, "QK", 3), (12, "QK", 4), (12, "V", 1), (13, "QK", 5),
    (14, "QK", 6), (14, "V", 2), (15, "QK", 7), (15, "V", 3)])
A1 = Attention("A1", 4, DH1, [
    (3, "XT", 0), (5, "OT", 0), (6, "QK", 0), (7, "Y", 0), (8, "QK", 1), (9, "QK", 2), (10, "QK", 3), (11, "V", 0)])


def build(nc, x_in, w0_in, router_in, wqkv_in, wout_in, w1_in, cent_in, bias1_in, const_in, sel_in,
          wa1_in, bqk1_in, wo1_in, brow1_in, out):
    with ExitStack() as ctx:
        def sem(name):
            return ctx.enter_context(nc.semaphore(name))

        at = {"byte": 0}

        def place(name, shape, dt, region=None):
            size = 4 if dt in (F32, F32R, U32) else 2
            for n in shape[1:]:
                size *= n
            size = (size + 31) // 32 * 32
            where = region if region is not None else at
            t = nc.alloc_sbuf_tensor_at(name, shape, dt, offset=where["byte"])
            where["byte"] += size
            assert where["byte"] <= where.get("end", 224 * 1024), name
            return t

        A_START, A_SIZE = 1280, NC0 * 256 * 4 * 2
        B_START, B_SIZE = A_START + A_SIZE, NC1 * 256 * 4 * 2 + 4096
        at["byte"] = B_START + B_SIZE

        def region_a():
            return {"byte": A_START, "end": A_START + A_SIZE}

        def region_b():
            return {"byte": B_START, "end": B_START + B_SIZE}

        r = region_a()
        w0hi = place("w0hi", [P, NC0, 256], F32R, r)
        w0lo = place("w0lo", [P, NC0, 256], F32R, r)
        r = region_b()
        w1hi = place("w1hi", [P, NC1, 256], F32R, r)
        w1lo = place("w1lo", [P, NC1, 256], F32R, r)

        x = place("x", [P, TILES, D], F32)
        stage = place("stage", [P, 2, PIECE], F32)
        xn = place("xn", [P, 2, GT, D], F32)
        xthi = place("xthi", [P, 2, N], F32R)
        xtlo = place("xtlo", [P, 2, N], F32R)
        acc_sb = place("acc_sb", [P, N], F32)
        ident = place("ident", [P, P], F32)
        mask = place("mask", [P, 320], F32)
        iota8 = place("iota8", [P, E0], F32)
        router = place("router", [P, 8 + 64], F32)
        rthi = place("rthi", [P, 8 + 64], F32R)
        rtlo = place("rtlo", [P, 8 + 64], F32R)
        stats = place("stats", [P, GT, 6], F32)
        mv = place("mv", [P, GT, 2], F32)
        var = place("var", [P, GT], F32)
        rstd = place("rstd", [P, GT], F32)
        phalf = place("phalf", [P, 8], F32)
        nhalf = place("nhalf", [P, GT], F32)

        def ffn_scratch(tag, r):
            return {
                "r": place("r" + tag, [P, 2, N], F32, r),
                "h": place("h" + tag, [P, HR, N], F32, r),
                "hhi": place("hhi" + tag, [P, RING, N], F32R, r),
                "hlo": place("hlo" + tag, [P, RING, N], F32R, r),
            }

        rb = region_b()
        f0 = ffn_scratch("0", rb)
        xe = place("xe", [P, 2, GT, D], F32, rb)
        xehi = place("xehi", [P, 2, N], F32R, rb)
        xelo = place("xelo", [P, 2, N], F32R, rb)
        g_e = place("g_e", [P, GT, E0], F32, rb)
        g_x = place("g_x", [P, GT, E0], F32, rb)
        g_p = place("g_p", [P, GT, E0], F32, rb)
        g_mx = place("g_mx", [P, GT, 8], F32, rb)
        g_ix = place("g_ix", [P, GT, 8], U32, rb)
        g_if = place("g_if", [P, GT, 2], F32, rb)
        g_s = place("g_s", [P, 8, GT], F32, rb)
        g_w = place("g_w", [P, GT, 2], F32, rb)
        g_sq = place("g_sq", [P, GT, 2], F32, rb)
        g_m = place("g_m", [P, 4, GT, E0], F32, rb)
        gate = place("gate", [P, 2, GT, E0], F32, rb)

        ra = region_a()
        sel = place("sel", [96, 16, P], BF16, ra)
        ident_b = place("ident_b", [P, P], BF16, ra)
        e_bias = place("e_bias", [P, E1], F32, ra)
        after_consts = dict(ra)
        f1 = ffn_scratch("1", ra)
        cwt = place("cwt", [96, 2, 2, N], BF16, ra)
        e_b = place("e_b", [P, GT, E1], F32, ra)
        e_sig = place("e_sig", [P, GT, E1], F32, ra)
        e_mx = place("e_mx", [P, GT, 8], F32, ra)
        e_rep = place("e_rep", [P, GT, E1], F32, ra)
        e_m = place("e_m", [P, GT, E1], F32, ra)
        e_w = place("e_w", [P, GT, E1], F32, ra)
        e_s = place("e_s", [P, 4, GT], F32, ra)
        e_cw = place("e_cw", [P, GT, E1], F32, ra)
        e_r1 = place("e_r1", [P, GT, E1], F32, ra)
        e_r2 = place("e_r2", [P, GT, E1], F32, ra)
        parts = place("parts", [P, GT, 2, 3, 32], BF16, ra)

        rb = region_b()
        wqkv_hi = place("wqkv_hi", [P, 3 * HEADS * DH0], F32R, rb)
        wqkv_lo = place("wqkv_lo", [P, 3 * HEADS * DH0], F32R, rb)
        wout = place("wout", [P, 8, D], F32, rb)
        o_sb0 = place("o_sb0", [P, BT, HEADS * DH0], F32, rb)
        ra = dict(after_consts)
        wa1_hi = place("wa1_hi", [P, 1024 + KV1 * DH1], F32R, ra)
        wa1_lo = place("wa1_lo", [P, 1024 + KV1 * DH1], F32R, ra)
        wo1 = place("wo1", [P, D], F32, ra)
        brow1 = place("brow1", [1, P + D + KV1 * DH1], F32, ra)
        bqk1 = place("bqk1", [P, 8], F32, ra)
        qk1 = place("qk1", [P, 2, 4, 2, 256], F32, ra)
        v1 = place("v1", [P, 2, BT, KV1 * DH1], F32, ra)
        o_sb1 = place("o_sb1", [P, BT, D], F32, ra)
        ot1 = place("ot1", [P, BT, D], F32, ra)
        MASKEDS = {"A0": place("masked0", [P, 2, 320], F32, rb), "A1": place("masked1", [P, 2, 320], F32, ra)}
        PTS = {"A0": place("pt0", [P, 4, 384], F32, rb), "A1": place("pt1", [P, 4, 384], F32, ra)}
        probs = place("probs", [P, 4, 384], F32)
        negmax = place("negmax", [P, 4, BT], F32)
        sums = place("sums", [P, 2, BT, HEADS], F32)
        rsums = place("rsums", [P, 2, BT, HEADS], F32)
        v0 = place("v0", [P, 2, BT, HEADS * DH0], F32, rb)
        ot0 = place("ot0", [P, BT, 8, P], F32, rb)
        qk0 = place("qk0", [P, 2, 8, 2, 256], F32)
        QK = {"A0": qk0, "A1": qk1}

        bank = [ctx.enter_context(nc.psum_tensor(f"bank{i}", [P, 512], F32)) for i in range(8)]
        MISC = 6

        def acc_bank(par):
            return bank[3 + 4 * par]

        dma_const = sem("dma_const")
        dma_sel = sem("dma_sel")
        dma_wout = sem("dma_wout")
        dma_a1 = sem("dma_a1")
        dma_x0 = sem("dma_x0")
        dma_x = sem("dma_x")
        dma_stage = [sem("dma_stage0"), sem("dma_stage1")]
        dma_out = sem("dma_out")
        consts_made = sem("consts_made")
        router_split = sem("router_split")
        w_hi = sem("w_hi")
        w_lo = sem("w_lo")
        phase_done = sem("phase_done")

        carried = sem("carried")

        def carry(eng):
            eng.sem_inc(carried, 1)

        var_ready = Signal(sem("var_ready"), F0=1, F1=1, A0=1, A1=1)
        stat_step = Signal(sem("stat_step"), F0=2, F1=2, A0=2, A1=2)
        rstd_ready = Signal(sem("rstd_ready"), F0=1, F1=1, A0=1, A1=1)
        xn_ready = Signal(sem("xn_ready"), F0=1, F1=1, A0=1, A1=1)
        xn_turned = Signal(sem("xn_turned"), F0=1, F1=1, A0=1, A1=1)
        xt_hi = Signal(sem("xt_hi"), F0=1, F1=1, A0=1, A1=1)
        xt_lo = Signal(sem("xt_lo"), F0=1, F1=1, A0=1, A1=1)
        logits = Signal(sem("logits"), F0=1, F1=1)
        logits_read = Signal(sem("logits_read"), F0=1, F1=1)
        gate_dve = Signal(sem("gate_dve"), F0=22, F1=20)
        gate_exp = Signal(sem("gate_exp"), F0=1)
        gate_sqrt = Signal(sem("gate_sqrt"), F0=1)
        gate_sig = Signal(sem("gate_sig"), F1=1)
        cw_turned = Signal(sem("cw_turned"), F1=1)
        cwt_ready = Signal(sem("cwt_ready"), F1=1)
        up_done = Signal(sem("up_done"), F0=NC0, F1=NC1)
        act_done = Signal(sem("act_done"), F0=NC0, F1=NC1)
        h_ready = Signal(sem("h_ready"), F0=NC0, F1=NC1)
        hi_ready = Signal(sem("hi_ready"), F0=NC0, F1=NC1)
        lo_ready = Signal(sem("lo_ready"), F0=NC0, F1=NC1)
        down_done = Signal(sem("down_done"), F0=NC0, F1=NC1)
        xe_ready = Signal(sem("xe_ready"), F0=E0)
        xe_turned = Signal(sem("xe_turned"), F0=E0)
        xe_hi = Signal(sem("xe_hi"), F0=E0)
        xe_lo = Signal(sem("xe_lo"), F0=E0)
        cb_done = Signal(sem("cb_done"), F1=NC1 - 1)
        scores = Signal(sem("scores"), A0=HEADS, A1=HEADS)
        masked_ready = Signal(sem("masked_ready"), A0=HEADS, A1=HEADS)
        exp_done = Signal(sem("exp_done"), A0=HEADS, A1=HEADS)
        p_turned = Signal(sem("p_turned"), A0=HEADS, A1=HEADS)
        pt_ready = Signal(sem("pt_ready"), A0=HEADS, A1=HEADS)
        pv_done = Signal(sem("pv_done"), A0=HEADS, A1=HEADS)
        rsum_ready = Signal(sem("rsum_ready"), A0=2, A1=2)
        o_ready = Signal(sem("o_ready"), A0=2, A1=2)
        qk_done = Signal(sem("qk_done"), A0=8, A1=4)
        qk_ready = Signal(sem("qk_ready"), A0=8, A1=4)
        v_done = Signal(sem("v_done"), A0=4, A1=1)
        v_ready = Signal(sem("v_ready"), A0=4, A1=1)
        ot_done = Signal(sem("ot_done"), A0=4, A1=1)
        ot_ready = Signal(sem("ot_ready"), A0=4, A1=1)
        job_read = {"XT": xt_lo, "QK": qk_ready, "V": v_ready, "OT": ot_ready}
        acc_copied = Signal(sem("acc_copied"), F0=1, F1=1)
        y_turned = Signal(sem("y_turned"), F0=1, F1=1)
        y_done = Signal(sem("y_done"), A0=1, A1=1)
        x_added = Signal(sem("x_added"), F0=1, F1=1, A0=1, A1=1)
        job_read["Y"] = x_added

        pieces = []

        def add_pieces(dram, hi, lo, cols):
            first = len(pieces)
            for c in range(0, cols, PIECE):
                n = min(PIECE, cols - c)
                pieces.append((dram[:, c:c + n], hi[:, c:c + n], lo[:, c:c + n], n))
            return first, len(pieces)

        def flat(t):
            return t[:].rearrange("p c k -> p (c k)")

        P0 = add_pieces(w0_in, flat(w0hi), flat(w0lo), NC0 * 256)
        PA0 = add_pieces(wqkv_in, wqkv_hi[:], wqkv_lo[:], 3 * HEADS * DH0)
        P1 = add_pieces(w1_in, flat(w1hi), flat(w1lo), NC1 * 256)
        PA1 = add_pieces(wa1_in, wa1_hi[:], wa1_lo[:], 1024 + KV1 * DH1)
        PIECES = {PHASES.index(kind): p for kind, p in (("F0", P0), ("A0", PA0), ("F1", P1), ("A1", PA1))
                  if kind in PHASES}
        CPP = PIECE // 256

        block = ctx.enter_context(nc.Block())

        def items(eng, ph, item):
            n = ITEMS[PHASES[ph]]
            item(0, 0, True, False)
            with eng.Fori(0, n // 2 - 1) as k:
                item(2 * k + 1, 1, False, False)
                item(2 * k + 2, 0, False, False)
            item(n - 1, 1, False, True)

        def enter(eng, ph):
            if ph:
                eng.wait_ge(phase_done, 4 * ph)

        def leave(eng):
            eng.drain().then_inc(phase_done, 1)

        @block.sync
        def _(sp):
            xv = x_in.rearrange("b (u p) d -> p (b u) d", p=P)
            ov = out.rearrange("b (u p) d -> p (b u) d", p=P)
            sp.dma_start(x[:, 0:GT, :], xv[:, 0:GT, :]).then_inc(dma_x0, 16)
            sp.dma_start(ident[:], const_in[:, 256:384]).then_inc(dma_const, 16)
            sp.dma_start(router[:, 0:8], router_in).then_inc(dma_const, 16)
            sp.dma_start(router[:, 8:72], cent_in).then_inc(dma_const, 16)
            sp.dma_start(mask[:], const_in[:, 384:704]).then_inc(dma_const, 16)
            sp.dma_start(iota8[:], const_in[:, 704:712]).then_inc(dma_const, 16)
            for i, (dram, _, _, n) in enumerate(pieces):
                if i == PA0[0]:
                    sp.wait_ge(phase_done, 4 * PHASES.index("A0"))
                    sp.dma_start(wout[:], wout_in.rearrange("(c p) d -> p c d", p=P)).then_inc(dma_wout, 16)
                if i == P1[0]:
                    sp.wait_ge(phase_done, 4 * PHASES.index("F1"))
                    sp.dma_start(sel[:], sel_in[0:96, 0:2048].rearrange("p (c k) -> p c k", c=16)).then_inc(dma_sel, 16)
                    sp.dma_start(ident_b[:], sel_in[:, 2048:2176]).then_inc(dma_sel, 16)
                    sp.dma_start(e_bias[:], bias1_in.rearrange("(a e) -> a e", a=1).broadcast_to([P, E1])).then_inc(dma_sel, 16)
                if i == PA1[0]:
                    sp.wait_ge(phase_done, 4 * PHASES.index("A1"))
                    sp.dma_start(wo1[:], wo1_in).then_inc(dma_a1, 16)
                    sp.dma_start(bqk1[:], bqk1_in).then_inc(dma_a1, 16)
                    sp.dma_start(brow1[:], brow1_in).then_inc(dma_a1, 16)
                if i >= 2:
                    sp.wait_ge(w_lo, i - 1)
                sp.dma_start(stage[:, i % 2, 0:n], dram).then_inc(dma_stage[i % 2], 16)
                if i == 1:
                    for g in range(1, GROUPS):
                        sp.dma_start(x[:, GT * g:GT * g + GT, :], xv[:, GT * g:GT * g + GT, :]).then_inc(dma_x, 16)
            for q in range(4):
                sp.wait_ge(x_added.sem, x_added.at(len(PHASES) - 1, 2 * q + 1, 1))
                sp.dma_start(ov[:, 8 * q:8 * q + 8, :], x[:, 8 * q:8 * q + 8, :]).then_inc(dma_out, 16)
            sp.wait_ge(dma_out, 64)

        @block.gpsimd
        def _(pool):
            nc.gpsimd.memset(phalf[:], 0.5).then_inc(consts_made, 1)
            nc.gpsimd.memset(nhalf[:], -0.5).then_inc(consts_made, 1)
            nc.gpsimd.memset(probs[:], 0.0).then_inc(consts_made, 1)
            pool.wait_ge(consts_made, 3)

            def piece_hi(i):
                _, hi, _, n = pieces[i]
                pool.wait_ge(dma_stage[i % 2], 16 * (i // 2 + 1))
                nc.gpsimd.tensor_scalar(hi, stage[:, i % 2, 0:n], 1.0, 1.0, ALU.mult, ALU.mult).then_inc(w_hi, 1)

            def rstd_of(ph, it, tiles):
                pool.wait_ge(var_ready.sem, var_ready.at(ph, it, 1))
                nc.gpsimd.tensor_tensor(rstd[:, 0:tiles], var[:, 0:tiles], nhalf[:, 0:tiles],
                                        ALU.pow).then_inc(rstd_ready.sem, 1)

            def sqrt_of(ph, it):
                pool.wait_ge(gate_dve.sem, gate_dve.at(ph, it, 14))
                nc.gpsimd.tensor_tensor(g_sq[:].rearrange("p t k -> p (t k)"), g_w[:].rearrange("p t k -> p (t k)"),
                                        phalf[:, 0:8], ALU.pow).then_inc(gate_sqrt.sem, 1)

            def gated_x(ph, it, par, e):
                if e == 0:
                    pool.wait_ge(gate_dve.sem, gate_dve.at(ph, it, gate_dve.per["F0"]))
                if xe_turned.past(ph, it, e - 1):
                    pool.wait_ge(xe_turned.sem, xe_turned.at(ph, it, e - 1))
                carry(pool)
                for j in range(GT):
                    ins = nc.gpsimd.tensor_scalar(xe[:, e % 2, j, :], xn[:, par, j, :],
                                                  gate[:, par, j, e:e + 1], 1.0, ALU.mult, ALU.mult)
                ins.then_inc(xe_ready.sem, 1)

            def f0_item(ph):
                def item(it, par, first, last):
                    for c in range(NC0):
                        if first and ph in PIECES and c % CPP == 0 and P0[0] + 2 + c // CPP < P0[1]:
                            piece_hi(P0[0] + 2 + c // CPP)
                        if c == 0:
                            gated_x(ph, it, par, 0)
                        if c % 4 == 1 and c // 4 + 1 < E0:
                            gated_x(ph, it, par, c // 4 + 1)
                        if c == 2 and not last:
                            rstd_of(ph, it + 1, GT)
                        if c == 28 and not last:
                            sqrt_of(ph, it + 1)
                        s = (par * NC0 + c)
                        pool.wait_ge(h_ready.sem, h_ready.at(ph, it, c + 1))
                        if down_done.past(ph, it, c + 1 - RING):
                            pool.wait_ge(down_done.sem, down_done.at(ph, it, c + 1 - RING))
                        carry(pool)
                        nc.gpsimd.tensor_scalar(f0["hhi"][:, s % RING, :], f0["h"][:, s % HR, :], 1.0, 1.0,
                                                ALU.mult, ALU.mult).then_inc(hi_ready.sem, 1)
                return item

            def f1_item(ph):
                def item(it, par, first, last):
                    if first and ph in PIECES:
                        for i in range(P1[0] + 2, P1[1]):
                            piece_hi(i)
                    if not last:
                        rstd_of(ph, it + 1, GT)
                return item

            def attention_item(ph):
                def item(it, par, first, last):
                    if not last:
                        rstd_of(ph, it + 1, BT)
                return item

            for ph, kind in enumerate(PHASES):
                enter(pool, ph)
                if ph in PIECES:
                    piece_hi(PIECES[ph][0])
                    piece_hi(PIECES[ph][0] + 1)
                if kind in ("F0", "F1"):
                    rstd_of(ph, 0, GT)
                    if kind == "F0":
                        sqrt_of(ph, 0)
                    items(pool, ph, f0_item(ph) if kind == "F0" else f1_item(ph))
                else:
                    rstd_of(ph, 0, BT)
                    for i in range(PIECES[ph][0] + 2, PIECES[ph][1]):
                        piece_hi(i)
                    items(pool, ph, attention_item(ph))
                leave(pool)

        @block.scalar
        def _(act):
            def xt_hi_of(ph, it, par, tiles):
                n = tiles * P
                act.wait_ge(xn_turned.sem, xn_turned.at(ph, it, 1))
                nc.scalar.activation(xthi[:, par, 0:n], bank[MISC][:, 0:n], ACT.Copy).then_inc(xt_hi.sem, 1)

            def acc_out(ph, it, par):
                act.wait_ge(down_done.sem, down_done.at(ph, it + 1, 0))
                if y_turned.past(ph, it, 0):
                    act.wait_ge(y_turned.sem, y_turned.at(ph, it, 0))
                nc.scalar.activation(acc_sb[:], acc_bank(par)[:], ACT.Copy).then_inc(acc_copied.sem, 1)

            def gate_exp_of(ph, it):
                act.wait_ge(gate_dve.sem, gate_dve.at(ph, it, 2))
                nc.scalar.activation(g_x[:], g_e[:], ACT.Exp).then_inc(gate_exp.sem, 1)

            def gate_sig_of(ph, it):
                act.wait_ge(logits_read.sem, logits_read.at(ph, it, 1))
                nc.scalar.activation(e_sig[:], bank[MISC][:, 0:GT * E1].rearrange("p (t e) -> p t e", t=GT),
                                     ACT.Sigmoid).then_inc(gate_sig.sem, 1)

            def cwt_of(ph, it, par):
                act.wait_ge(cw_turned.sem, cw_turned.at(ph, it, 1))
                nc.scalar.activation(cwt[:, par, :, :].rearrange("p h n -> p (h n)"),
                                     bank[MISC][0:96, :].bitcast(BF16), ACT.Copy).then_inc(cwt_ready.sem, 1)

            def xe_hi_of(ph, it, e):
                act.wait_ge(xe_turned.sem, xe_turned.at(ph, it, e + 1))
                used = SH0 + SH0 * (e - 1)
                if e >= 2:
                    act.wait_ge(up_done.sem, up_done.at(ph, it, used))
                elif up_done.past(ph, it, 0):
                    act.wait_ge(up_done.sem, up_done.at(ph, it, 0) - (1 - e) * SH0)
                nc.scalar.activation(xehi[:, e % 2, :], bank[4 + e % 2][:], ACT.Copy).then_inc(xe_hi.sem, 1)

            def act_of(ph, it, par, c, func, f, nch):
                s = par * nch + c
                act.wait_ge(up_done.sem, up_done.at(ph, it, c + 1))
                if h_ready.past(ph, it, c - 1):
                    act.wait_ge(h_ready.sem, h_ready.at(ph, it, c - 1))
                nc.scalar.activation(f["r"][:, s % 2, :], bank[s % UPB][:], func).then_inc(act_done.sem, 1)

            def square_of(ph, it, par, c):
                s = par * NC0 + c
                act.wait_ge(act_done.sem, act_done.at(ph, it, c + 1))
                if lo_ready.past(ph, it, c + 1 - HR):
                    act.wait_ge(lo_ready.sem, lo_ready.at(ph, it, c + 1 - HR))
                nc.scalar.activation(f0["h"][:, s % HR, :], f0["r"][:, s % 2, :], ACT.Square).then_inc(h_ready.sem, 1)

            def f0_item(ph):
                def item(it, par, first, last):
                    for c in range(NC0):
                        act_of(ph, it, par, c, ACT.Relu, f0, NC0)
                        if c >= 1:
                            square_of(ph, it, par, c - 1)
                        if c % 4 == 1 and c // 4 < E0:
                            xe_hi_of(ph, it, c // 4)
                        if c == 5 and not first:
                            acc_out(ph, it - 1, 1 - par)
                        if c == 12 and not last:
                            xt_hi_of(ph, it + 1, 1 - par, GT)
                        if c == 20 and not last:
                            gate_exp_of(ph, it + 1)
                    square_of(ph, it, par, NC0 - 1)
                    if last:
                        acc_out(ph, it, par)
                return item

            def hi_of(ph, it, par, c):
                s = par * NC1 + c
                act.wait_ge(h_ready.sem, h_ready.at(ph, it, c + 1))
                if down_done.past(ph, it, c + 1 - RING):
                    act.wait_ge(down_done.sem, down_done.at(ph, it, c + 1 - RING))
                nc.scalar.activation(f1["hhi"][:, s % RING, :], f1["h"][:, s % HR, :], ACT.Copy).then_inc(hi_ready.sem, 1)

            def f1_item(ph):
                def item(it, par, first, last):
                    for c in range(NC1):
                        act_of(ph, it, par, c, ACT.Silu, f1, NC1)
                        if c >= 1:
                            hi_of(ph, it, par, c - 1)
                        if c == 5 and not first:
                            acc_out(ph, it - 1, 1 - par)
                        if c == 12 and not last:
                            xt_hi_of(ph, it + 1, 1 - par, GT)
                        if c == 16 and not last:
                            gate_sig_of(ph, it + 1)
                        if c == 28 and not last:
                            cwt_of(ph, it + 1, 1 - par)
                    hi_of(ph, it, par, NC1 - 1)
                    if last:
                        acc_out(ph, it, par)
                return item

            def exp_of(ph, it, par, u):
                act.wait_ge(masked_ready.sem, masked_ready.at(ph, it, u + 1))
                if p_turned.past(ph, it, u - 3):
                    act.wait_ge(p_turned.sem, p_turned.at(ph, it, u - 3))
                for t in range(BT):
                    masked = MASKEDS[PHASES[ph]]
                    src = masked[:, u % 2, 0:128] if t == 0 else masked[:, u % 2, 128:320]
                    dst = probs[:, u % 4, 0:128] if t == 0 else probs[:, u % 4, 192:384]
                    ins = nc.scalar.activation(dst, src, ACT.Exp, bias=negmax[:, u % 4, t:t + 1], scale=-1.0,
                                               accum_out=sums[:, par, t, u:u + 1])
                ins.then_inc(exp_done.sem, 1)

            def job_act(ph, a, it, par, name, i):
                b = bank[6 + [j[1:] for j in a.jobs].index((name, i)) % 2]
                if name == "XT":
                    act.wait_ge(xn_turned.sem, xn_turned.at(ph, it, 1))
                    if v_done.past(ph, it - 1, 0):
                        act.wait_ge(v_done.sem, v_done.at(ph, it - 1, 0))
                        act.wait_ge(qk_done.sem, qk_done.at(ph, it - 1, 0))
                    nc.scalar.activation(xthi[:, par, 0:256], b[:, 0:256], ACT.Copy).then_inc(xt_hi.sem, 1)
                if name == "QK":
                    act.wait_ge(qk_done.sem, qk_done.at(ph, it, i + 1))
                    if scores.past(ph, it - 1, 0):
                        act.wait_ge(scores.sem, scores.at(ph, it - 1, 0))
                    if a is A0:
                        nc.scalar.activation(qk0[:, par, i, :, :].rearrange("p w n -> p (w n)"), b[:],
                                             ACT.Copy).then_inc(qk_ready.sem, 1)
                    else:
                        nc.scalar.activation(qk1[:, par, i, 0, :], b[:, 0:256], ACT.Identity, bias=bqk1[:, 2 * i:2 * i + 1])
                        nc.scalar.activation(qk1[:, par, i, 1, :], b[:, 256:512], ACT.Identity,
                                             bias=bqk1[:, 2 * i + 1:2 * i + 2]).then_inc(qk_ready.sem, 1)
                if name == "V":
                    act.wait_ge(v_done.sem, v_done.at(ph, it, i + 1))
                    if pv_done.past(ph, it - 1, 0):
                        act.wait_ge(pv_done.sem, pv_done.at(ph, it - 1, 0))
                    if a is A0:
                        half, t = divmod(i, 2)
                        nc.scalar.activation(v0[:, par, t, 512 * half:512 * half + 512], b[:], ACT.Copy).then_inc(v_ready.sem, 1)
                    else:
                        nc.scalar.activation(v1[:, par].rearrange("p t n -> p (t n)"), b[:, 0:64], ACT.Copy).then_inc(v_ready.sem, 1)
                if name == "OT":
                    act.wait_ge(ot_done.sem, ot_done.at(ph, it, i + 1))
                    if y_done.past(ph, it, 0):
                        act.wait_ge(y_done.sem, y_done.at(ph, it, 0))
                    if a is A0:
                        half, t = divmod(i, 2)
                        nc.scalar.activation(ot0[:, t, 4 * half:4 * half + 4, :].rearrange("p c n -> p (c n)"), b[:],
                                             ACT.Copy).then_inc(ot_ready.sem, 1)
                    else:
                        nc.scalar.activation(ot1[:].rearrange("p t n -> p (t n)"), b[:, 0:256], ACT.Copy).then_inc(ot_ready.sem, 1)

            def attention_item(ph, a):
                def item(it, par, first, last):
                    for u in range(HEADS):
                        exp_of(ph, it, par, u)
                        for step, name, i in a.jobs:
                            if step == u and name in NEXT and not last:
                                job_act(ph, a, it + 1, 1 - par, name, i)
                            if step == u and name == "OT" and not first:
                                job_act(ph, a, it - 1, 1 - par, name, i)
                    if last:
                        for _, name, i in a.jobs:
                            if name == "OT":
                                job_act(ph, a, it, par, name, i)
                return item

            act.wait_ge(consts_made, 3)
            for ph, kind in enumerate(PHASES):
                enter(act, ph)
                if kind in ("A0", "A1"):
                    a = A0 if kind == "A0" else A1
                    if a is A1:
                        act.wait_ge(dma_a1, 48)
                    for _, name, i in a.jobs:
                        if name in NEXT:
                            job_act(ph, a, 0, 0, name, i)
                    items(act, ph, attention_item(ph, a))
                if kind in ("F0", "F1"):
                    xt_hi_of(ph, 0, 0, GT)
                    if kind == "F0":
                        gate_exp_of(ph, 0)
                    else:
                        gate_sig_of(ph, 0)
                        cwt_of(ph, 0, 0)
                    items(act, ph, f0_item(ph) if kind == "F0" else f1_item(ph))
                leave(act)

        @block.vector
        def _(dve):
            def piece_lo(i):
                _, hi, lo, n = pieces[i]
                dve.wait_ge(w_hi, i + 1)
                nc.vector.tensor_tensor(lo, stage[:, i % 2, 0:n], hi.bitcast(F32), ALU.subtract).then_inc(w_lo, 1)

            def stats_of(ph, it, tiles, step):
                if step == 0:
                    for j in range(tiles):
                        ins = nc.vector.bn_stats(stats[:, j, :], x[:, bass.ds(it * tiles + j, 1), :].rearrange("p a d -> p (a d)"))
                    ins.then_inc(stat_step.sem, 1)
                if step == 1:
                    dve.wait_ge(stat_step.sem, stat_step.at(ph, it, 1))
                    carry(dve)
                    for j in range(tiles):
                        ins = nc.vector.bn_aggr(mv[:, j, :], stats[:, j, :])
                    ins.then_inc(stat_step.sem, 1)
                if step == 2:
                    dve.wait_ge(stat_step.sem, stat_step.at(ph, it, 2))
                    nc.vector.tensor_scalar(var[:, 0:tiles], mv[:, 0:tiles, 1], EPS, None, ALU.add).then_inc(var_ready.sem, 1)

            def xn_of(ph, it, par, tiles):
                dve.wait_ge(rstd_ready.sem, rstd_ready.at(ph, it, 1))
                for j in range(tiles):
                    ins = nc.vector.tensor_scalar(xn[:, par, j, :], x[:, bass.ds(it * tiles + j, 1), :].rearrange("p a d -> p (a d)"),
                                                  mv[:, j, 0:1], rstd[:, j:j + 1], ALU.subtract, ALU.mult)
                ins.then_inc(xn_ready.sem, 1)

            def xt_lo_of(ph, it, par, tiles, b=None):
                n = tiles * P
                b = bank[MISC] if b is None else b
                dve.wait_ge(xt_hi.sem, xt_hi.at(ph, it, 1))
                nc.vector.tensor_tensor(xtlo[:, par, 0:n], b[:, 0:n], xthi[:, par, 0:n].bitcast(F32),
                                        ALU.subtract).then_inc(xt_lo.sem, 1)

            def x_add(ph, it):
                dve.wait_ge(y_turned.sem, y_turned.at(ph, it, 1))
                xs = x[:, bass.ds(it * GT, GT), :].rearrange("p t d -> p (t d)")
                nc.vector.scalar_tensor_tensor(out=xs, in0=bank[MISC][:], scalar=0.5, in1=xs,
                                               op0=ALU.mult, op1=ALU.add).then_inc(x_added.sem, 1)

            def bc(ap, n):
                return ap.unsqueeze(2).broadcast_to([P, GT, n])

            def gate0(ph, it, par, k):
                step = gate_dve
                if k == 1:
                    dve.wait_ge(logits.sem, logits.at(ph, it, 1))
                elif k == 3:
                    dve.wait_ge(gate_exp.sem, gate_exp.at(ph, it, 1))
                elif k == 15:
                    dve.wait_ge(gate_sqrt.sem, gate_sqrt.at(ph, it, 1))
                if k > 1:
                    dve.wait_ge(step.sem, step.at(ph, it, k - 1))
                lg = bank[MISC][:, 0:GT * E0].rearrange("p (t e) -> p t e", t=GT)
                top, total, inv, den, denc, dinv = (g_s[:, i, :] for i in range(6))
                if k == 1:
                    ins = nc.vector.tensor_reduce(top, lg, AX_X, ALU.max)
                elif k == 2:
                    ins = nc.vector.tensor_tensor(g_e[:], lg, bc(top, E0), ALU.subtract)
                elif k == 3:
                    ins = nc.vector.tensor_reduce(total, g_x[:], AX_X, ALU.add)
                elif k == 4:
                    ins = nc.vector.reciprocal(inv, total)
                elif k == 5:
                    ins = nc.vector.tensor_tensor(g_p[:], g_x[:], bc(inv, E0), ALU.mult)
                elif k == 6:
                    carry(dve)
                    for j in range(GT):
                        ins = nc.vector.max(g_mx[:, j, :], g_p[:, j, :])
                elif k == 7:
                    carry(dve)
                    for j in range(GT):
                        ins = nc.vector.max_index(g_ix[:, j, :], g_mx[:, j, :], g_p[:, j, :])
                elif k == 8:
                    ins = nc.vector.tensor_copy(g_if[:], g_ix[:, :, 0:2])
                elif k == 9:
                    ins = nc.vector.tensor_tensor(den, g_mx[:, :, 0], g_mx[:, :, 1], ALU.add)
                elif k == 10:
                    ins = nc.vector.tensor_scalar(denc, den, 1e-9, None, ALU.max)
                elif k == 11:
                    ins = nc.vector.reciprocal(dinv, denc)
                elif k == 12:
                    ins = nc.vector.tensor_tensor(g_m[:, 0], iota8[:].unsqueeze(1).broadcast_to([P, GT, E0]),
                                                  bc(g_if[:, :, 0], E0), ALU.is_equal)
                elif k == 13:
                    ins = nc.vector.tensor_tensor(g_m[:, 1], iota8[:].unsqueeze(1).broadcast_to([P, GT, E0]),
                                                  bc(g_if[:, :, 1], E0), ALU.is_equal)
                elif k == 14:
                    ins = nc.vector.tensor_tensor(g_w[:], g_mx[:, :, 0:2], bc(dinv, 2), ALU.mult)
                elif k == 15:
                    ins = nc.vector.tensor_tensor(g_m[:, 2], g_m[:, 0], bc(g_sq[:, :, 0], E0), ALU.mult)
                elif k == 16:
                    ins = nc.vector.tensor_tensor(g_m[:, 3], g_m[:, 1], bc(g_sq[:, :, 1], E0), ALU.mult)
                elif k == 17:
                    ins = nc.vector.tensor_tensor(gate[:, par], g_m[:, 2], g_m[:, 3], ALU.add)
                if k == 2:
                    ins.then_inc(logits_read.sem, 1)
                    ins = nc.vector.tensor_copy(g_s[:, 7, :], top)
                ins.then_inc(step.sem, 1 if k < 17 else 6)

            def gate1(ph, it, par, k):
                step = gate_dve
                if k == 1:
                    dve.wait_ge(logits.sem, logits.at(ph, it, 1))
                elif k == 5:
                    dve.wait_ge(gate_sig.sem, gate_sig.at(ph, it, 1))
                if k > 1:
                    dve.wait_ge(step.sem, step.at(ph, it, k - 1))
                lg = bank[MISC][:, 0:GT * E1].rearrange("p (t e) -> p t e", t=GT)
                total, guard, inv = (e_s[:, i, :] for i in range(3))

                def halves(t):
                    return t[:].rearrange("p t (h e) -> p t h e", h=2)

                if k == 1:
                    ins = nc.vector.tensor_tensor(e_b[:], lg, e_bias[:].unsqueeze(1).broadcast_to([P, GT, E1]), ALU.add)
                    ins.then_inc(logits_read.sem, 1)
                    dve.wait_ge(logits_read.sem, logits_read.at(ph, it, 1))
                    carry(dve)
                    for j in range(GT):
                        ins = nc.vector.max(e_mx[:, j, :], e_b[:, j, :])
                elif k == 2:
                    carry(dve)
                    for j in range(GT):
                        ins = nc.vector.match_replace(e_rep[:, j, :], e_mx[:, j, :], e_b[:, j, :], -3e38)
                elif k == 3:
                    ins = nc.vector.tensor_tensor(e_m[:], e_b[:], e_rep[:], ALU.not_equal)
                elif k == 5:
                    ins = nc.vector.tensor_tensor(e_w[:], e_sig[:], e_m[:], ALU.mult)
                elif k == 6:
                    ins = nc.vector.tensor_reduce(total, e_w[:], AX_X, ALU.add)
                elif k == 7:
                    ins = nc.vector.tensor_scalar(guard, total, 1e-8, None, ALU.add)
                elif k == 8:
                    ins = nc.vector.reciprocal(inv, guard)
                elif k == 9:
                    ins = nc.vector.tensor_tensor(e_cw[:], e_w[:], bc(inv, E1), ALU.mult)
                elif k == 10:
                    ins = nc.vector.tensor_copy(parts[:, :, :, 0, :], halves(e_cw))
                elif k == 11:
                    ins = nc.vector.tensor_tensor(halves(e_r1), halves(e_cw), parts[:, :, :, 0, :], ALU.subtract)
                elif k == 12:
                    ins = nc.vector.tensor_copy(parts[:, :, :, 1, :], halves(e_r1))
                elif k == 13:
                    ins = nc.vector.tensor_tensor(halves(e_r2), halves(e_r1), parts[:, :, :, 1, :], ALU.subtract)
                elif k == 14:
                    ins = nc.vector.tensor_copy(parts[:, :, :, 2, :], halves(e_r2))
                elif k == 4:
                    ins = nc.vector.tensor_copy(e_s[:, 3, :], e_mx[:, :, 7])
                ins.then_inc(step.sem, 1 if k < 14 else 7)

            def xe_lo_of(ph, it, e):
                dve.wait_ge(xe_hi.sem, xe_hi.at(ph, it, e + 1))
                nc.vector.tensor_tensor(xelo[:, e % 2, :], bank[4 + e % 2][:], xehi[:, e % 2, :].bitcast(F32),
                                        ALU.subtract).then_inc(xe_lo.sem, 1)

            def lo_of(ph, it, par, c, f, nch):
                s = par * nch + c
                dve.wait_ge(hi_ready.sem, hi_ready.at(ph, it, c + 1))
                nc.vector.tensor_tensor(f["hlo"][:, s % RING, :], f["h"][:, s % HR, :], f["hhi"][:, s % RING, :].bitcast(F32),
                                        ALU.subtract).then_inc(lo_ready.sem, 1)

            def f0_item(ph):
                def item(it, par, first, last):
                    for c in range(NC0):
                        if first and ph in PIECES and c % CPP == 0 and P0[0] + 2 + c // CPP < P0[1]:
                            piece_lo(P0[0] + 2 + c // CPP)
                        if c % 4 == 1 and c // 4 < E0:
                            xe_lo_of(ph, it, c // 4)
                        if not last and c in (0, 1, 2):
                            if c == 0 and ph == 0 and first:
                                dve.wait_ge(dma_x, 16 * (GROUPS - 1))
                            stats_of(ph, it + 1, GT, c)
                        if c == 4 and not last:
                            xn_of(ph, it + 1, 1 - par, GT)
                        if c == 9 and not first:
                            x_add(ph, it - 1)
                        if c == 12 and not last:
                            xt_lo_of(ph, it + 1, 1 - par, GT)
                        if 18 <= c <= 27 and not last and (c != 18):
                            for k in {19: (1, 2), 20: (), 21: (3,), 22: (4, 5), 23: (6, 7), 24: (8, 9), 25: (10, 11), 26: (12, 13), 27: (14,)}[c]:
                                gate0(ph, it + 1, 1 - par, k)
                        if c in (30, 31, 32) and not last:
                            gate0(ph, it + 1, 1 - par, c - 15)
                        if c >= 1:
                            lo_of(ph, it, par, c - 1, f0, NC0)
                    lo_of(ph, it, par, NC0 - 1, f0, NC0)
                    if last:
                        x_add(ph, it)
                return item

            def mult_of(ph, it, par, c):
                s = par * NC1 + c
                dve.wait_ge(act_done.sem, act_done.at(ph, it, c + 1))
                if lo_ready.past(ph, it, c + 1 - HR):
                    dve.wait_ge(lo_ready.sem, lo_ready.at(ph, it, c + 1 - HR))
                hb, rb_ = f1["h"][:, s % HR, :], f1["r"][:, s % 2, :]
                if c == 0:
                    ins = nc.vector.tensor_copy(hb, rb_)
                else:
                    dve.wait_ge(cb_done.sem, cb_done.at(ph, it, c))
                    ins = nc.vector.tensor_tensor(hb, bank[4 + (c - 1) % 2][:], rb_, ALU.mult)
                ins.then_inc(h_ready.sem, 1)

            def f1_item(ph):
                def item(it, par, first, last):
                    if first and ph in PIECES:
                        for i in range(P1[0] + 2, P1[1]):
                            piece_lo(i)
                    for c in range(NC1):
                        if not last and c in (0, 1, 2):
                            stats_of(ph, it + 1, GT, c)
                        if c == 4 and not last:
                            xn_of(ph, it + 1, 1 - par, GT)
                        if c == 9 and not first:
                            x_add(ph, it - 1)
                        if c == 12 and not last:
                            xt_lo_of(ph, it + 1, 1 - par, GT)
                        if 15 <= c <= 22 and not last:
                            for k in {15: (1,), 16: (2,), 17: (3, 4), 18: (5, 6), 19: (7, 8), 20: (9, 10), 21: (11, 12), 22: (13, 14)}[c]:
                                gate1(ph, it + 1, 1 - par, k)
                        mult_of(ph, it, par, c)
                        if c >= 1:
                            lo_of(ph, it, par, c - 1, f1, NC1)
                    lo_of(ph, it, par, NC1 - 1, f1, NC1)
                    if last:
                        x_add(ph, it)
                return item

            def mask_of(ph, a, it, par, u):
                dve.wait_ge(scores.sem, scores.at(ph, it, u + 1))
                if exp_done.past(ph, it, u - 1):
                    dve.wait_ge(exp_done.sem, exp_done.at(ph, it, u - 1))
                carry(dve)
                for t in range(BT):
                    cols = slice(0, 128) if t == 0 else slice(128, 320)
                    ins = nc.vector.tensor_tensor_reduce(
                        out=MASKEDS[a.kind][:, u % 2, cols], in0=bank[u % 2][:, cols], in1=mask[:, cols], scale=-a.scale,
                        scalar=3e38, op0=ALU.add, op1=ALU.min, accum_out=negmax[:, u % 4, t:t + 1])
                ins.then_inc(masked_ready.sem, 1)

            def pt_of(ph, it, u):
                dve.wait_ge(p_turned.sem, p_turned.at(ph, it, u + 1))
                if pv_done.past(ph, it, u - 3):
                    dve.wait_ge(pv_done.sem, pv_done.at(ph, it, u - 3))
                nc.vector.tensor_copy(PTS[PHASES[ph]][:, u % 4, :], bank[2 + u % 2][:, 0:384]).then_inc(pt_ready.sem, 1)

            def norm_of(ph, a, it, par, half):
                hs = slice(8 * half, 8 * half + 8)
                dve.wait_ge(exp_done.sem, exp_done.at(ph, it, 8 * half + 8))
                nc.vector.reciprocal(rsums[:, par, :, hs], sums[:, par, :, hs]).then_inc(rsum_ready.sem, 1)
                dve.wait_ge(pv_done.sem, pv_done.at(ph, it, 8 * half + 8))
                if ot_done.past(ph, it, 0):
                    dve.wait_ge(ot_done.sem, ot_done.at(ph, it, 0))
                dve.wait_ge(rsum_ready.sem, rsum_ready.at(ph, it, half + 1))
                for t in range(BT):
                    r = rsums[:, par, t, hs].unsqueeze(2).broadcast_to([P, 8, a.dh])
                    if a is A0:
                        o, src = o_sb0[:, t, 512 * half:512 * half + 512], bank[4 + t][:]
                    else:
                        o, src = o_sb1[:, t, 64 * half:64 * half + 64], bank[4 + half][:, 64 * t:64 * t + 64]
                    ins = nc.vector.tensor_tensor(o.rearrange("p (h d) -> p h d", d=a.dh),
                                                  src.rearrange("p (h d) -> p h d", d=a.dh), r, ALU.mult)
                ins.then_inc(o_ready.sem, 1)

            def y_of(ph, a, it):
                b = bank[6 + [j[1] for j in a.jobs].index("Y") % 2]
                dve.wait_ge(y_done.sem, y_done.at(ph, it, 1))
                xs = x[:, bass.ds(it * BT, BT), :].rearrange("p t d -> p (t d)")
                nc.vector.tensor_tensor(xs, b[:, 0:256], xs, ALU.add).then_inc(x_added.sem, 1)

            def attention_item(ph, a):
                xt_bank = bank[6 + [j[1] for j in a.jobs].index("XT") % 2]
                y_step = [j[0] for j in a.jobs if j[1] == "Y"][0]

                def item(it, par, first, last):
                    for u in range(HEADS):
                        if u == 3 and not first:
                            norm_of(ph, a, it - 1, 1 - par, 1)
                        if u == 11:
                            norm_of(ph, a, it, par, 0)
                        mask_of(ph, a, it, par, u)
                        if u >= 2:
                            pt_of(ph, it, u - 2)
                        elif not first:
                            pt_of(ph, it - 1, u + HEADS - 2)
                        if not last:
                            if u == 0:
                                for step in range(3):
                                    stats_of(ph, it + 1, BT, step)
                            if u == 1:
                                xn_of(ph, it + 1, 1 - par, BT)
                            if u == 4:
                                xt_lo_of(ph, it + 1, 1 - par, BT, xt_bank)
                        if u == y_step + 1 and not first:
                            y_of(ph, a, it - 1)
                    if last:
                        pt_of(ph, it, HEADS - 2)
                        pt_of(ph, it, HEADS - 1)
                        norm_of(ph, a, it, par, 1)
                        y_of(ph, a, it)
                return item

            dve.wait_ge(dma_const, 80)
            nc.vector.tensor_copy(rthi[:], router[:]).then_inc(router_split, 1)
            dve.wait_ge(router_split, 1)
            nc.vector.tensor_tensor(rtlo[:], router[:], rthi[:].bitcast(F32), ALU.subtract).then_inc(router_split, 1)
            for ph, kind in enumerate(PHASES):
                enter(dve, ph)
                if ph == 0:
                    dve.wait_ge(dma_x0, 16)
                tiles = GT if kind in ("F0", "F1") else BT
                for step in range(3):
                    stats_of(ph, 0, tiles, step)
                xn_of(ph, 0, 0, tiles)
                if kind in ("A0", "A1"):
                    a = A0 if kind == "A0" else A1
                    xt_lo_of(ph, 0, 0, tiles, bank[6 + [j[1] for j in a.jobs].index("XT") % 2])
                else:
                    xt_lo_of(ph, 0, 0, tiles)
                if ph in PIECES:
                    piece_lo(PIECES[ph][0])
                    piece_lo(PIECES[ph][0] + 1)
                if kind in ("A0", "A1"):
                    for i in range(PIECES[ph][0] + 2, PIECES[ph][1]):
                        piece_lo(i)
                    items(dve, ph, attention_item(ph, a))
                if kind == "F0":
                    for k in range(1, 18):
                        gate0(ph, 0, 0, k)
                    items(dve, ph, f0_item(ph))
                if kind == "F1":
                    dve.wait_ge(dma_sel, 48)
                    for k in range(1, 15):
                        gate1(ph, 0, 0, k)
                    items(dve, ph, f1_item(ph))
                leave(dve)

        @block.tensor
        def _(pe):
            def three(o, whi, wlo, vhi, vlo, start=True, stop=True):
                nc.tensor.matmul(o, whi, vhi, start=start, stop=False)
                nc.tensor.matmul(o, whi, vlo, start=False, stop=False)
                return nc.tensor.matmul(o, wlo, vhi, start=False, stop=stop)

            def turn_xn(ph, it, par, tiles):
                pe.wait_ge(xn_ready.sem, xn_ready.at(ph, it, 1))
                if x_added.past(ph, it - 1, 0):
                    pe.wait_ge(x_added.sem, x_added.at(ph, it - 1, 0))
                if PHASES[ph] == "F1" and cwt_ready.past(ph, it, 0):
                    pe.wait_ge(cwt_ready.sem, cwt_ready.at(ph, it, 0))
                for j in range(tiles):
                    mm = nc.tensor.transpose(bank[MISC][:, j * P:(j + 1) * P], xn[:, par, j, :], ident[:])
                mm.then_inc(xn_turned.sem, 1)

            def route(ph, it, par, first_col, ne):
                pe.wait_ge(xt_lo.sem, xt_lo.at(ph, it, 1))
                cols = slice(first_col, first_col + ne)
                for j in range(GT):
                    o = bank[MISC][:, j * ne:(j + 1) * ne]
                    tok = slice(j * P, (j + 1) * P)
                    mm = three(o, xthi[:, par, tok], xtlo[:, par, tok], rthi[:, cols], rtlo[:, cols])
                mm.then_inc(logits.sem, 1)

            def turn_xe(ph, it, e):
                pe.wait_ge(xe_ready.sem, xe_ready.at(ph, it, e + 1))
                if xe_lo.past(ph, it, e - 1):
                    pe.wait_ge(xe_lo.sem, xe_lo.at(ph, it, e - 1))
                for j in range(GT):
                    mm = nc.tensor.transpose(bank[4 + e % 2][:, j * P:(j + 1) * P], xe[:, e % 2, j, :], ident[:])
                mm.then_inc(xe_turned.sem, 1)

            def turn_cw(ph, it):
                pe.wait_ge(gate_dve.sem, gate_dve.at(ph, it, gate_dve.per["F1"]))
                pe.wait_ge(gate_sig.sem, gate_sig.at(ph, it, 1))
                turned = bank[MISC][0:96, :].bitcast(BF16)
                for h in range(2):
                    for j in range(GT):
                        mm = nc.tensor.transpose(turned[:, (h * GT + j) * P:(h * GT + j + 1) * P],
                                                 parts[:, j, h, :, :].rearrange("p k e -> p (k e)"), ident_b[:])
                mm.then_inc(cw_turned.sem, 1)

            def turn_acc(ph, it, prepared):
                pe.wait_ge(acc_copied.sem, acc_copied.at(ph, it, 1))
                pe.wait_ge(logits_read.sem, logits_read.at(ph, prepared, 1))
                if PHASES[ph] == "F1":
                    pe.wait_ge(cwt_ready.sem, cwt_ready.at(ph, prepared, 1))
                for j in range(GT):
                    mm = nc.tensor.transpose(bank[MISC][:, j * P:(j + 1) * P], acc_sb[:, j * P:(j + 1) * P], ident[:])
                mm.then_inc(y_turned.sem, 1)

            def up(ph, it, par, c, nch, whi, wlo, vhi, vlo):
                s = par * nch + c
                if act_done.past(ph, it, c + 1 - UPB):
                    pe.wait_ge(act_done.sem, act_done.at(ph, it, c + 1 - UPB))
                three(bank[s % UPB][:], whi[:, c, 0:128], wlo[:, c, 0:128], vhi, vlo).then_inc(up_done.sem, 1)

            def down(ph, it, par, c, nch, whi, wlo, f):
                s = par * nch + c
                pe.wait_ge(lo_ready.sem, lo_ready.at(ph, it, c + 1))
                if c == 0 and acc_copied.past(ph, it, -1):
                    pe.wait_ge(acc_copied.sem, acc_copied.at(ph, it, -1))
                three(acc_bank(par)[:], whi[:, c, 128:256], wlo[:, c, 128:256], f["hhi"][:, s % RING, :],
                      f["hlo"][:, s % RING, :], start=(c == 0), stop=(c == nch - 1)).then_inc(down_done.sem, 1)

            def lagged_down(ph, it, par, c, first, nch, whi, wlo, f):
                if c >= LAG:
                    down(ph, it, par, c - LAG, nch, whi, wlo, f)
                elif not first:
                    down(ph, it - 1, 1 - par, nch + c - LAG, nch, whi, wlo, f)

            def tail(ph, it, par, nch, whi, wlo, f):
                for c in range(nch - LAG, nch):
                    down(ph, it, par, c, nch, whi, wlo, f)
                turn_acc(ph, it, it)

            def f0_item(ph):
                def item(it, par, first, last):
                    for c in range(NC0):
                        if first and ph in PIECES and c % CPP == 0:
                            pe.wait_ge(w_lo, P0[0] + c // CPP + 1)
                        if c % 4 == 0 and c // 4 < E0:
                            turn_xe(ph, it, c // 4)
                        if c < SH0:
                            vhi, vlo = xthi[:, par, :], xtlo[:, par, :]
                        else:
                            e = (c - SH0) // SH0
                            if c % SH0 == 0:
                                pe.wait_ge(xe_lo.sem, xe_lo.at(ph, it, e + 1))
                            vhi, vlo = xehi[:, e % 2, :], xelo[:, e % 2, :]
                        up(ph, it, par, c, NC0, w0hi, w0lo, vhi, vlo)
                        lagged_down(ph, it, par, c, first, NC0, w0hi, w0lo, f0)
                        if c == 7 and not first:
                            turn_acc(ph, it - 1, it)
                        if c == 11 and not last:
                            turn_xn(ph, it + 1, 1 - par, GT)
                        if c == 17 and not last:
                            route(ph, it + 1, 1 - par, 0, E0)
                    if last:
                        tail(ph, it, par, NC0, w0hi, w0lo, f0)
                return item

            def cb(ph, it, par, c):
                if c == 1:
                    pe.wait_ge(cwt_ready.sem, cwt_ready.at(ph, it, 1))
                if h_ready.past(ph, it, c - 1):
                    pe.wait_ge(h_ready.sem, h_ready.at(ph, it, c - 1))
                half, j = divmod(c - 1, 16)
                nc.tensor.matmul(bank[4 + (c - 1) % 2][:], sel[:, j, :], cwt[:, par, half, :],
                                 start=True, stop=True).then_inc(cb_done.sem, 1)

            def f1_item(ph):
                def item(it, par, first, last):
                    for c in range(NC1):
                        if first and ph in PIECES and c % CPP == 0:
                            pe.wait_ge(w_lo, P1[0] + c // CPP + 1)
                        up(ph, it, par, c, NC1, w1hi, w1lo, xthi[:, par, :], xtlo[:, par, :])
                        if c >= 1:
                            cb(ph, it, par, c)
                        lagged_down(ph, it, par, c, first, NC1, w1hi, w1lo, f1)
                        if c == 7 and not first:
                            turn_acc(ph, it - 1, it)
                        if c == 11 and not last:
                            turn_xn(ph, it + 1, 1 - par, GT)
                        if c == 14 and not last:
                            route(ph, it + 1, 1 - par, 8, E1)
                        if c == 26 and not last:
                            turn_cw(ph, it + 1)
                    if last:
                        tail(ph, it, par, NC1, w1hi, w1lo, f1)
                return item

            def job_pe(ph, a, item_kind, it, par, name, i, here):
                index = [j[1:] for j in a.jobs].index((name, i))
                b = bank[6 + index % 2]
                prev = a.before(item_kind, index)
                if prev:
                    back, pname, pi = prev
                    batch = here - back + (1 if pname in NEXT else -1)
                    pe.wait_ge(job_read[pname].sem, job_read[pname].at(ph, batch, pi + 1))
                if name == "XT":
                    pe.wait_ge(xn_ready.sem, xn_ready.at(ph, it, 1))
                    for j in range(BT):
                        mm = nc.tensor.transpose(b[:, j * P:(j + 1) * P], xn[:, par, j, :], ident[:])
                    mm.then_inc(xn_turned.sem, 1)
                if name == "QK":
                    if i == 0:
                        pe.wait_ge(xt_lo.sem, xt_lo.at(ph, it, 1))
                    for w in range(2):
                        if a is A0:
                            cols = slice(1024 * w + P * i, 1024 * w + P * i + P)
                            whi, wlo = wqkv_hi[:, cols], wqkv_lo[:, cols]
                        else:
                            cols = slice(P * (2 * i + w), P * (2 * i + w) + P)
                            whi, wlo = wa1_hi[:, cols], wa1_lo[:, cols]
                        mm = three(b[:, 256 * w:256 * w + 256], whi, wlo, xthi[:, par, 0:256], xtlo[:, par, 0:256])
                    mm.then_inc(qk_done.sem, 1)
                if name == "V":
                    if a is A0:
                        half, t = divmod(i, 2)
                        tok = slice(P * t, P * t + P)
                        cols = slice(2048 + 512 * half, 2048 + 512 * half + 512)
                        mm = three(b[:], xthi[:, par, tok], xtlo[:, par, tok], wqkv_hi[:, cols], wqkv_lo[:, cols])
                    else:
                        for t in range(BT):
                            tok = slice(P * t, P * t + P)
                            cols = slice(1024, 1056)
                            o = b[:, 32 * t:32 * t + 32]
                            three(o, xthi[:, par, tok], xtlo[:, par, tok], wa1_hi[:, cols], wa1_lo[:, cols], stop=False)
                            mm = nc.tensor.matmul(o, brow1[:, 0:P], brow1[:, P + D:P + D + 32], start=False, stop=True)
                    mm.then_inc(v_done.sem, 1)
                if name == "OT":
                    if a is A0:
                        half, t = divmod(i, 2)
                        pe.wait_ge(o_ready.sem, o_ready.at(ph, it, half + 1))
                        for c in range(4):
                            mm = nc.tensor.transpose(b[:, c * P:(c + 1) * P], o_sb0[:, t, 512 * half + c * P:512 * half + (c + 1) * P], ident[:])
                    else:
                        pe.wait_ge(o_ready.sem, o_ready.at(ph, it, 2))
                        for t in range(BT):
                            mm = nc.tensor.transpose(b[:, t * P:(t + 1) * P], o_sb1[:, t, :], ident[:])
                    mm.then_inc(ot_done.sem, 1)
                if name == "Y":
                    pe.wait_ge(ot_ready.sem, ot_ready.at(ph, it + 1, 0))
                    for t in range(BT):
                        o = b[:, t * P:(t + 1) * P]
                        if a is A0:
                            for c in range(8):
                                mm = nc.tensor.matmul(o, ot0[:, t, c, :], wout[:, c, :], start=(c == 0), stop=(c == 7))
                        else:
                            nc.tensor.matmul(o, ot1[:, t, :], wo1[:], start=True, stop=False)
                            mm = nc.tensor.matmul(o, brow1[:, 0:P], brow1[:, P:P + D], start=False, stop=True)
                    mm.then_inc(y_done.sem, 1)

            def scores_of(ph, a, it, par, u):
                c, r = divmod(u, a.heads_a_chunk)
                if r == 0:
                    pe.wait_ge(qk_ready.sem, qk_ready.at(ph, it, c + 1))
                if masked_ready.past(ph, it, u - 1):
                    pe.wait_ge(masked_ready.sem, masked_ready.at(ph, it, u - 1))
                rows = slice(a.rows * r, a.rows * r + a.rows)
                q, k = QK[a.kind][rows, par, c, 0, :], QK[a.kind][rows, par, c, 1, :]
                nc.tensor.matmul(bank[u % 2][:, 0:128], q[:, 0:128], k[:, 0:128], start=True, stop=True)
                nc.tensor.matmul(bank[u % 2][:, 128:320], q[:, 128:256], k[:, 64:256],
                                 start=True, stop=True).then_inc(scores.sem, 1)

            def turn_p(ph, it, u):
                pe.wait_ge(exp_done.sem, exp_done.at(ph, it, u + 1))
                if pt_ready.past(ph, it, u - 1):
                    pe.wait_ge(pt_ready.sem, pt_ready.at(ph, it, u - 1))
                for c in range(3):
                    mm = nc.tensor.transpose(bank[2 + u % 2][:, c * P:(c + 1) * P], probs[:, u % 4, c * P:(c + 1) * P], ident[:])
                mm.then_inc(p_turned.sem, 1)

            def pv_of(ph, a, it, par, u):
                half, g = divmod(u, 8)
                pe.wait_ge(pt_ready.sem, pt_ready.at(ph, it, u + 1))
                if g == 0:
                    pe.wait_ge(v_ready.sem, v_ready.at(ph, it, 2 * half + 2 if a is A0 else 1))
                    k = half if a is A0 else half - 1
                    if o_ready.past(ph, it, k):
                        pe.wait_ge(o_ready.sem, o_ready.at(ph, it, k))
                if a is A0:
                    o = [bank[4 + t][:, 64 * g:64 * g + 64] for t in range(BT)]
                    v = [v0[:, par, t, 64 * u:64 * u + 64] for t in range(BT)]
                else:
                    o = [bank[4 + half][:, 64 * t + 8 * g:64 * t + 8 * g + 8] for t in range(BT)]
                    v = [v1[:, par, t, 8 * (u // 4):8 * (u // 4) + 8] for t in range(BT)]
                pt = PTS[a.kind]
                nc.tensor.matmul(o[0], pt[:, u % 4, 0:128], v[0], start=True, stop=True)
                nc.tensor.matmul(o[1], pt[:, u % 4, 128:256], v[0], start=True, stop=False)
                nc.tensor.matmul(o[1], pt[:, u % 4, 256:384], v[1], start=False, stop=True).then_inc(pv_done.sem, 1)

            def attention_item(ph, a):
                def item(it, par, first, last):
                    kind = 0 if first else 2 if last else 1
                    for u in range(HEADS):
                        scores_of(ph, a, it, par, u)
                        if u >= 2:
                            turn_p(ph, it, u - 2)
                        elif not first:
                            turn_p(ph, it - 1, u + HEADS - 2)
                        if u >= 3:
                            pv_of(ph, a, it, par, u - 3)
                        elif not first:
                            pv_of(ph, a, it - 1, 1 - par, u + HEADS - 3)
                        for step, name, i in a.jobs:
                            if step == u and name in NEXT and not last:
                                job_pe(ph, a, kind, it + 1, 1 - par, name, i, it)
                            if step == u and name not in NEXT and not first:
                                job_pe(ph, a, kind, it - 1, 1 - par, name, i, it)
                    if last:
                        turn_p(ph, it, HEADS - 2)
                        pv_of(ph, a, it, par, HEADS - 3)
                        turn_p(ph, it, HEADS - 1)
                        pv_of(ph, a, it, par, HEADS - 2)
                        pv_of(ph, a, it, par, HEADS - 1)
                        for _, name, i in a.jobs:
                            if name not in NEXT:
                                job_pe(ph, a, 3, it, par, name, i, it + 1)
                return item

            pe.wait_ge(router_split, 2)
            for ph, kind in enumerate(PHASES):
                enter(pe, ph)
                if kind in ("A0", "A1"):
                    a = A0 if kind == "A0" else A1
                    if a is A0:
                        pe.wait_ge(dma_wout, 16)
                    else:
                        pe.wait_ge(dma_a1, 48)
                    for _, name, i in a.jobs:
                        if name in NEXT:
                            job_pe(ph, a, -1, 0, 0, name, i, -1)
                            pe.wait_ge(w_lo, PIECES[ph][1])
                    items(pe, ph, attention_item(ph, a))
                if kind in ("F0", "F1"):
                    turn_xn(ph, 0, 0, GT)
                    if kind == "F0":
                        route(ph, 0, 0, 0, E0)
                        items(pe, ph, f0_item(ph))
                    else:
                        route(ph, 0, 0, 8, E1)
                        pe.wait_ge(dma_sel, 48)
                        turn_cw(ph, 0)
                        items(pe, ph, f1_item(ph))
                leave(pe)


def kernel(**inputs):
    import numpy as np
    import concourse.bacc as bacc
    from concourse.bass_utils import run_bass_kernel_spmd as run

    def f32(name):
        return np.ascontiguousarray(inputs[name])

    def chunks(fc, proj):
        n = fc.shape[0] // P
        up = fc.reshape(n, P, D).transpose(2, 0, 1)
        down = proj.reshape(D, n, P).transpose(2, 1, 0)
        return np.ascontiguousarray(np.concatenate([up, down], axis=2).reshape(P, n * 256))

    fc, proj = f32("L0_ffn_w_fc"), f32("L0_ffn_w_proj")
    w0 = np.concatenate([
        chunks(f32("L0_ffn_shared_fc"), f32("L0_ffn_shared_proj")),
        *[chunks(fc[e], proj[e]) for e in range(E0)]], axis=1)
    up1, down1 = f32("L1_ffn_W_up"), f32("L1_ffn_W_down")
    pad = np.zeros((D, FF1), up1.dtype)
    fc1 = np.concatenate([f32("L1_ffn_Ws_up"), pad, up1.transpose(1, 0, 2).reshape(D, E1 * FF1)], axis=1).T
    proj1 = np.concatenate([f32("L1_ffn_Ws_down"), pad.T, down1.reshape(E1 * FF1, D)], axis=0).T
    w1 = chunks(np.ascontiguousarray(fc1), np.ascontiguousarray(proj1))

    wq, bq = f32("L1_attn_Wq").reshape(D, KV1, 4, DH1), f32("L1_attn_bq").reshape(KV1, 4, DH1)
    wk, bk = f32("L1_attn_Wk").reshape(D, KV1, DH1), f32("L1_attn_bk").reshape(KV1, DH1)
    wa = np.zeros((D, KV1, 2, 4, 32), np.float32)
    ba = np.zeros((KV1, 2, 4, 32), np.float32)
    wa[:, :, 0, :, 0:DH1], ba[:, 0, :, 0:DH1] = wq, bq
    wa[:, :, 1, :, 0:DH1], ba[:, 1, :, 0:DH1] = wk[:, :, None, :], bk[:, None, :]
    wa1 = np.concatenate([wa.reshape(D, 1024), f32("L1_attn_Wv")], axis=1)
    bqk1 = np.ascontiguousarray(ba.reshape(8, P).T)
    brow1 = np.concatenate([np.ones(P, np.float32), f32("L1_attn_bo"), f32("L1_attn_bv")])[None, :]

    const = np.zeros((P, 712), np.float32)
    const[:, 256:384] = np.eye(P)
    q = np.arange(P)[:, None]
    k0 = np.arange(128)[None, :]
    const[:, 384:512] = np.where((k0 <= q) & (k0 > q - WINDOW), 0, MASKED)
    k1 = np.arange(64, 256)[None, :]
    const[:, 512:704] = np.where((k1 <= q + P) & (k1 > q + P - WINDOW), 0, MASKED)
    const[:, 704:712] = np.arange(8)[None, :]
    sel = np.zeros((P, 17, P), np.float32)
    for j in range(16):
        for part in range(3):
            sel[part * 32 + 2 * j, j, 0:64] = 1
            sel[part * 32 + 2 * j + 1, j, 64:128] = 1
    sel[:, 16, :] = np.eye(P)
    import ml_dtypes
    sel = sel.reshape(P, 17 * P).astype(ml_dtypes.bfloat16)

    arrays = {
        "x": f32("L0_attn_x"), "w0": w0, "router": np.ascontiguousarray(f32("L0_ffn_router_w").T),
        "wqkv": f32("L0_attn_Wqkv"), "wout": f32("L0_attn_Wout"), "w1": w1,
        "cent": np.ascontiguousarray(f32("L1_ffn_centroids").T), "bias1": f32("L1_ffn_expert_biases"),
        "const": const, "sel": sel,
        "wa1": wa1, "bqk1": bqk1, "wo1": f32("L1_attn_Wo"), "brow1": brow1,
    }
    nc = bacc.Bacc("TRN2", target_bir_lowering=False, num_devices=1, dynamic_dma_scratch_size=1024)
    aps = [nc.dram_tensor("in_" + n, a.shape, mybir.dt.from_np(a.dtype), kind="ExternalInput").ap()
           for n, a in arrays.items()]
    out = nc.dram_tensor("out_0", arrays["x"].shape, F32, kind="ExternalOutput").ap()
    build(nc, *aps, out)
    res = run(nc, [{"in_" + n: a for n, a in arrays.items()}], core_ids=[0])
    return res.results[0]["out_0"]
```

```python
from contextlib import ExitStack

import concourse.bass as bass
from concourse import mybir

ALU = mybir.AluOpType
ACT = mybir.ActivationFunctionType
F32 = mybir.dt.float32
F32R = mybir.dt.float32r
BF16 = mybir.dt.bfloat16
U32 = mybir.dt.uint32
AX_X = mybir.AxisListType.X

P = 128
D = 128
TILES = 32
GT = 4
GROUPS = TILES // GT
BT = 2
BATCHES = TILES // BT
N = GT * P

E0, FF0 = 8, 512
E1, FF1, TOPK1 = 64, 64, 8
NC0 = (E0 + 1) * FF0 // P
SH0 = FF0 // P
NC1 = 1 + E1 * FF1 // P
H0, DH0 = 16, 64
H1, KV1, DH1 = 16, 4, 8
WINDOW = 64
UPB = 3
LAG = 5
RING = 6
HR = 6
RR = 3
EPS = 1e-5
MASKED = -1e30
PIECE = 768

PHASES = ("F0", "A0", "F0", "F1", "A1", "F1")
ITEMS = {"F0": GROUPS, "F1": GROUPS, "A0": BATCHES, "A1": BATCHES}


class Signal:

    def __init__(self, sem, **per):
        self.sem, self.per = sem, per

    def at(self, ph, it, k):
        base = sum(self.per.get(q, 0) * ITEMS[q] for q in PHASES[:ph])
        return it * self.per.get(PHASES[ph], 0) + (base + k)

    def past(self, ph, it, k):
        return not isinstance(it, int) or it * self.per[PHASES[ph]] + k > 0


POOL_LO = (5, 8, 11, 14, 16, 18, 20, 22, 24, 28)


class Attention:

    def __init__(self, kind, heads_a_chunk, dh, jobs):
        self.kind, self.heads_a_chunk, self.dh = kind, heads_a_chunk, dh
        self.rows = P // heads_a_chunk
        self.chunks = HEADS // heads_a_chunk
        self.group = 2 * heads_a_chunk
        self.scale = dh ** -0.5
        self.jobs = jobs
        assert len(jobs) % 2 == 0

    def before(self, item, index):
        back = 0
        while item >= -1:
            index -= 2
            if index < 0:
                index += len(self.jobs)
                back += 1
                item = {3: 2, 2: 1, 1: 1, 0: -1, -1: -2}[item]
                if item == -2:
                    return None
            _, name, number = self.jobs[index]
            if (item not in (-1, 0) or name in NEXT) and (item < 2 or name not in NEXT):
                return back, name, number


HEADS = 16
NEXT = ("XT", "QK", "V")
A0 = Attention("A0", 2, DH0, [
    (3, "XT", 0), (5, "QK", 0), (6, "Y", 0), (7, "QK", 1), (8, "QK", 2), (9, "QK", 3), (10, "V", 0),
    (11, "QK", 4), (11, "V", 1), (12, "QK", 5), (13, "QK", 6), (13, "V", 2), (14, "QK", 7), (15, "V", 3)])
A1 = Attention("A1", 4, DH1, [
    (3, "XT", 0), (5, "QK", 0), (6, "Y", 0), (8, "QK", 1), (10, "QK", 2), (11, "QK", 3), (13, "V", 0), (14, "V", 1)])
TURN_LAG = 3
PV_LAG = 4
O_LAG = 5


def late(u, lag, it, par, first):
    h = u - lag
    if 0 <= h < HEADS:
        return it, par, h
    if h < 0 and not first:
        return it - 1, 1 - par, h + HEADS
    return None


def steps(last):
    return range(HEADS + (O_LAG if last else 0))


def build(nc, x_in, w0_in, router_in, wqkv_in, wout_in, w1_in, cent_in, bias1_in, const_in, sel_in,
          wa1_in, bqk1_in, wo1_in, brow1_in, out):
    with ExitStack() as ctx:
        def sem(name):
            return ctx.enter_context(nc.semaphore(name))

        at = {"byte": 0}

        def place(name, shape, dt, region=None):
            size = 4 if dt in (F32, F32R, U32) else 2
            for n in shape[1:]:
                size *= n
            size = (size + 31) // 32 * 32
            where = region if region is not None else at
            t = nc.alloc_sbuf_tensor_at(name, shape, dt, offset=where["byte"])
            where["byte"] += size
            assert where["byte"] <= where.get("end", 224 * 1024), name
            return t

        A_START, A_SIZE = 1280, NC0 * 256 * 4 * 2
        B_START, B_SIZE = A_START + A_SIZE, NC1 * 256 * 4 * 2 + 4096
        at["byte"] = B_START + B_SIZE

        def region_a():
            return {"byte": A_START, "end": A_START + A_SIZE}

        def region_b():
            return {"byte": B_START, "end": B_START + B_SIZE}

        r = region_a()
        w0hi = place("w0hi", [P, NC0, 256], F32R, r)
        w0lo = place("w0lo", [P, NC0, 256], F32R, r)
        r = region_b()
        w1hi = place("w1hi", [P, NC1, 256], F32R, r)
        w1lo = place("w1lo", [P, NC1, 256], F32R, r)

        x = place("x", [P, TILES, D], F32)
        stage = place("stage", [P, 2, PIECE], F32)
        xn = place("xn", [P, 2, GT, D], F32)
        xthi = place("xthi", [P, 2, N], F32R)
        xtlo = place("xtlo", [P, 2, N], F32R)
        acc_sb = place("acc_sb", [P, N], F32)
        ident = place("ident", [P, P], F32)
        mask = place("mask", [P, 320], F32)
        iota8 = place("iota8", [P, E0], F32)
        router = place("router", [P, 8 + 64], F32)
        rthi = place("rthi", [P, 8 + 64], F32R)
        rtlo = place("rtlo", [P, 8 + 64], F32R)
        stats = place("stats", [P, GT, 6], F32)
        mv = place("mv", [P, GT, 2], F32)
        var = place("var", [P, GT], F32)
        rstd = place("rstd", [P, GT], F32)
        phalf = place("phalf", [P, 8], F32)
        nhalf = place("nhalf", [P, GT], F32)

        def ffn_scratch(tag, r):
            return {
                "r": place("r" + tag, [P, RR, N], F32, r),
                "h": place("h" + tag, [P, HR, N], F32, r),
                "hhi": place("hhi" + tag, [P, RING, N], F32R, r),
                "hlo": place("hlo" + tag, [P, RING, N], F32R, r),
            }

        rb = region_b()
        f0 = ffn_scratch("0", rb)
        xe = place("xe", [P, 2, GT, D], F32, rb)
        xehi = place("xehi", [P, 2, N], F32R, rb)
        xelo = place("xelo", [P, 2, N], F32R, rb)
        g_e = place("g_e", [P, GT, E0], F32, rb)
        g_x = place("g_x", [P, GT, E0], F32, rb)
        g_p = place("g_p", [P, GT, E0], F32, rb)
        g_mx = place("g_mx", [P, GT, 8], F32, rb)
        g_ix = place("g_ix", [P, GT, 8], U32, rb)
        g_if = place("g_if", [P, GT, 2], F32, rb)
        g_s = place("g_s", [P, 8, GT], F32, rb)
        g_w = place("g_w", [P, GT, 2], F32, rb)
        g_sq = place("g_sq", [P, GT, 2], F32, rb)
        g_m = place("g_m", [P, 4, GT, E0], F32, rb)
        gate = place("gate", [P, 2, GT, E0], F32, rb)

        ra = region_a()
        sel = place("sel", [96, 16, P], BF16, ra)
        ident_b = place("ident_b", [P, P], BF16, ra)
        e_bias = place("e_bias", [P, E1], F32, ra)
        after_consts = dict(ra)
        f1 = ffn_scratch("1", ra)
        cwt = place("cwt", [96, 2, 2, N], BF16, ra)
        e_b = place("e_b", [P, GT, E1], F32, ra)
        e_sig = place("e_sig", [P, GT, E1], F32, ra)
        e_mx = place("e_mx", [P, GT, 8], F32, ra)
        e_rep = place("e_rep", [P, GT, E1], F32, ra)
        e_m = place("e_m", [P, GT, E1], F32, ra)
        e_w = place("e_w", [P, GT, E1], F32, ra)
        e_s = place("e_s", [P, 4, GT], F32, ra)
        e_cw = place("e_cw", [P, GT, E1], F32, ra)
        e_r1 = place("e_r1", [P, GT, E1], F32, ra)
        e_r2 = place("e_r2", [P, GT, E1], F32, ra)
        parts = place("parts", [P, GT, 2, 3, 32], BF16, ra)

        rb = region_b()
        wqkv_hi = place("wqkv_hi", [P, 3 * HEADS * DH0], F32R, rb)
        wqkv_lo = place("wqkv_lo", [P, 3 * HEADS * DH0], F32R, rb)
        wout = place("wout", [P, 8, D], F32, rb)
        ra = dict(after_consts)
        wa1_hi = place("wa1_hi", [P, 1024 + P], F32R, ra)
        wa1_lo = place("wa1_lo", [P, 1024 + P], F32R, ra)
        wo1 = place("wo1", [P, KV1, D], F32, ra)
        brow1 = place("brow1", [1, P + D + P], F32, ra)
        bqk1 = place("bqk1", [P, 16], F32, ra)
        lo_row = place("lo_row", [P, 4], F32, ra)
        qk_t = place("qk_t", [P, 2, 2, 256], F32, ra)
        qk_h = place("qk_h", [P, 2, 2, 256], F32R, ra)
        qk1 = place("qk1", [P, 2, 4, 2, 256], F32R, ra)
        v1 = place("v1", [P, 2, BT, P], F32, ra)
        ot1 = place("ot1", [P, 2, 4, 256], F32, ra)
        MASKEDS = {"A0": place("masked0", [P, 2, 320], F32, rb), "A1": place("masked1", [P, 2, 320], F32, ra)}
        PTS = {"A0": place("pt0", [P, 4, 384], F32, rb), "A1": place("pt1", [P, 4, 384], F32, ra)}
        probs = place("probs", [P, 4, 384], F32)
        negmax = place("negmax", [P, 4, BT], F32)
        sums = place("sums", [P, 4, BT], F32)
        rsums = place("rsums", [P, 4, BT], F32)
        v0 = place("v0", [P, 2, BT, HEADS * DH0], F32, rb)
        ot0 = place("ot0", [P, 2, 8, 256], F32, rb)
        qk0 = place("qk0", [P, 2, 8, 2, 256], F32)
        QK = {"A0": qk0, "A1": qk1}
        OT = {"A0": ot0, "A1": ot1}

        bank = [ctx.enter_context(nc.psum_tensor(f"bank{i}", [P, 512], F32)) for i in range(8)]
        MISC = 6

        def acc_bank(par):
            return bank[3 + 4 * par]

        dma_const = sem("dma_const")
        dma_sel = sem("dma_sel")
        dma_wout = sem("dma_wout")
        dma_a1 = sem("dma_a1")
        dma_x0 = sem("dma_x0")
        dma_x = sem("dma_x")
        dma_stage = [sem("dma_stage0"), sem("dma_stage1")]
        dma_out = sem("dma_out")
        consts_made = sem("consts_made")
        router_split = sem("router_split")
        w_hi = sem("w_hi")
        w_lo = sem("w_lo")
        phase_done = sem("phase_done")

        carried = sem("carried")

        def carry(eng):
            eng.sem_inc(carried, 1)

        var_ready = Signal(sem("var_ready"), F0=1, F1=1, A0=1, A1=1)
        stat_step = Signal(sem("stat_step"), F0=2, F1=2, A0=2, A1=2)
        rstd_ready = Signal(sem("rstd_ready"), F0=1, F1=1, A0=1, A1=1)
        xn_ready = Signal(sem("xn_ready"), F0=1, F1=1, A0=1, A1=1)
        xn_turned = Signal(sem("xn_turned"), F0=1, F1=1, A0=1, A1=1)
        xt_hi = Signal(sem("xt_hi"), F0=1, F1=1, A0=1, A1=1)
        xt_lo = Signal(sem("xt_lo"), F0=1, F1=1, A0=1, A1=1)
        logits = Signal(sem("logits"), F0=1, F1=1)
        logits_read = Signal(sem("logits_read"), F0=1, F1=1)
        gate_dve = Signal(sem("gate_dve"), F0=22, F1=20)
        gate_exp = Signal(sem("gate_exp"), F0=1)
        gate_sqrt = Signal(sem("gate_sqrt"), F0=1)
        gate_sig = Signal(sem("gate_sig"), F1=1)
        cw_turned = Signal(sem("cw_turned"), F1=1)
        cwt_ready = Signal(sem("cwt_ready"), F1=1)
        up_done = Signal(sem("up_done"), F0=NC0, F1=NC1)
        act_done = Signal(sem("act_done"), F0=NC0, F1=NC1)
        h_ready = Signal(sem("h_ready"), F0=NC0, F1=NC1)
        hi_ready = Signal(sem("hi_ready"), F0=NC0, F1=NC1)
        lo_ready = Signal(sem("lo_ready"), F0=NC0, F1=NC1 - len(POOL_LO))
        lo_pool = Signal(sem("lo_pool"), F1=len(POOL_LO))

        def wait_lo(eng, ph, it, c):
            nch = NC0 if PHASES[ph] == "F0" else NC1
            if c < 0:
                it, c = it - 1, c + nch
            if isinstance(it, int) and it < 0:
                return
            if PHASES[ph] == "F1" and c in POOL_LO:
                eng.wait_ge(lo_pool.sem, lo_pool.at(ph, it, POOL_LO.index(c) + 1))
            else:
                others = sum(q < c for q in POOL_LO) if PHASES[ph] == "F1" else 0
                eng.wait_ge(lo_ready.sem, lo_ready.at(ph, it, c + 1 - others))
        down_done = Signal(sem("down_done"), F0=NC0, F1=NC1)
        xe_ready = Signal(sem("xe_ready"), F0=E0)
        xe_turned = Signal(sem("xe_turned"), F0=E0)
        xe_hi = Signal(sem("xe_hi"), F0=E0)
        xe_lo = Signal(sem("xe_lo"), F0=E0)
        cb_done = Signal(sem("cb_done"), F1=NC1 - 1)
        scores = Signal(sem("scores"), A0=HEADS, A1=HEADS)
        masked_ready = Signal(sem("masked_ready"), A0=HEADS, A1=HEADS)
        exp_done = Signal(sem("exp_done"), A0=HEADS, A1=HEADS)
        p_turned = Signal(sem("p_turned"), A0=HEADS, A1=HEADS)
        pt_ready = Signal(sem("pt_ready"), A0=HEADS, A1=HEADS)
        pv_done = Signal(sem("pv_done"), A0=HEADS, A1=HEADS)
        rsum_ready = Signal(sem("rsum_ready"), A0=HEADS, A1=HEADS)
        p_ready = Signal(sem("p_ready"), A0=HEADS, A1=HEADS)
        qk_done = Signal(sem("qk_done"), A0=8, A1=4)
        qk_ready = Signal(sem("qk_ready"), A0=8, A1=4)
        qk_parts = Signal(sem("qk_parts"), A1=4)
        v_done = Signal(sem("v_done"), A0=4, A1=2)
        v_ready = Signal(sem("v_ready"), A0=4, A1=2)
        ot_ready = Signal(sem("ot_ready"), A0=4, A1=2)

        def job_read(a, name):
            return {"XT": xt_lo, "QK": qk_ready if a is A0 else qk_parts, "V": v_ready, "Y": x_added}[name]

        acc_copied = Signal(sem("acc_copied"), F0=1, F1=1)
        y_turned = Signal(sem("y_turned"), F0=1, F1=1)
        y_done = Signal(sem("y_done"), A0=1, A1=1)
        x_added = Signal(sem("x_added"), F0=1, F1=1, A0=1, A1=1)

        pieces = []

        def add_pieces(dram, hi, lo, cols):
            first = len(pieces)
            for c in range(0, cols, PIECE):
                n = min(PIECE, cols - c)
                pieces.append((dram[:, c:c + n], hi[:, c:c + n], lo[:, c:c + n], n))
            return first, len(pieces)

        def flat(t):
            return t[:].rearrange("p c k -> p (c k)")

        P0 = add_pieces(w0_in, flat(w0hi), flat(w0lo), NC0 * 256)
        PA0 = add_pieces(wqkv_in, wqkv_hi[:], wqkv_lo[:], 3 * HEADS * DH0)
        P1 = add_pieces(w1_in, flat(w1hi), flat(w1lo), NC1 * 256)
        PA1 = add_pieces(wa1_in, wa1_hi[:], wa1_lo[:], 1024 + P)
        PIECES = {PHASES.index(kind): p for kind, p in (("F0", P0), ("A0", PA0), ("F1", P1), ("A1", PA1))
                  if kind in PHASES}
        CPP = PIECE // 256

        block = ctx.enter_context(nc.Block())

        def items(eng, ph, item):
            n = ITEMS[PHASES[ph]]
            item(0, 0, True, False)
            with eng.Fori(0, n // 2 - 1) as k:
                item(2 * k + 1, 1, False, False)
                item(2 * k + 2, 0, False, False)
            item(n - 1, 1, False, True)

        def enter(eng, ph):
            if ph:
                eng.wait_ge(phase_done, 4 * ph)

        def leave(eng):
            eng.drain().then_inc(phase_done, 1)

        @block.sync
        def _(sp):
            xv = x_in.rearrange("b (u p) d -> p (b u) d", p=P)
            ov = out.rearrange("b (u p) d -> p (b u) d", p=P)
            sp.dma_start(x[:, 0:GT, :], xv[:, 0:GT, :]).then_inc(dma_x0, 16)
            sp.dma_start(ident[:], const_in[:, 256:384]).then_inc(dma_const, 16)
            sp.dma_start(router[:, 0:8], router_in).then_inc(dma_const, 16)
            sp.dma_start(router[:, 8:72], cent_in).then_inc(dma_const, 16)
            sp.dma_start(mask[:], const_in[:, 384:704]).then_inc(dma_const, 16)
            sp.dma_start(iota8[:], const_in[:, 704:712]).then_inc(dma_const, 16)
            for i, (dram, _, _, n) in enumerate(pieces):
                if i == PA0[0]:
                    sp.wait_ge(phase_done, 4 * PHASES.index("A0"))
                    sp.dma_start(wout[:], wout_in.rearrange("(c p) d -> p c d", p=P)).then_inc(dma_wout, 16)
                if i == P1[0]:
                    sp.wait_ge(phase_done, 4 * PHASES.index("F1"))
                    sp.dma_start(sel[:], sel_in[0:96, 0:2048].rearrange("p (c k) -> p c k", c=16)).then_inc(dma_sel, 16)
                    sp.dma_start(ident_b[:], sel_in[:, 2048:2176]).then_inc(dma_sel, 16)
                    sp.dma_start(e_bias[:], bias1_in.rearrange("(a e) -> a e", a=1).broadcast_to([P, E1])).then_inc(dma_sel, 16)
                if i == PA1[0]:
                    sp.wait_ge(phase_done, 4 * PHASES.index("A1"))
                    sp.dma_start(wo1[:], wo1_in.rearrange("(c p) d -> p c d", p=P)).then_inc(dma_a1, 16)
                    sp.dma_start(bqk1[:], bqk1_in[:, 0:16]).then_inc(dma_a1, 16)
                    sp.dma_start(lo_row[:], bqk1_in[:, 16:20]).then_inc(dma_a1, 16)
                    sp.dma_start(brow1[:], brow1_in).then_inc(dma_a1, 16)
                if i >= 2:
                    sp.wait_ge(w_lo, i - 1)
                sp.dma_start(stage[:, i % 2, 0:n], dram).then_inc(dma_stage[i % 2], 16)
                if i == 1:
                    for g in range(1, GROUPS):
                        sp.dma_start(x[:, GT * g:GT * g + GT, :], xv[:, GT * g:GT * g + GT, :]).then_inc(dma_x, 16)
            for q in range(4):
                sp.wait_ge(x_added.sem, x_added.at(len(PHASES) - 1, 2 * q + 1, 1))
                sp.dma_start(ov[:, 8 * q:8 * q + 8, :], x[:, 8 * q:8 * q + 8, :]).then_inc(dma_out, 16)
            sp.wait_ge(dma_out, 64)

        @block.gpsimd
        def _(pool):
            nc.gpsimd.memset(phalf[:], 0.5).then_inc(consts_made, 1)
            nc.gpsimd.memset(nhalf[:], -0.5).then_inc(consts_made, 1)
            nc.gpsimd.memset(probs[:], 0.0).then_inc(consts_made, 1)
            pool.wait_ge(consts_made, 3)

            def piece_hi(i):
                _, hi, _, n = pieces[i]
                pool.wait_ge(dma_stage[i % 2], 16 * (i // 2 + 1))
                nc.gpsimd.tensor_scalar(hi, stage[:, i % 2, 0:n], 1.0, 1.0, ALU.mult, ALU.mult).then_inc(w_hi, 1)

            def rstd_of(ph, it, tiles):
                pool.wait_ge(var_ready.sem, var_ready.at(ph, it, 1))
                nc.gpsimd.tensor_tensor(rstd[:, 0:tiles], var[:, 0:tiles], nhalf[:, 0:tiles],
                                        ALU.pow).then_inc(rstd_ready.sem, 1)

            def sqrt_of(ph, it):
                pool.wait_ge(gate_dve.sem, gate_dve.at(ph, it, 14))
                nc.gpsimd.tensor_tensor(g_sq[:].rearrange("p t k -> p (t k)"), g_w[:].rearrange("p t k -> p (t k)"),
                                        phalf[:, 0:8], ALU.pow).then_inc(gate_sqrt.sem, 1)

            def gated_x(ph, it, par, e):
                if e == 0:
                    pool.wait_ge(gate_dve.sem, gate_dve.at(ph, it, gate_dve.per["F0"]))
                if xe_turned.past(ph, it, e - 1):
                    pool.wait_ge(xe_turned.sem, xe_turned.at(ph, it, e - 1))
                carry(pool)
                for j in range(GT):
                    ins = nc.gpsimd.tensor_scalar(xe[:, e % 2, j, :], xn[:, par, j, :],
                                                  gate[:, par, j, e:e + 1], 1.0, ALU.mult, ALU.mult)
                ins.then_inc(xe_ready.sem, 1)

            def f0_item(ph):
                def item(it, par, first, last):
                    for c in range(NC0):
                        if first and ph in PIECES and c % CPP == 0 and P0[0] + 2 + c // CPP < P0[1]:
                            piece_hi(P0[0] + 2 + c // CPP)
                        if c == 0 and first:
                            gated_x(ph, it, par, 0)
                        if c == NC0 - 2 and not last:
                            gated_x(ph, it + 1, 1 - par, 0)
                        if c % 4 == 1 and c // 4 + 1 < E0:
                            gated_x(ph, it, par, c // 4 + 1)
                        if c == 7 and not last:
                            rstd_of(ph, it + 1, GT)
                        if c == 28 and not last:
                            sqrt_of(ph, it + 1)
                        s = (par * NC0 + c)
                        pool.wait_ge(h_ready.sem, h_ready.at(ph, it, c + 1))
                        if down_done.past(ph, it, c + 1 - RING):
                            pool.wait_ge(down_done.sem, down_done.at(ph, it, c + 1 - RING))
                        carry(pool)
                        nc.gpsimd.tensor_scalar(f0["hhi"][:, s % RING, :], f0["h"][:, s % HR, :], 1.0, 1.0,
                                                ALU.mult, ALU.mult).then_inc(hi_ready.sem, 1)
                return item

            def f1_item(ph):
                def item(it, par, first, last):
                    if first and ph in PIECES:
                        for i in range(P1[0] + 2, P1[1]):
                            piece_hi(i)
                    for c in range(NC1):
                        if c == 7 and not last:
                            rstd_of(ph, it + 1, GT)
                        if c in POOL_LO:
                            lo_of_pool(ph, it, par, c)
                return item

            def lo_of_pool(ph, it, par, c):
                s = par * NC1 + c
                pool.wait_ge(hi_ready.sem, hi_ready.at(ph, it, c + 1))
                nc.gpsimd.tensor_tensor(f1["hlo"][:, s % RING, :], f1["h"][:, s % HR, :],
                                        f1["hhi"][:, s % RING, :].bitcast(F32), ALU.subtract).then_inc(lo_pool.sem, 1)

            def attention_item(ph):
                def item(it, par, first, last):
                    for u in range(HEADS):
                        if u == 2 and not last:
                            rstd_of(ph, it + 1, BT)
                        norm_of(ph, it, u)
                return item

            def norm_of(ph, it, u):
                pool.wait_ge(rsum_ready.sem, rsum_ready.at(ph, it, u + 1))
                carry(pool)
                for t, keys in enumerate((slice(0, 128), slice(192, 384))):
                    p = probs[:, u % 4, keys]
                    ins = nc.gpsimd.tensor_scalar(p, p, rsums[:, u % 4, t:t + 1], 1.0, ALU.mult, ALU.mult)
                ins.then_inc(p_ready.sem, 1)

            for ph, kind in enumerate(PHASES):
                enter(pool, ph)
                if ph in PIECES:
                    piece_hi(PIECES[ph][0])
                    piece_hi(PIECES[ph][0] + 1)
                if kind in ("F0", "F1"):
                    rstd_of(ph, 0, GT)
                    if kind == "F0":
                        sqrt_of(ph, 0)
                    items(pool, ph, f0_item(ph) if kind == "F0" else f1_item(ph))
                else:
                    rstd_of(ph, 0, BT)
                    for i in range(PIECES[ph][0] + 2, PIECES[ph][1]):
                        piece_hi(i)
                    items(pool, ph, attention_item(ph))
                leave(pool)

        @block.scalar
        def _(act):
            def xt_hi_of(ph, it, par, tiles):
                n = tiles * P
                act.wait_ge(xn_turned.sem, xn_turned.at(ph, it, 1))
                nc.scalar.activation(xthi[:, par, 0:n], bank[MISC][:, 0:n], ACT.Copy).then_inc(xt_hi.sem, 1)

            def acc_out(ph, it, par):
                act.wait_ge(down_done.sem, down_done.at(ph, it + 1, 0))
                if y_turned.past(ph, it, 0):
                    act.wait_ge(y_turned.sem, y_turned.at(ph, it, 0))
                nc.scalar.activation(acc_sb[:], acc_bank(par)[:], ACT.Copy).then_inc(acc_copied.sem, 1)

            def gate_exp_of(ph, it):
                act.wait_ge(gate_dve.sem, gate_dve.at(ph, it, 2))
                nc.scalar.activation(g_x[:], g_e[:], ACT.Exp).then_inc(gate_exp.sem, 1)

            def gate_sig_of(ph, it):
                act.wait_ge(logits_read.sem, logits_read.at(ph, it, 1))
                nc.scalar.activation(e_sig[:], bank[MISC][:, 0:GT * E1].rearrange("p (t e) -> p t e", t=GT),
                                     ACT.Sigmoid).then_inc(gate_sig.sem, 1)

            def cwt_of(ph, it, par):
                act.wait_ge(cw_turned.sem, cw_turned.at(ph, it, 1))
                nc.scalar.activation(cwt[:, par, :, :].rearrange("p h n -> p (h n)"),
                                     bank[MISC][0:96, :].bitcast(BF16), ACT.Copy).then_inc(cwt_ready.sem, 1)

            def xe_hi_of(ph, it, e):
                act.wait_ge(xe_turned.sem, xe_turned.at(ph, it, e + 1))
                used = SH0 + SH0 * (e - 1)
                if e >= 2:
                    act.wait_ge(up_done.sem, up_done.at(ph, it, used))
                elif up_done.past(ph, it, 0):
                    act.wait_ge(up_done.sem, up_done.at(ph, it, 0) - (1 - e) * SH0)
                nc.scalar.activation(xehi[:, e % 2, :], bank[4 + e % 2][:], ACT.Copy).then_inc(xe_hi.sem, 1)

            def act_of(ph, it, par, c, func, f, nch):
                s = par * nch + c
                act.wait_ge(up_done.sem, up_done.at(ph, it, c + 1))
                if h_ready.past(ph, it, c + 1 - RR):
                    act.wait_ge(h_ready.sem, h_ready.at(ph, it, c + 1 - RR))
                nc.scalar.activation(f["r"][:, s % RR, :], bank[s % UPB][:], func).then_inc(act_done.sem, 1)

            def square_of(ph, it, par, c):
                s = par * NC0 + c
                act.wait_ge(act_done.sem, act_done.at(ph, it, c + 1))
                wait_lo(act, ph, it, c - HR)
                nc.scalar.activation(f0["h"][:, s % HR, :], f0["r"][:, s % RR, :], ACT.Square).then_inc(h_ready.sem, 1)

            def f0_item(ph):
                def item(it, par, first, last):
                    for c in range(NC0):
                        act_of(ph, it, par, c, ACT.Relu, f0, NC0)
                        if c >= 1:
                            square_of(ph, it, par, c - 1)
                        if c % 4 == 1 and c // 4 < E0 and not (first and c == 1):
                            xe_hi_of(ph, it, c // 4)
                        if first and c == 2:
                            xe_hi_of(ph, it, 0)
                        if c == 6 and not first:
                            acc_out(ph, it - 1, 1 - par)
                        if c == 13 and not last:
                            xt_hi_of(ph, it + 1, 1 - par, GT)
                        if c == 20 and not last:
                            gate_exp_of(ph, it + 1)
                    square_of(ph, it, par, NC0 - 1)
                    if last:
                        acc_out(ph, it, par)
                return item

            def hi_of(ph, it, par, c):
                s = par * NC1 + c
                act.wait_ge(h_ready.sem, h_ready.at(ph, it, c + 1))
                if down_done.past(ph, it, c + 1 - RING):
                    act.wait_ge(down_done.sem, down_done.at(ph, it, c + 1 - RING))
                nc.scalar.activation(f1["hhi"][:, s % RING, :], f1["h"][:, s % HR, :], ACT.Copy).then_inc(hi_ready.sem, 1)

            def f1_item(ph):
                def item(it, par, first, last):
                    for c in range(NC1):
                        act_of(ph, it, par, c, ACT.Silu, f1, NC1)
                        if c >= 1:
                            hi_of(ph, it, par, c - 1)
                        if c == 6 and not first:
                            acc_out(ph, it - 1, 1 - par)
                        if c == 13 and not last:
                            xt_hi_of(ph, it + 1, 1 - par, GT)
                        if c == 17 and not last:
                            gate_sig_of(ph, it + 1)
                        if c == 28 and not last:
                            cwt_of(ph, it + 1, 1 - par)
                    hi_of(ph, it, par, NC1 - 1)
                    if last:
                        acc_out(ph, it, par)
                return item

            def exp_of(ph, it, par, u):
                act.wait_ge(masked_ready.sem, masked_ready.at(ph, it, u + 1))
                if p_turned.past(ph, it, u - 3):
                    act.wait_ge(p_turned.sem, p_turned.at(ph, it, u - 3))
                for t in range(BT):
                    masked = MASKEDS[PHASES[ph]]
                    src = masked[:, u % 2, 0:128] if t == 0 else masked[:, u % 2, 128:320]
                    dst = probs[:, u % 4, 0:128] if t == 0 else probs[:, u % 4, 192:384]
                    ins = nc.scalar.activation(dst, src, ACT.Exp, bias=negmax[:, u % 4, t:t + 1], scale=-1.0,
                                               accum_out=sums[:, u % 4, t:t + 1])
                ins.then_inc(exp_done.sem, 1)

            def job_act(ph, a, it, par, name, i):
                b = bank[6 + [j[1:] for j in a.jobs].index((name, i)) % 2]
                if name == "XT":
                    act.wait_ge(xn_turned.sem, xn_turned.at(ph, it, 1))
                    if v_done.past(ph, it - 1, 0):
                        act.wait_ge(v_done.sem, v_done.at(ph, it - 1, 0))
                        act.wait_ge(qk_done.sem, qk_done.at(ph, it - 1, 0))
                    nc.scalar.activation(xthi[:, par, 0:256], b[:, 0:256], ACT.Copy).then_inc(xt_hi.sem, 1)
                if name == "QK":
                    act.wait_ge(qk_done.sem, qk_done.at(ph, it, i + 1))
                    if a is A0 and scores.past(ph, it - 1, 0):
                        act.wait_ge(scores.sem, scores.at(ph, it - 1, 0))
                    if a is A0:
                        nc.scalar.activation(qk0[:, par, i, :, :].rearrange("p w n -> p (w n)"), b[:],
                                             ACT.Copy).then_inc(qk_ready.sem, 1)
                    else:
                        if qk_ready.past(ph, it, i - 1):
                            act.wait_ge(qk_ready.sem, qk_ready.at(ph, it, i - 1))
                        for w in range(2):
                            src, col = b[:, 256 * w:256 * w + 256], 2 * i + w
                            nc.scalar.activation(qk_h[:, i % 2, w, :], src, ACT.Identity, bias=bqk1[:, col:col + 1])
                            ins = nc.scalar.activation(qk_t[:, i % 2, w, :], src, ACT.Identity,
                                                       bias=bqk1[:, 8 + col:9 + col], scale=lo_row[:, w:w + 1])
                        ins.then_inc(qk_parts.sem, 1)
                if name == "V":
                    act.wait_ge(v_done.sem, v_done.at(ph, it, i + 1))
                    if pv_done.past(ph, it - 1, 0):
                        act.wait_ge(pv_done.sem, pv_done.at(ph, it - 1, 0))
                    if a is A0:
                        half, t = divmod(i, 2)
                        nc.scalar.activation(v0[:, par, t, 512 * half:512 * half + 512], b[:], ACT.Copy).then_inc(v_ready.sem, 1)
                    else:
                        nc.scalar.activation(v1[:, par, i, :], b[:, 0:P], ACT.Copy).then_inc(v_ready.sem, 1)
            def o_out(ph, a, it, par, k):
                act.wait_ge(pv_done.sem, pv_done.at(ph, it, a.group * (k + 1)))
                if k == 0 and y_done.past(ph, it - 1, 0):
                    act.wait_ge(y_done.sem, y_done.at(ph, it - 1, 0))
                nc.scalar.activation(OT[a.kind][:, par, 2 * k:2 * k + 2, :].rearrange("p c n -> p (c n)"),
                                     bank[4 + k % 2][:], ACT.Copy).then_inc(ot_ready.sem, 1)

            def attention_item(ph, a):
                def item(it, par, first, last):
                    for u in steps(last):
                        if u < HEADS:
                            exp_of(ph, it, par, u)
                        out_of = late(u, O_LAG, it, par, first)
                        if out_of and (out_of[2] + 1) % a.group == 0:
                            o_out(ph, a, out_of[0], out_of[1], out_of[2] // a.group)
                        for step, name, i in a.jobs:
                            if step == u and name in NEXT and not last:
                                job_act(ph, a, it + 1, 1 - par, name, i)
                return item

            act.wait_ge(consts_made, 3)
            for ph, kind in enumerate(PHASES):
                enter(act, ph)
                if kind in ("A0", "A1"):
                    a = A0 if kind == "A0" else A1
                    if a is A1:
                        act.wait_ge(dma_a1, 64)
                    for _, name, i in a.jobs:
                        if name in NEXT:
                            job_act(ph, a, 0, 0, name, i)
                    items(act, ph, attention_item(ph, a))
                if kind in ("F0", "F1"):
                    xt_hi_of(ph, 0, 0, GT)
                    if kind == "F0":
                        gate_exp_of(ph, 0)
                    else:
                        gate_sig_of(ph, 0)
                        cwt_of(ph, 0, 0)
                    items(act, ph, f0_item(ph) if kind == "F0" else f1_item(ph))
                leave(act)

        @block.vector
        def _(dve):
            def piece_lo(i):
                _, hi, lo, n = pieces[i]
                dve.wait_ge(w_hi, i + 1)
                nc.vector.tensor_tensor(lo, stage[:, i % 2, 0:n], hi.bitcast(F32), ALU.subtract).then_inc(w_lo, 1)

            def stats_of(ph, it, tiles, step):
                if step == 0:
                    for j in range(tiles):
                        ins = nc.vector.bn_stats(stats[:, j, :], x[:, bass.ds(it * tiles + j, 1), :].rearrange("p a d -> p (a d)"))
                    ins.then_inc(stat_step.sem, 1)
                if step == 1:
                    dve.wait_ge(stat_step.sem, stat_step.at(ph, it, 1))
                    carry(dve)
                    for j in range(tiles):
                        ins = nc.vector.bn_aggr(mv[:, j, :], stats[:, j, :])
                    ins.then_inc(stat_step.sem, 1)
                if step == 2:
                    dve.wait_ge(stat_step.sem, stat_step.at(ph, it, 2))
                    nc.vector.tensor_scalar(var[:, 0:tiles], mv[:, 0:tiles, 1], EPS, None, ALU.add).then_inc(var_ready.sem, 1)

            def xn_of(ph, it, par, tiles):
                dve.wait_ge(rstd_ready.sem, rstd_ready.at(ph, it, 1))
                for j in range(tiles):
                    ins = nc.vector.tensor_scalar(xn[:, par, j, :], x[:, bass.ds(it * tiles + j, 1), :].rearrange("p a d -> p (a d)"),
                                                  mv[:, j, 0:1], rstd[:, j:j + 1], ALU.subtract, ALU.mult)
                ins.then_inc(xn_ready.sem, 1)

            def xt_lo_of(ph, it, par, tiles, b=None):
                n = tiles * P
                b = bank[MISC] if b is None else b
                dve.wait_ge(xt_hi.sem, xt_hi.at(ph, it, 1))
                nc.vector.tensor_tensor(xtlo[:, par, 0:n], b[:, 0:n], xthi[:, par, 0:n].bitcast(F32),
                                        ALU.subtract).then_inc(xt_lo.sem, 1)

            def x_add(ph, it):
                dve.wait_ge(y_turned.sem, y_turned.at(ph, it, 1))
                xs = x[:, bass.ds(it * GT, GT), :].rearrange("p t d -> p (t d)")
                nc.vector.scalar_tensor_tensor(out=xs, in0=bank[MISC][:], scalar=0.5, in1=xs,
                                               op0=ALU.mult, op1=ALU.add).then_inc(x_added.sem, 1)

            def bc(ap, n):
                return ap.unsqueeze(2).broadcast_to([P, GT, n])

            def gate0(ph, it, par, k):
                step = gate_dve
                if k == 1:
                    dve.wait_ge(logits.sem, logits.at(ph, it, 1))
                elif k == 3:
                    dve.wait_ge(gate_exp.sem, gate_exp.at(ph, it, 1))
                elif k == 15:
                    dve.wait_ge(gate_sqrt.sem, gate_sqrt.at(ph, it, 1))
                if k > 1:
                    dve.wait_ge(step.sem, step.at(ph, it, k - 1))
                lg = bank[MISC][:, 0:GT * E0].rearrange("p (t e) -> p t e", t=GT)
                top, total, inv, den, denc, dinv = (g_s[:, i, :] for i in range(6))
                if k == 1:
                    ins = nc.vector.tensor_reduce(top, lg, AX_X, ALU.max)
                elif k == 2:
                    ins = nc.vector.tensor_tensor(g_e[:], lg, bc(top, E0), ALU.subtract)
                elif k == 3:
                    ins = nc.vector.tensor_reduce(total, g_x[:], AX_X, ALU.add)
                elif k == 4:
                    ins = nc.vector.reciprocal(inv, total)
                elif k == 5:
                    ins = nc.vector.tensor_tensor(g_p[:], g_x[:], bc(inv, E0), ALU.mult)
                elif k == 6:
                    carry(dve)
                    for j in range(GT):
                        ins = nc.vector.max(g_mx[:, j, :], g_p[:, j, :])
                elif k == 7:
                    carry(dve)
                    for j in range(GT):
                        ins = nc.vector.max_index(g_ix[:, j, :], g_mx[:, j, :], g_p[:, j, :])
                elif k == 8:
                    ins = nc.vector.tensor_copy(g_if[:], g_ix[:, :, 0:2])
                elif k == 9:
                    ins = nc.vector.tensor_tensor(den, g_mx[:, :, 0], g_mx[:, :, 1], ALU.add)
                elif k == 10:
                    ins = nc.vector.tensor_scalar(denc, den, 1e-9, None, ALU.max)
                elif k == 11:
                    ins = nc.vector.reciprocal(dinv, denc)
                elif k == 12:
                    ins = nc.vector.tensor_tensor(g_m[:, 0], iota8[:].unsqueeze(1).broadcast_to([P, GT, E0]),
                                                  bc(g_if[:, :, 0], E0), ALU.is_equal)
                elif k == 13:
                    ins = nc.vector.tensor_tensor(g_m[:, 1], iota8[:].unsqueeze(1).broadcast_to([P, GT, E0]),
                                                  bc(g_if[:, :, 1], E0), ALU.is_equal)
                elif k == 14:
                    ins = nc.vector.tensor_tensor(g_w[:], g_mx[:, :, 0:2], bc(dinv, 2), ALU.mult)
                elif k == 15:
                    ins = nc.vector.tensor_tensor(g_m[:, 2], g_m[:, 0], bc(g_sq[:, :, 0], E0), ALU.mult)
                elif k == 16:
                    ins = nc.vector.tensor_tensor(g_m[:, 3], g_m[:, 1], bc(g_sq[:, :, 1], E0), ALU.mult)
                elif k == 17:
                    ins = nc.vector.tensor_tensor(gate[:, par], g_m[:, 2], g_m[:, 3], ALU.add)
                if k == 2:
                    ins.then_inc(logits_read.sem, 1)
                    ins = nc.vector.tensor_copy(g_s[:, 7, :], top)
                ins.then_inc(step.sem, 1 if k < 17 else 6)

            def gate1(ph, it, par, k):
                step = gate_dve
                if k == 1:
                    dve.wait_ge(logits.sem, logits.at(ph, it, 1))
                elif k == 5:
                    dve.wait_ge(gate_sig.sem, gate_sig.at(ph, it, 1))
                if k > 1:
                    dve.wait_ge(step.sem, step.at(ph, it, k - 1))
                lg = bank[MISC][:, 0:GT * E1].rearrange("p (t e) -> p t e", t=GT)
                total, guard, inv = (e_s[:, i, :] for i in range(3))

                def halves(t):
                    return t[:].rearrange("p t (h e) -> p t h e", h=2)

                if k == 1:
                    ins = nc.vector.tensor_tensor(e_b[:], lg, e_bias[:].unsqueeze(1).broadcast_to([P, GT, E1]), ALU.add)
                    ins.then_inc(logits_read.sem, 1)
                    dve.wait_ge(logits_read.sem, logits_read.at(ph, it, 1))
                    carry(dve)
                    for j in range(GT):
                        ins = nc.vector.max(e_mx[:, j, :], e_b[:, j, :])
                elif k == 2:
                    carry(dve)
                    for j in range(GT):
                        ins = nc.vector.match_replace(e_rep[:, j, :], e_mx[:, j, :], e_b[:, j, :], -3e38)
                elif k == 3:
                    ins = nc.vector.tensor_tensor(e_m[:], e_b[:], e_rep[:], ALU.not_equal)
                elif k == 5:
                    ins = nc.vector.tensor_tensor(e_w[:], e_sig[:], e_m[:], ALU.mult)
                elif k == 6:
                    ins = nc.vector.tensor_reduce(total, e_w[:], AX_X, ALU.add)
                elif k == 7:
                    ins = nc.vector.tensor_scalar(guard, total, 1e-8, None, ALU.add)
                elif k == 8:
                    ins = nc.vector.reciprocal(inv, guard)
                elif k == 9:
                    ins = nc.vector.tensor_tensor(e_cw[:], e_w[:], bc(inv, E1), ALU.mult)
                elif k == 10:
                    ins = nc.vector.tensor_copy(parts[:, :, :, 0, :], halves(e_cw))
                elif k == 11:
                    ins = nc.vector.tensor_tensor(halves(e_r1), halves(e_cw), parts[:, :, :, 0, :], ALU.subtract)
                elif k == 12:
                    ins = nc.vector.tensor_copy(parts[:, :, :, 1, :], halves(e_r1))
                elif k == 13:
                    ins = nc.vector.tensor_tensor(halves(e_r2), halves(e_r1), parts[:, :, :, 1, :], ALU.subtract)
                elif k == 14:
                    ins = nc.vector.tensor_copy(parts[:, :, :, 2, :], halves(e_r2))
                elif k == 4:
                    ins = nc.vector.tensor_copy(e_s[:, 3, :], e_mx[:, :, 7])
                ins.then_inc(step.sem, 1 if k < 14 else 7)

            def xe_lo_of(ph, it, e):
                dve.wait_ge(xe_hi.sem, xe_hi.at(ph, it, e + 1))
                nc.vector.tensor_tensor(xelo[:, e % 2, :], bank[4 + e % 2][:], xehi[:, e % 2, :].bitcast(F32),
                                        ALU.subtract).then_inc(xe_lo.sem, 1)

            def lo_of(ph, it, par, c, f, nch):
                s = par * nch + c
                dve.wait_ge(hi_ready.sem, hi_ready.at(ph, it, c + 1))
                nc.vector.tensor_tensor(f["hlo"][:, s % RING, :], f["h"][:, s % HR, :], f["hhi"][:, s % RING, :].bitcast(F32),
                                        ALU.subtract).then_inc(lo_ready.sem, 1)

            def f0_item(ph):
                def item(it, par, first, last):
                    for c in range(NC0):
                        if first and ph in PIECES and c % CPP == 0 and P0[0] + 2 + c // CPP < P0[1]:
                            piece_lo(P0[0] + 2 + c // CPP)
                        if c % 4 == 1 and c // 4 < E0 and not (first and c == 1):
                            xe_lo_of(ph, it, c // 4)
                        if first and c == 2:
                            xe_lo_of(ph, it, 0)
                        if not last and c in (5, 6, 7):
                            if c == 5 and ph == 0 and first:
                                dve.wait_ge(dma_x, 16 * (GROUPS - 1))
                            stats_of(ph, it + 1, GT, c - 5)
                        if c == 10 and not last:
                            xn_of(ph, it + 1, 1 - par, GT)
                        if c == 9 and not first:
                            x_add(ph, it - 1)
                        if c == 13 and not last:
                            xt_lo_of(ph, it + 1, 1 - par, GT)
                        if 18 <= c <= 27 and not last and (c != 18):
                            for k in {19: (1, 2), 20: (), 21: (3,), 22: (4, 5), 23: (6, 7), 24: (8, 9), 25: (10, 11), 26: (12, 13), 27: (14,)}[c]:
                                gate0(ph, it + 1, 1 - par, k)
                        if c in (30, 31, 32) and not last:
                            gate0(ph, it + 1, 1 - par, c - 15)
                        if c >= 1:
                            lo_of(ph, it, par, c - 1, f0, NC0)
                    lo_of(ph, it, par, NC0 - 1, f0, NC0)
                    if last:
                        x_add(ph, it)
                return item

            def mult_of(ph, it, par, c):
                s = par * NC1 + c
                dve.wait_ge(act_done.sem, act_done.at(ph, it, c + 1))
                wait_lo(dve, ph, it, c - HR)
                hb, rb_ = f1["h"][:, s % HR, :], f1["r"][:, s % RR, :]
                if c == 0:
                    ins = nc.vector.tensor_copy(hb, rb_)
                else:
                    dve.wait_ge(cb_done.sem, cb_done.at(ph, it, c))
                    ins = nc.vector.tensor_tensor(hb, bank[4 + (c - 1) % 2][:], rb_, ALU.mult)
                ins.then_inc(h_ready.sem, 1)

            def f1_item(ph):
                def item(it, par, first, last):
                    if first and ph in PIECES:
                        for i in range(P1[0] + 2, P1[1]):
                            piece_lo(i)
                    for c in range(NC1):
                        if not last and c in (5, 6, 7):
                            stats_of(ph, it + 1, GT, c - 5)
                        if c == 10 and not last:
                            xn_of(ph, it + 1, 1 - par, GT)
                        if c == 9 and not first:
                            x_add(ph, it - 1)
                        if c == 13 and not last:
                            xt_lo_of(ph, it + 1, 1 - par, GT)
                        if 16 <= c <= 25 and not last:
                            for k in {16: (1,), 17: (2,), 18: (3, 4), 19: (5,), 20: (6, 7, 8), 21: (9,), 22: (10,), 23: (11,), 24: (12, 13), 25: (14,)}[c]:
                                gate1(ph, it + 1, 1 - par, k)
                        mult_of(ph, it, par, c)
                        if c >= 1 and c - 1 not in POOL_LO:
                            lo_of(ph, it, par, c - 1, f1, NC1)
                    lo_of(ph, it, par, NC1 - 1, f1, NC1)
                    if last:
                        x_add(ph, it)
                return item

            def mask_of(ph, a, it, par, u):
                dve.wait_ge(scores.sem, scores.at(ph, it, u + 1))
                if exp_done.past(ph, it, u - 1):
                    dve.wait_ge(exp_done.sem, exp_done.at(ph, it, u - 1))
                carry(dve)
                for t in range(BT):
                    cols = slice(0, 128) if t == 0 else slice(128, 320)
                    ins = nc.vector.tensor_tensor_reduce(
                        out=MASKEDS[a.kind][:, u % 2, cols], in0=bank[u % 2][:, cols], in1=mask[:, cols], scale=-a.scale,
                        scalar=3e38, op0=ALU.add, op1=ALU.min, accum_out=negmax[:, u % 4, t:t + 1])
                ins.then_inc(masked_ready.sem, 1)

            def pt_of(ph, it, u):
                dve.wait_ge(p_turned.sem, p_turned.at(ph, it, u + 1))
                if pv_done.past(ph, it, u - 3):
                    dve.wait_ge(pv_done.sem, pv_done.at(ph, it, u - 3))
                nc.vector.tensor_copy(PTS[PHASES[ph]][:, u % 4, :], bank[2 + u % 2][:, 0:384]).then_inc(pt_ready.sem, 1)

            def rsum_of(ph, it, u):
                dve.wait_ge(exp_done.sem, exp_done.at(ph, it, u + 1))
                nc.vector.reciprocal(rsums[:, u % 4, :], sums[:, u % 4, :]).then_inc(rsum_ready.sem, 1)

            def qk_of(ph, it, par, i):
                dve.wait_ge(qk_parts.sem, qk_parts.at(ph, it, i + 1))
                if scores.past(ph, it - 1, 0):
                    dve.wait_ge(scores.sem, scores.at(ph, it - 1, 0))
                for w in range(2):
                    ins = nc.vector.scalar_tensor_tensor(
                        out=qk1[:, par, i, w, :], in0=qk_h[:, i % 2, w, :].bitcast(F32), scalar=lo_row[:, 2 + w:3 + w],
                        in1=qk_t[:, i % 2, w, :], op0=ALU.mult, op1=ALU.add)
                ins.then_inc(qk_ready.sem, 1)

            def y_of(ph, a, it):
                b = bank[6 + [j[1] for j in a.jobs].index("Y") % 2]
                dve.wait_ge(y_done.sem, y_done.at(ph, it, 1))
                xs = x[:, bass.ds(it * BT, BT), :].rearrange("p t d -> p (t d)")
                nc.vector.tensor_tensor(xs, b[:, 0:256], xs, ALU.add).then_inc(x_added.sem, 1)

            def attention_item(ph, a):
                xt_bank = bank[6 + [j[1] for j in a.jobs].index("XT") % 2]
                y_step = [j[0] for j in a.jobs if j[1] == "Y"][0]

                def item(it, par, first, last):
                    for u in steps(last):
                        if u < HEADS:
                            mask_of(ph, a, it, par, u)
                        sum_of = late(u, 1, it, par, first)
                        if sum_of:
                            rsum_of(ph, sum_of[0], sum_of[2])
                        turned = late(u, TURN_LAG, it, par, first)
                        if turned:
                            pt_of(ph, turned[0], turned[2])
                        if not last:
                            if u == 0:
                                for step in range(3):
                                    stats_of(ph, it + 1, BT, step)
                            if u == 2:
                                xn_of(ph, it + 1, 1 - par, BT)
                            if u == 4:
                                xt_lo_of(ph, it + 1, 1 - par, BT, xt_bank)
                            for step, name, i in a.jobs:
                                if a is A1 and name == "QK" and step + 1 == u:
                                    qk_of(ph, it + 1, 1 - par, i)
                        if u == y_step + 1 and not first:
                            y_of(ph, a, it - 1)
                    if last:
                        y_of(ph, a, it)
                return item

            dve.wait_ge(dma_const, 80)
            nc.vector.tensor_copy(rthi[:], router[:]).then_inc(router_split, 1)
            dve.wait_ge(router_split, 1)
            nc.vector.tensor_tensor(rtlo[:], router[:], rthi[:].bitcast(F32), ALU.subtract).then_inc(router_split, 1)
            for ph, kind in enumerate(PHASES):
                enter(dve, ph)
                if ph == 0:
                    dve.wait_ge(dma_x0, 16)
                tiles = GT if kind in ("F0", "F1") else BT
                for step in range(3):
                    stats_of(ph, 0, tiles, step)
                xn_of(ph, 0, 0, tiles)
                if kind in ("A0", "A1"):
                    a = A0 if kind == "A0" else A1
                    xt_lo_of(ph, 0, 0, tiles, bank[6 + [j[1] for j in a.jobs].index("XT") % 2])
                else:
                    xt_lo_of(ph, 0, 0, tiles)
                if ph in PIECES:
                    piece_lo(PIECES[ph][0])
                    piece_lo(PIECES[ph][0] + 1)
                if kind in ("A0", "A1"):
                    for i in range(PIECES[ph][0] + 2, PIECES[ph][1]):
                        piece_lo(i)
                    if a is A1:
                        dve.wait_ge(dma_a1, 64)
                        for i in range(a.chunks):
                            qk_of(ph, 0, 0, i)
                    items(dve, ph, attention_item(ph, a))
                if kind == "F0":
                    for k in range(1, 18):
                        gate0(ph, 0, 0, k)
                    items(dve, ph, f0_item(ph))
                if kind == "F1":
                    dve.wait_ge(dma_sel, 48)
                    for k in range(1, 15):
                        gate1(ph, 0, 0, k)
                    items(dve, ph, f1_item(ph))
                leave(dve)

        @block.tensor
        def _(pe):
            def three(o, whi, wlo, vhi, vlo, start=True, stop=True):
                nc.tensor.matmul(o, whi, vhi, start=start, stop=False)
                nc.tensor.matmul(o, whi, vlo, start=False, stop=False)
                return nc.tensor.matmul(o, wlo, vhi, start=False, stop=stop)

            def turn_xn(ph, it, par, tiles):
                pe.wait_ge(xn_ready.sem, xn_ready.at(ph, it, 1))
                if x_added.past(ph, it - 1, 0):
                    pe.wait_ge(x_added.sem, x_added.at(ph, it - 1, 0))
                if PHASES[ph] == "F1" and cwt_ready.past(ph, it, 0):
                    pe.wait_ge(cwt_ready.sem, cwt_ready.at(ph, it, 0))
                for j in range(tiles):
                    mm = nc.tensor.transpose(bank[MISC][:, j * P:(j + 1) * P], xn[:, par, j, :], ident[:])
                mm.then_inc(xn_turned.sem, 1)

            def route(ph, it, par, first_col, ne):
                pe.wait_ge(xt_lo.sem, xt_lo.at(ph, it, 1))
                cols = slice(first_col, first_col + ne)
                for j in range(GT):
                    o = bank[MISC][:, j * ne:(j + 1) * ne]
                    tok = slice(j * P, (j + 1) * P)
                    mm = three(o, xthi[:, par, tok], xtlo[:, par, tok], rthi[:, cols], rtlo[:, cols])
                mm.then_inc(logits.sem, 1)

            def turn_xe(ph, it, e):
                pe.wait_ge(xe_ready.sem, xe_ready.at(ph, it, e + 1))
                if xe_lo.past(ph, it, e - 1):
                    pe.wait_ge(xe_lo.sem, xe_lo.at(ph, it, e - 1))
                for j in range(GT):
                    mm = nc.tensor.transpose(bank[4 + e % 2][:, j * P:(j + 1) * P], xe[:, e % 2, j, :], ident[:])
                mm.then_inc(xe_turned.sem, 1)

            def turn_cw(ph, it):
                pe.wait_ge(gate_dve.sem, gate_dve.at(ph, it, gate_dve.per["F1"]))
                pe.wait_ge(gate_sig.sem, gate_sig.at(ph, it, 1))
                turned = bank[MISC][0:96, :].bitcast(BF16)
                for h in range(2):
                    for j in range(GT):
                        mm = nc.tensor.transpose(turned[:, (h * GT + j) * P:(h * GT + j + 1) * P],
                                                 parts[:, j, h, :, :].rearrange("p k e -> p (k e)"), ident_b[:])
                mm.then_inc(cw_turned.sem, 1)

            def turn_acc(ph, it, prepared):
                pe.wait_ge(acc_copied.sem, acc_copied.at(ph, it, 1))
                pe.wait_ge(logits_read.sem, logits_read.at(ph, prepared, 1))
                if PHASES[ph] == "F1":
                    pe.wait_ge(cwt_ready.sem, cwt_ready.at(ph, prepared, 1))
                for j in range(GT):
                    mm = nc.tensor.transpose(bank[MISC][:, j * P:(j + 1) * P], acc_sb[:, j * P:(j + 1) * P], ident[:])
                mm.then_inc(y_turned.sem, 1)

            def up(ph, it, par, c, nch, whi, wlo, vhi, vlo):
                s = par * nch + c
                if act_done.past(ph, it, c + 1 - UPB):
                    pe.wait_ge(act_done.sem, act_done.at(ph, it, c + 1 - UPB))
                three(bank[s % UPB][:], whi[:, c, 0:128], wlo[:, c, 0:128], vhi, vlo).then_inc(up_done.sem, 1)

            def down(ph, it, par, c, nch, whi, wlo, f):
                s = par * nch + c
                wait_lo(pe, ph, it, c)
                if c == 0 and acc_copied.past(ph, it, -1):
                    pe.wait_ge(acc_copied.sem, acc_copied.at(ph, it, -1))
                three(acc_bank(par)[:], whi[:, c, 128:256], wlo[:, c, 128:256], f["hhi"][:, s % RING, :],
                      f["hlo"][:, s % RING, :], start=(c == 0), stop=(c == nch - 1)).then_inc(down_done.sem, 1)

            def lagged_down(ph, it, par, c, first, nch, whi, wlo, f):
                if c >= LAG:
                    down(ph, it, par, c - LAG, nch, whi, wlo, f)
                elif not first:
                    down(ph, it - 1, 1 - par, nch + c - LAG, nch, whi, wlo, f)

            def tail(ph, it, par, nch, whi, wlo, f):
                if PHASES[ph] == "F1":
                    cb(ph, it, par, nch - 1)
                for c in range(nch - LAG, nch):
                    down(ph, it, par, c, nch, whi, wlo, f)
                turn_acc(ph, it, it)

            def f0_item(ph):
                def item(it, par, first, last):
                    for c in range(NC0):
                        if first and ph in PIECES and c % CPP == 0:
                            pe.wait_ge(w_lo, P0[0] + c // CPP + 1)
                        if c % 4 == 1 and c // 4 < E0 and not (first and c == 1):
                            turn_xe(ph, it, c // 4)
                        if first and c == 2:
                            turn_xe(ph, it, 0)
                        if c < SH0:
                            vhi, vlo = xthi[:, par, :], xtlo[:, par, :]
                        else:
                            e = (c - SH0) // SH0
                            if c % SH0 == 0:
                                pe.wait_ge(xe_lo.sem, xe_lo.at(ph, it, e + 1))
                            vhi, vlo = xehi[:, e % 2, :], xelo[:, e % 2, :]
                        up(ph, it, par, c, NC0, w0hi, w0lo, vhi, vlo)
                        lagged_down(ph, it, par, c, first, NC0, w0hi, w0lo, f0)
                        if c == 8 and not first:
                            turn_acc(ph, it - 1, it)
                        if c == 13 and not last:
                            turn_xn(ph, it + 1, 1 - par, GT)
                        if c == 17 and not last:
                            route(ph, it + 1, 1 - par, 0, E0)
                    if last:
                        tail(ph, it, par, NC0, w0hi, w0lo, f0)
                return item

            def cb(ph, it, par, c):
                if c == 1:
                    pe.wait_ge(cwt_ready.sem, cwt_ready.at(ph, it, 1))
                if h_ready.past(ph, it, c - 1):
                    pe.wait_ge(h_ready.sem, h_ready.at(ph, it, c - 1))
                half, j = divmod(c - 1, 16)
                nc.tensor.matmul(bank[4 + (c - 1) % 2][:], sel[:, j, :], cwt[:, par, half, :],
                                 start=True, stop=True).then_inc(cb_done.sem, 1)

            def f1_item(ph):
                def item(it, par, first, last):
                    for c in range(NC1):
                        if first and ph in PIECES and c % CPP == 0:
                            pe.wait_ge(w_lo, P1[0] + c // CPP + 1)
                        up(ph, it, par, c, NC1, w1hi, w1lo, xthi[:, par, :], xtlo[:, par, :])
                        if c >= 2:
                            cb(ph, it, par, c - 1)
                        elif c == 0 and not first:
                            cb(ph, it - 1, 1 - par, NC1 - 1)
                        lagged_down(ph, it, par, c, first, NC1, w1hi, w1lo, f1)
                        if c == 8 and not first:
                            turn_acc(ph, it - 1, it)
                        if c == 13 and not last:
                            turn_xn(ph, it + 1, 1 - par, GT)
                        if c == 16 and not last:
                            route(ph, it + 1, 1 - par, 8, E1)
                        if c == 26 and not last:
                            turn_cw(ph, it + 1)
                    if last:
                        tail(ph, it, par, NC1, w1hi, w1lo, f1)
                return item

            def job_pe(ph, a, item_kind, it, par, name, i, here):
                index = [j[1:] for j in a.jobs].index((name, i))
                b = bank[6 + index % 2]
                prev = a.before(item_kind, index)
                if prev:
                    back, pname, pi = prev
                    batch = here - back + (1 if pname in NEXT else -1)
                    read = job_read(a, pname)
                    pe.wait_ge(read.sem, read.at(ph, batch, pi + 1))
                if name == "XT":
                    pe.wait_ge(xn_ready.sem, xn_ready.at(ph, it, 1))
                    for j in range(BT):
                        mm = nc.tensor.transpose(b[:, j * P:(j + 1) * P], xn[:, par, j, :], ident[:])
                    mm.then_inc(xn_turned.sem, 1)
                if name == "QK":
                    if i == 0:
                        pe.wait_ge(xt_lo.sem, xt_lo.at(ph, it, 1))
                    for w in range(2):
                        if a is A0:
                            cols = slice(1024 * w + P * i, 1024 * w + P * i + P)
                            whi, wlo = wqkv_hi[:, cols], wqkv_lo[:, cols]
                        else:
                            cols = slice(P * (2 * i + w), P * (2 * i + w) + P)
                            whi, wlo = wa1_hi[:, cols], wa1_lo[:, cols]
                        mm = three(b[:, 256 * w:256 * w + 256], whi, wlo, xthi[:, par, 0:256], xtlo[:, par, 0:256])
                    mm.then_inc(qk_done.sem, 1)
                if name == "V":
                    if a is A0:
                        half, t = divmod(i, 2)
                        tok = slice(P * t, P * t + P)
                        cols = slice(2048 + 512 * half, 2048 + 512 * half + 512)
                        mm = three(b[:], xthi[:, par, tok], xtlo[:, par, tok], wqkv_hi[:, cols], wqkv_lo[:, cols])
                    else:
                        tok = slice(P * i, P * i + P)
                        cols = slice(1024, 1024 + P)
                        three(b[:, 0:P], xthi[:, par, tok], xtlo[:, par, tok], wa1_hi[:, cols], wa1_lo[:, cols], stop=False)
                        mm = nc.tensor.matmul(b[:, 0:P], brow1[:, 0:P], brow1[:, P + D:P + D + P], start=False, stop=True)
                    mm.then_inc(v_done.sem, 1)
                if name == "Y":
                    pe.wait_ge(ot_ready.sem, ot_ready.at(ph, it + 1, 0))
                    w = wout if a is A0 else wo1
                    for t in range(BT):
                        o = b[:, t * P:(t + 1) * P]
                        for c in range(a.chunks):
                            mm = nc.tensor.matmul(o, OT[a.kind][:, par, c, t * P:(t + 1) * P], w[:, c, :], start=(c == 0),
                                                  stop=(a is A0 and c == a.chunks - 1))
                        if a is A1:
                            mm = nc.tensor.matmul(o, brow1[:, 0:P], brow1[:, P:P + D], start=False, stop=True)
                    mm.then_inc(y_done.sem, 1)

            def scores_of(ph, a, it, par, u):
                c, r = divmod(u, a.heads_a_chunk)
                if r == 0:
                    pe.wait_ge(qk_ready.sem, qk_ready.at(ph, it, c + 1))
                if masked_ready.past(ph, it, u - 1):
                    pe.wait_ge(masked_ready.sem, masked_ready.at(ph, it, u - 1))
                rows = slice(a.rows * r, a.rows * r + a.rows)
                q, k = QK[a.kind][rows, par, c, 0, :], QK[a.kind][rows, par, c, 1, :]
                nc.tensor.matmul(bank[u % 2][:, 0:128], q[:, 0:128], k[:, 0:128], start=True, stop=True)
                nc.tensor.matmul(bank[u % 2][:, 128:320], q[:, 128:256], k[:, 64:256],
                                 start=True, stop=True).then_inc(scores.sem, 1)

            def turn_p(ph, it, u):
                pe.wait_ge(p_ready.sem, p_ready.at(ph, it, u + 1))
                if pt_ready.past(ph, it, u - 1):
                    pe.wait_ge(pt_ready.sem, pt_ready.at(ph, it, u - 1))
                for c in range(3):
                    mm = nc.tensor.transpose(bank[2 + u % 2][:, c * P:(c + 1) * P], probs[:, u % 4, c * P:(c + 1) * P], ident[:])
                mm.then_inc(p_turned.sem, 1)

            def pv_of(ph, a, it, par, u):
                k, g = divmod(u, a.group)
                pe.wait_ge(pt_ready.sem, pt_ready.at(ph, it, u + 1))
                if g == 0:
                    pe.wait_ge(v_ready.sem, v_ready.at(ph, it, 2 * (u // 8) + 2 if a is A0 else 2))
                    if ot_ready.past(ph, it, k - 1):
                        pe.wait_ge(ot_ready.sem, ot_ready.at(ph, it, k - 1))
                c, r = divmod(g, a.heads_a_chunk)
                rows = slice(a.rows * r, a.rows * r + a.rows)
                if a is A0:
                    v = [v0[:, par, t, 64 * u:64 * u + 64] for t in range(BT)]
                else:
                    v = [v1[:, par, t, 32 * (u // 4):32 * (u // 4) + 32] for t in range(BT)]
                o, pt = bank[4 + k % 2], PTS[a.kind]
                nc.tensor.matmul(o[rows, 256 * c:256 * c + 256], v[0], pt[:, u % 4, 0:256], start=True, stop=False)
                nc.tensor.matmul(o[rows, 256 * c + 128:256 * c + 256], v[1], pt[:, u % 4, 256:384],
                                 start=False, stop=True).then_inc(pv_done.sem, 1)

            def attention_item(ph, a):
                def item(it, par, first, last):
                    kind = 0 if first else 2 if last else 1
                    for u in steps(last):
                        if u < HEADS:
                            scores_of(ph, a, it, par, u)
                        turned = late(u, TURN_LAG, it, par, first)
                        if turned:
                            turn_p(ph, turned[0], turned[2])
                        summed = late(u, PV_LAG, it, par, first)
                        if summed:
                            pv_of(ph, a, *summed)
                        for step, name, i in a.jobs:
                            if step == u and name in NEXT and not last:
                                job_pe(ph, a, kind, it + 1, 1 - par, name, i, it)
                            if step == u and name not in NEXT and not first:
                                job_pe(ph, a, kind, it - 1, 1 - par, name, i, it)
                    if last:
                        job_pe(ph, a, 3, it, par, "Y", 0, it + 1)
                return item

            pe.wait_ge(router_split, 2)
            for ph, kind in enumerate(PHASES):
                enter(pe, ph)
                if kind in ("A0", "A1"):
                    a = A0 if kind == "A0" else A1
                    if a is A0:
                        pe.wait_ge(dma_wout, 16)
                    else:
                        pe.wait_ge(dma_a1, 64)
                    for _, name, i in a.jobs:
                        if name in NEXT:
                            job_pe(ph, a, -1, 0, 0, name, i, -1)
                            pe.wait_ge(w_lo, PIECES[ph][1])
                    items(pe, ph, attention_item(ph, a))
                if kind in ("F0", "F1"):
                    turn_xn(ph, 0, 0, GT)
                    if kind == "F0":
                        route(ph, 0, 0, 0, E0)
                        items(pe, ph, f0_item(ph))
                    else:
                        route(ph, 0, 0, 8, E1)
                        pe.wait_ge(dma_sel, 48)
                        turn_cw(ph, 0)
                        items(pe, ph, f1_item(ph))
                leave(pe)


def kernel(**inputs):
    import numpy as np
    import concourse.bacc as bacc
    from concourse.bass_utils import run_bass_kernel_spmd as run

    def f32(name):
        return np.ascontiguousarray(inputs[name])

    def chunks(fc, proj):
        n = fc.shape[0] // P
        up = fc.reshape(n, P, D).transpose(2, 0, 1)
        down = proj.reshape(D, n, P).transpose(2, 1, 0)
        return np.ascontiguousarray(np.concatenate([up, down], axis=2).reshape(P, n * 256))

    fc, proj = f32("L0_ffn_w_fc"), f32("L0_ffn_w_proj")
    w0 = np.concatenate([
        chunks(f32("L0_ffn_shared_fc"), f32("L0_ffn_shared_proj")),
        *[chunks(fc[e], proj[e]) for e in range(E0)]], axis=1)
    up1, down1 = f32("L1_ffn_W_up"), f32("L1_ffn_W_down")
    pad = np.zeros((D, FF1), up1.dtype)
    fc1 = np.concatenate([f32("L1_ffn_Ws_up"), pad, up1.transpose(1, 0, 2).reshape(D, E1 * FF1)], axis=1).T
    proj1 = np.concatenate([f32("L1_ffn_Ws_down"), pad.T, down1.reshape(E1 * FF1, D)], axis=0).T
    w1 = chunks(np.ascontiguousarray(fc1), np.ascontiguousarray(proj1))

    wq, bq = f32("L1_attn_Wq").reshape(D, KV1, 4, 1, DH1), f32("L1_attn_bq").reshape(KV1, 4, 1, DH1)
    wk, bk = f32("L1_attn_Wk").reshape(D, KV1, 1, 1, DH1), f32("L1_attn_bk").reshape(KV1, 1, 1, DH1)
    wa = np.zeros((D, KV1, 2, 4, 4, DH1), np.float32)
    ba = np.zeros((KV1, 2, 4, 4, DH1), np.float32)
    wa[:, :, 0], wa[:, :, 1] = wq, wk
    ba[:, 0], ba[:, 1] = bq, bk
    wv = np.zeros((D, KV1, 32), np.float32)
    wv[:, :, 0:DH1] = f32("L1_attn_Wv").reshape(D, KV1, DH1)
    bv = np.zeros((KV1, 32), np.float32)
    bv[:, 0:DH1] = f32("L1_attn_bv").reshape(KV1, DH1)
    wo = np.zeros((HEADS, 32, D), np.float32)
    wo[:, 0:DH1] = f32("L1_attn_Wo").reshape(HEADS, DH1, D)
    wa1 = np.concatenate([wa.reshape(D, 1024), wv.reshape(D, P)], axis=1)
    is_lo = np.zeros((2, 4, 4, DH1), bool)
    is_lo[0, :, 1::2], is_lo[1, :, 2:4] = True, True
    is_lo = is_lo.reshape(2, P)
    ba = ba.reshape(8, P)
    ba_lo = np.where(np.tile(is_lo, (4, 1)), ba, np.zeros_like(ba))
    bqk1 = np.concatenate([ba, ba_lo, np.where(is_lo, 1, 0), np.where(is_lo, -1, 1)]).astype(np.float32).T.copy()
    brow1 = np.concatenate([np.ones(P, np.float32), f32("L1_attn_bo"), bv.reshape(P)])[None, :]

    const = np.zeros((P, 712), np.float32)
    const[:, 256:384] = np.eye(P)
    q = np.arange(P)[:, None]
    k0 = np.arange(128)[None, :]
    const[:, 384:512] = np.where((k0 <= q) & (k0 > q - WINDOW), 0, MASKED)
    k1 = np.arange(64, 256)[None, :]
    const[:, 512:704] = np.where((k1 <= q + P) & (k1 > q + P - WINDOW), 0, MASKED)
    const[:, 704:712] = np.arange(8)[None, :]
    sel = np.zeros((P, 17, P), np.float32)
    for j in range(16):
        for part in range(3):
            sel[part * 32 + 2 * j, j, 0:64] = 1
            sel[part * 32 + 2 * j + 1, j, 64:128] = 1
    sel[:, 16, :] = np.eye(P)
    import ml_dtypes
    sel = sel.reshape(P, 17 * P).astype(ml_dtypes.bfloat16)

    arrays = {
        "x": f32("L0_attn_x"), "w0": w0, "router": np.ascontiguousarray(f32("L0_ffn_router_w").T),
        "wqkv": f32("L0_attn_Wqkv"), "wout": f32("L0_attn_Wout"), "w1": w1,
        "cent": np.ascontiguousarray(f32("L1_ffn_centroids").T), "bias1": f32("L1_ffn_expert_biases"),
        "const": const, "sel": sel,
        "wa1": wa1, "bqk1": bqk1, "wo1": wo.reshape(HEADS * 32, D), "brow1": brow1,
    }
    nc = bacc.Bacc("TRN2", target_bir_lowering=False, num_devices=1, dynamic_dma_scratch_size=1024)
    aps = [nc.dram_tensor("in_" + n, a.shape, mybir.dt.from_np(a.dtype), kind="ExternalInput").ap()
           for n, a in arrays.items()]
    out = nc.dram_tensor("out_0", arrays["x"].shape, F32, kind="ExternalOutput").ap()
    build(nc, *aps, out)
    res = run(nc, [{"in_" + n: a for n, a in arrays.items()}], core_ids=[0])
    return res.results[0]["out_0"]
```

```python
from contextlib import ExitStack

import concourse.bass as bass
from concourse import mybir

ALU = mybir.AluOpType
ACT = mybir.ActivationFunctionType
F32 = mybir.dt.float32
F32R = mybir.dt.float32r
BF16 = mybir.dt.bfloat16
U32 = mybir.dt.uint32
AX_X = mybir.AxisListType.X

P = 128
D = 128
TILES = 32
GT = 4
GROUPS = TILES // GT
BT = 2
BATCHES = TILES // BT
N = GT * P

E0, FF0 = 8, 512
E1, FF1, TOPK1 = 64, 64, 8
NC0 = (E0 + 1) * FF0 // P
SH0 = FF0 // P
NC1 = 1 + E1 * FF1 // P
H0, DH0 = 16, 64
H1, KV1, DH1 = 16, 4, 8
WINDOW = 64
UPB = 3
LAG = 5
RING = 6
HR = 6
RR = 3
EPS = 1e-5
MASKED = -1e30
PIECE = 768

PHASES = ("F0", "A0", "F0", "F1", "A1", "F1")
ITEMS = {"F0": GROUPS, "F1": GROUPS, "A0": BATCHES, "A1": BATCHES}


class Signal:

    def __init__(self, sem, **per):
        self.sem, self.per = sem, per

    def at(self, ph, it, k):
        base = sum(self.per.get(q, 0) * ITEMS[q] for q in PHASES[:ph])
        return it * self.per.get(PHASES[ph], 0) + (base + k)

    def past(self, ph, it, k):
        return not isinstance(it, int) or it * self.per[PHASES[ph]] + k > 0


POOL_LO = (5, 8, 11, 14, 16, 18, 20, 22, 24, 28)

HEADS = 16


class Attention:

    def __init__(self, kind, heads_a_chunk, dh, y_steps, jobs):
        self.kind, self.heads_a_chunk, self.dh = kind, heads_a_chunk, dh
        self.rows = P // heads_a_chunk
        self.chunks = HEADS // heads_a_chunk
        self.group = 2 * heads_a_chunk
        self.scale = dh ** -0.5
        self.jobs = jobs
        self.y_steps = y_steps
        self.y_step, = (step for step, name, _, _ in jobs if name == "Y")
        self.xt_step, = (step for step, name, _, _ in jobs if name == "XT")
        assert len(jobs) % 2 == 0

    def index(self, name, number):
        return [job[1:3] for job in self.jobs].index((name, number))

    def before(self, item, index):
        back = 0
        while item >= -1:
            index -= 2
            if index < 0:
                index += len(self.jobs)
                back += 1
                item = {3: 2, 2: 1, 1: 1, 0: -1, -1: -2}[item]
                if item == -2:
                    return None
            _, name, number, offset = self.jobs[index]
            if {-1: offset == 1, 0: offset >= 0, 1: True, 2: offset <= 0 or name == "XT", 3: offset == -1}[item]:
                return back, name, number, offset


A0 = Attention("A0", 2, DH0, 3, [
    (0, "QK", 4, 0), (1, "QK", 5, 0), (2, "QK", 6, 0), (3, "QK", 7, 0), (4, "XT", 0, 1), (5, "V", 2, 0),
    (6, "V", 3, 0), (7, "QK", 0, 1), (8, "QK", 1, 1), (9, "Y", 0, -1), (12, "QK", 2, 1), (13, "V", 0, 1),
    (14, "QK", 3, 1), (15, "V", 1, 1)])
A1 = Attention("A1", 4, DH1, 2, [
    (0, "QK", 2, 0), (3, "QK", 3, 0), (5, "XT", 0, 1), (7, "QK", 0, 1), (8, "V", 0, 1), (10, "Y", 0, -1),
    (12, "QK", 1, 1), (15, "V", 1, 1)])
SUM_LAG = 2
TURN_LAG = 5
PV_LAG = 7
O_LAG = 8


def following(ph, it, par, last):
    if not last:
        return ph, it + 1, 1 - par, GT if PHASES[ph] in ("F0", "F1") else BT
    if ph + 1 < len(PHASES):
        return ph + 1, 0, 0, GT if PHASES[ph + 1] in ("F0", "F1") else BT
    return None


F0_DVE = {19: (1, 2), 21: (3,), 22: (4, 5), 23: (6, 7), 24: (8, 9), 25: (10, 11), 26: (12, 13), 27: (14,),
          30: (15,), 31: (16,), 32: (17,)}
F1_DVE = {16: (1,), 17: (2,), 18: (3, 4), 19: (5,), 20: (6, 7, 8), 21: (9,), 22: (10,), 23: (11,), 24: (12, 13), 25: (14,)}
ROUTING = {
    ("F0", "F0"): (17, 20, 28, F0_DVE),
    ("F1", "F1"): (16, 17, None, F1_DVE),
    ("F0", "F1"): (17, 20, None, {step + 3: ks for step, ks in F1_DVE.items()}),
    ("A0", "F0"): (8, 11, 16, {9: (1,), 10: (2,), 13: (3,), 14: (4,), 15: (5,), 16: (6, 7), 17: (8, 9), 18: (10, 11, 12),
                                19: (13, 14), 22: (15, 16, 17)}),
    ("A1", "F1"): (8, 17, None, {16: (1, 2), 17: (3, 4), 19: (5, 6), 20: (7, 8), 21: (9, 10), 22: (11, 12), 23: (13, 14)}),
}


def routing(ph, nxt):
    return ROUTING.get((PHASES[ph], PHASES[nxt[0]]) if nxt else None, (None, None, None, {}))


PR = 8


def late(u, lag, it, par, first):
    h = u - lag
    if 0 <= h < HEADS:
        return it, par, h
    if h < 0 and not first:
        return it - 1, 1 - par, h + HEADS
    return None


def steps(last):
    return range(HEADS + (O_LAG if last else 0))


def build(nc, x_in, w0_in, router_in, wqkv_in, wout_in, w1_in, cent_in, bias1_in, const_in, sel_in,
          wa1_in, bqk1_in, wo1_in, brow1_in, out):
    with ExitStack() as ctx:
        def sem(name):
            return ctx.enter_context(nc.semaphore(name))

        at = {"byte": 0}

        def place(name, shape, dt, region=None):
            size = 4 if dt in (F32, F32R, U32) else 2
            for n in shape[1:]:
                size *= n
            size = (size + 31) // 32 * 32
            where = region if region is not None else at
            t = nc.alloc_sbuf_tensor_at(name, shape, dt, offset=where["byte"])
            where["byte"] += size
            assert where["byte"] <= where.get("end", 224 * 1024), name
            return t

        A_START, A_SIZE = 1280, NC0 * 256 * 4 * 2
        B_START, B_SIZE = A_START + A_SIZE, NC1 * 256 * 4 * 2 + 512
        at["byte"] = B_START + B_SIZE

        def region_a():
            return {"byte": A_START, "end": A_START + A_SIZE}

        def region_b():
            return {"byte": B_START, "end": B_START + B_SIZE}

        r = region_a()
        w0hi = place("w0hi", [P, NC0, 256], F32R, r)
        w0lo = place("w0lo", [P, NC0, 256], F32R, r)
        r = region_b()
        w1hi = place("w1hi", [P, NC1, 256], F32R, r)
        w1lo = place("w1lo", [P, NC1, 256], F32R, r)

        x = place("x", [P, TILES, D], F32)
        stage = place("stage", [P, 2, PIECE], F32)
        xn = place("xn", [P, 2, GT, D], F32)
        xthi = place("xthi", [P, 2, N], F32R)
        xtlo = place("xtlo", [P, 2, N], F32R)
        acc_sb = place("acc_sb", [P, N], F32)
        ident = place("ident", [P, P], F32)
        mask = place("mask", [P, 320], F32)
        iota8 = place("iota8", [P, E0], F32)
        ident_b = place("ident_b", [P, P], BF16)
        e_bias = place("e_bias", [P, E1], F32)
        router = place("router", [P, 8 + 64], F32)
        router0 = place("router0", [P, 2, E0], F32R)
        router1 = place("router1", [P, 2, E1], F32R)
        stats = place("stats", [P, GT, 6], F32)
        mv = place("mv", [P, GT, 2], F32)
        var = place("var", [P, GT], F32)
        rstd = place("rstd", [P, GT], F32)
        phalf = place("phalf", [P, 8], F32)
        nhalf = place("nhalf", [P, GT], F32)

        gate = place("gate", [P, 2, GT, E0], F32)
        shared = dict(at)
        e_a = place("e_a", [P, GT, E1], F32)
        e_b = place("e_b", [P, GT, E1], F32)
        e_sig = place("e_sig", [P, GT, E1], F32)
        e_rep = place("e_rep", [P, GT, E1], F32)
        e_mx = place("e_mx", [P, GT, 8], F32)
        e_s = place("e_s", [P, 3, GT], F32)
        parts = place("parts", [P, GT, 2, 3, 32], BF16)
        shared["end"] = at["byte"]
        g_l = place("g_l", [P, GT, E0], F32, shared)
        g_e = place("g_e", [P, GT, E0], F32, shared)
        g_x = place("g_x", [P, GT, E0], F32, shared)
        g_p = place("g_p", [P, GT, E0], F32, shared)
        g_mx = place("g_mx", [P, GT, 8], F32, shared)
        g_ix = place("g_ix", [P, GT, 8], U32, shared)
        g_if = place("g_if", [P, GT, 2], F32, shared)
        g_s = place("g_s", [P, 6, GT], F32, shared)
        g_w = place("g_w", [P, GT, 2], F32, shared)
        g_sq = place("g_sq", [P, GT, 2], F32, shared)
        g_m = place("g_m", [P, 4, GT, E0], F32, shared)
        e_m, e_w, e_cw, e_r1, e_r2 = e_rep, e_sig, e_b, e_a, e_sig

        def ffn_scratch(tag, r):
            return {
                "r": place("r" + tag, [P, RR, N], F32, r),
                "h": place("h" + tag, [P, HR, N], F32, r),
                "hhi": place("hhi" + tag, [P, RING, N], F32R, r),
                "hlo": place("hlo" + tag, [P, RING, N], F32R, r),
            }

        rb = region_b()
        f0 = ffn_scratch("0", rb)
        xe = place("xe", [P, 2, GT, D], F32, rb)
        xehi = place("xehi", [P, 2, N], F32R, rb)
        xelo = place("xelo", [P, 2, N], F32R, rb)
        ra = region_a()
        sel = place("sel", [96, 16, P], BF16, ra)
        after_consts = dict(ra)
        f1 = ffn_scratch("1", ra)
        cwt = place("cwt", [96, 2, 2, N], BF16, ra)
        rb = region_b()
        wqkv_hi = place("wqkv_hi", [P, 3 * HEADS * DH0], F32R, rb)
        wqkv_lo = place("wqkv_lo", [P, 3 * HEADS * DH0], F32R, rb)
        wout = place("wout", [P, 8, D], F32, rb)
        ra = dict(after_consts)
        wa1_hi = place("wa1_hi", [P, 1024 + P], F32R, ra)
        wa1_lo = place("wa1_lo", [P, 1024 + P], F32R, ra)
        wo1 = place("wo1", [P, KV1, D], F32, ra)
        brow1 = place("brow1", [1, P + D + P], F32, ra)
        bqk1 = place("bqk1", [P, 8], F32, ra)
        less_hi = place("less_hi", [P, 2], F32, ra)
        qk_v = place("qk_v", [P, 2, 2, 256], F32, ra)
        qk_h = place("qk_h", [P, 2, 2, 256], F32R, ra)
        qk1 = place("qk1", [P, 2, 4, 2, 256], F32R, ra)
        v1 = place("v1", [P, 2, BT, P], F32, ra)
        ot1 = place("ot1", [P, 4, 256], F32, ra)
        MASKEDS = {"A0": place("masked0", [P, 2, 320], F32, rb), "A1": place("masked1", [P, 2, 320], F32, ra)}
        PTS = {"A0": place("pt0", [P, 4, 384], F32), "A1": place("pt1", [P, 4, 384], F32, ra)}
        PROBS = {"A0": place("probs0", [P, PR, 384], F32, rb), "A1": place("probs1", [P, PR, 384], F32, ra)}
        negmax = place("negmax", [P, PR, BT], F32)
        sums = place("sums", [P, PR, BT], F32)
        rsums = place("rsums", [P, PR, BT], F32)
        v0 = place("v0", [P, 2, BT, HEADS * DH0], F32, rb)
        ot0 = place("ot0", [P, 8, 256], F32, rb)
        qk0 = place("qk0", [P, 2, 8, 2, 256], F32)
        QK = {"A0": qk0, "A1": qk1}
        OT = {"A0": ot0, "A1": ot1}

        bank = [ctx.enter_context(nc.psum_tensor(f"bank{i}", [P, 512], F32)) for i in range(8)]
        MISC = 6

        def acc_bank(par):
            return bank[3 + 4 * par]

        dma_const = sem("dma_const")
        dma_sel = sem("dma_sel")
        dma_wout = sem("dma_wout")
        dma_a1 = sem("dma_a1")
        dma_x0 = sem("dma_x0")
        dma_x = sem("dma_x")
        dma_stage = [sem("dma_stage0"), sem("dma_stage1")]
        dma_out = sem("dma_out")
        consts_made = sem("consts_made")
        router_split = sem("router_split")
        w_hi = sem("w_hi")
        w_lo = sem("w_lo")
        phase_done = sem("phase_done")
        probs_zeroed = sem("probs_zeroed")

        carried = sem("carried")

        def carry(eng):
            eng.sem_inc(carried, 1)

        var_ready = Signal(sem("var_ready"), F0=1, F1=1, A0=1, A1=1)
        stat_step = Signal(sem("stat_step"), F0=2, F1=2, A0=2, A1=2)
        rstd_ready = Signal(sem("rstd_ready"), F0=1, F1=1, A0=1, A1=1)
        xn_ready = Signal(sem("xn_ready"), F0=1, F1=1, A0=1, A1=1)
        xn_turned = Signal(sem("xn_turned"), F0=1, F1=1, A0=1, A1=1)
        xt_hi = Signal(sem("xt_hi"), F0=1, F1=1, A0=1, A1=1)
        xt_lo = Signal(sem("xt_lo"), F0=1, F1=1, A0=1, A1=1)
        logits = Signal(sem("logits"), F0=1, F1=1)
        logits_read = Signal(sem("logits_read"), F0=1, F1=1)
        gate_dve = Signal(sem("gate_dve"), F0=17, F1=14)
        gate_exp = Signal(sem("gate_exp"), F0=1)
        gate_sqrt = Signal(sem("gate_sqrt"), F0=1)
        gate_sig = Signal(sem("gate_sig"), F1=1)
        cw_turned = Signal(sem("cw_turned"), F1=1)
        cwt_ready = Signal(sem("cwt_ready"), F1=1)
        up_done = Signal(sem("up_done"), F0=NC0, F1=NC1)
        act_done = Signal(sem("act_done"), F0=NC0, F1=NC1)
        h_ready = Signal(sem("h_ready"), F0=NC0, F1=NC1)
        hi_ready = Signal(sem("hi_ready"), F0=NC0, F1=NC1)
        lo_ready = Signal(sem("lo_ready"), F0=NC0, F1=NC1 - len(POOL_LO))
        lo_pool = Signal(sem("lo_pool"), F1=len(POOL_LO))

        def wait_lo(eng, ph, it, c):
            nch = NC0 if PHASES[ph] == "F0" else NC1
            if c < 0:
                it, c = it - 1, c + nch
            if isinstance(it, int) and it < 0:
                return
            if PHASES[ph] == "F1" and c in POOL_LO:
                eng.wait_ge(lo_pool.sem, lo_pool.at(ph, it, POOL_LO.index(c) + 1))
            else:
                others = sum(q < c for q in POOL_LO) if PHASES[ph] == "F1" else 0
                eng.wait_ge(lo_ready.sem, lo_ready.at(ph, it, c + 1 - others))
        down_done = Signal(sem("down_done"), F0=NC0, F1=NC1)
        xe_ready = Signal(sem("xe_ready"), F0=E0)
        xe_turned = Signal(sem("xe_turned"), F0=E0)
        xe_hi = Signal(sem("xe_hi"), F0=E0)
        xe_lo = Signal(sem("xe_lo"), F0=E0)
        cb_done = Signal(sem("cb_done"), F1=NC1 - 1)
        scores = Signal(sem("scores"), A0=HEADS, A1=HEADS)
        masked_ready = Signal(sem("masked_ready"), A0=HEADS, A1=HEADS)
        exp_done = Signal(sem("exp_done"), A0=HEADS, A1=HEADS)
        p_turned = Signal(sem("p_turned"), A0=HEADS, A1=HEADS)
        pt_ready = Signal(sem("pt_ready"), A0=HEADS, A1=HEADS)
        pv_done = Signal(sem("pv_done"), A0=HEADS, A1=HEADS)
        rsum_ready = Signal(sem("rsum_ready"), A0=HEADS // 2, A1=HEADS // 2)
        p_ready = Signal(sem("p_ready"), A0=HEADS, A1=HEADS)
        qk_done = Signal(sem("qk_done"), A0=8, A1=4)
        qk_ready = Signal(sem("qk_ready"), A0=8, A1=4)
        qk_value = Signal(sem("qk_value"), A1=4)
        qk_parts = Signal(sem("qk_parts"), A1=4)
        v_done = Signal(sem("v_done"), A0=4, A1=2)
        v_ready = Signal(sem("v_ready"), A0=4, A1=2)
        ot_ready = Signal(sem("ot_ready"), A0=4, A1=2)

        def job_read(a, name):
            return {"XT": xt_lo, "QK": qk_ready if a is A0 else qk_value, "V": v_ready, "Y": x_added}[name]

        acc_copied = Signal(sem("acc_copied"), F0=1, F1=1)
        y_turned = Signal(sem("y_turned"), F0=1, F1=1)
        y_done = Signal(sem("y_done"), A0=1, A1=1)
        x_added = Signal(sem("x_added"), F0=1, F1=1, A0=1, A1=1)

        pieces = []

        def add_pieces(dram, hi, lo, cols):
            first = len(pieces)
            for c in range(0, cols, PIECE):
                n = min(PIECE, cols - c)
                pieces.append((dram[:, c:c + n], hi[:, c:c + n], lo[:, c:c + n], n))
            return first, len(pieces)

        def flat(t):
            return t[:].rearrange("p c k -> p (c k)")

        P0 = add_pieces(w0_in, flat(w0hi), flat(w0lo), NC0 * 256)
        PA0 = add_pieces(wqkv_in, wqkv_hi[:], wqkv_lo[:], 3 * HEADS * DH0)
        P1 = add_pieces(w1_in, flat(w1hi), flat(w1lo), NC1 * 256)
        PA1 = add_pieces(wa1_in, wa1_hi[:], wa1_lo[:], 1024 + P)
        PIECES = {PHASES.index(kind): p for kind, p in (("F0", P0), ("A0", PA0), ("F1", P1), ("A1", PA1))
                  if kind in PHASES}
        CPP = PIECE // 256

        block = ctx.enter_context(nc.Block())

        def items(eng, ph, item):
            n = ITEMS[PHASES[ph]]
            item(0, 0, True, False)
            with eng.Fori(0, n // 2 - 1) as k:
                item(2 * k + 1, 1, False, False)
                item(2 * k + 2, 0, False, False)
            item(n - 1, 1, False, True)

        def enter(eng, ph):
            if ph:
                eng.wait_ge(phase_done, 4 * ph)

        def leave(eng):
            eng.drain().then_inc(phase_done, 1)

        @block.sync
        def _(sp):
            xv = x_in.rearrange("b (u p) d -> p (b u) d", p=P)
            ov = out.rearrange("b (u p) d -> p (b u) d", p=P)
            sp.dma_start(x[:, 0:GT, :], xv[:, 0:GT, :]).then_inc(dma_x0, 16)
            sp.dma_start(ident[:], const_in[:, 0:128]).then_inc(dma_const, 16)
            sp.dma_start(router[:, 0:8], router_in).then_inc(dma_const, 16)
            sp.dma_start(router[:, 8:72], cent_in).then_inc(dma_const, 16)
            sp.dma_start(mask[:], const_in[:, 128:448]).then_inc(dma_const, 16)
            sp.dma_start(iota8[:], const_in[:, 448:456]).then_inc(dma_const, 16)
            sp.dma_start(ident_b[:], sel_in[:, 2048:2176]).then_inc(dma_const, 16)
            sp.dma_start(e_bias[:], bias1_in.rearrange("(a e) -> a e", a=1).broadcast_to([P, E1])).then_inc(dma_const, 16)
            for i, (dram, _, _, n) in enumerate(pieces):
                if i >= 2:
                    sp.wait_ge(w_lo, i - 1)
                sp.dma_start(stage[:, i % 2, 0:n], dram).then_inc(dma_stage[i % 2], 16)
                if i == 1:
                    for g in range(1, GROUPS):
                        sp.dma_start(x[:, GT * g:GT * g + GT, :], xv[:, GT * g:GT * g + GT, :]).then_inc(dma_x, 16)
                if i == PA0[0] + 1:
                    sp.wait_ge(phase_done, 4 * PHASES.index("A0"))
                    sp.dma_start(wout[:], wout_in.rearrange("(c p) d -> p c d", p=P)).then_inc(dma_wout, 16)
                if i == P1[0] + 1:
                    sp.wait_ge(phase_done, 4 * PHASES.index("F1"))
                    sp.dma_start(sel[:], sel_in[0:96, 0:2048].rearrange("p (c k) -> p c k", c=16)).then_inc(dma_sel, 16)
                if i == PA1[0] + 1:
                    sp.wait_ge(phase_done, 4 * PHASES.index("A1"))
                    sp.dma_start(wo1[:], wo1_in.rearrange("(c p) d -> p c d", p=P)).then_inc(dma_a1, 16)
                    sp.dma_start(bqk1[:], bqk1_in[:, 0:8]).then_inc(dma_a1, 16)
                    sp.dma_start(less_hi[:], bqk1_in[:, 8:10]).then_inc(dma_a1, 16)
                    sp.dma_start(brow1[:], brow1_in).then_inc(dma_a1, 16)
            for q in range(4):
                sp.wait_ge(x_added.sem, x_added.at(len(PHASES) - 1, 2 * q + 1, 1))
                sp.dma_start(ov[:, 8 * q:8 * q + 8, :], x[:, 8 * q:8 * q + 8, :]).then_inc(dma_out, 16)
            sp.wait_ge(dma_out, 64)

        @block.gpsimd
        def _(pool):
            nc.gpsimd.memset(phalf[:], 0.5).then_inc(consts_made, 1)
            nc.gpsimd.memset(nhalf[:], -0.5).then_inc(consts_made, 1)
            pool.wait_ge(consts_made, 2)

            def piece_hi(i):
                _, hi, _, n = pieces[i]
                pool.wait_ge(dma_stage[i % 2], 16 * (i // 2 + 1))
                nc.gpsimd.tensor_scalar(hi, stage[:, i % 2, 0:n], 1.0, 1.0, ALU.mult, ALU.mult).then_inc(w_hi, 1)

            def rstd_of(ph, it, par, tiles):
                pool.wait_ge(var_ready.sem, var_ready.at(ph, it, 1))
                nc.gpsimd.tensor_tensor(rstd[:, 0:tiles], var[:, 0:tiles], nhalf[:, 0:tiles],
                                        ALU.pow).then_inc(rstd_ready.sem, 1)

            def sqrt_of(ph, it):
                pool.wait_ge(gate_dve.sem, gate_dve.at(ph, it, 14))
                nc.gpsimd.tensor_tensor(g_sq[:].rearrange("p t k -> p (t k)"), g_w[:].rearrange("p t k -> p (t k)"),
                                        phalf[:, 0:8], ALU.pow).then_inc(gate_sqrt.sem, 1)

            def gated_x(ph, it, par, e):
                if e == 0:
                    pool.wait_ge(gate_dve.sem, gate_dve.at(ph, it, gate_dve.per["F0"]))
                if xe_turned.past(ph, it, e - 1):
                    pool.wait_ge(xe_turned.sem, xe_turned.at(ph, it, e - 1))
                carry(pool)
                for j in range(GT):
                    ins = nc.gpsimd.tensor_scalar(xe[:, e % 2, j, :], xn[:, par, j, :],
                                                  gate[:, par, j, e:e + 1], 1.0, ALU.mult, ALU.mult)
                ins.then_inc(xe_ready.sem, 1)

            def f0_item(ph):
                def item(it, par, first, last):
                    nxt = following(ph, it, par, last)
                    for c in range(NC0):
                        if first and ph in PIECES and c % CPP == 0 and P0[0] + 2 + c // CPP < P0[1]:
                            piece_hi(P0[0] + 2 + c // CPP)
                        if c == 0 and first:
                            gated_x(ph, it, par, 0)
                        if c == NC0 - 2 and not last:
                            gated_x(ph, it + 1, 1 - par, 0)
                        if c % 4 == 1 and c // 4 + 1 < E0:
                            gated_x(ph, it, par, c // 4 + 1)
                        if c == 7 and nxt:
                            rstd_of(*nxt)
                        if c == routing(ph, nxt)[2]:
                            sqrt_of(nxt[0], nxt[1])
                        s = (par * NC0 + c)
                        pool.wait_ge(h_ready.sem, h_ready.at(ph, it, c + 1))
                        if down_done.past(ph, it, c + 1 - RING):
                            pool.wait_ge(down_done.sem, down_done.at(ph, it, c + 1 - RING))
                        carry(pool)
                        nc.gpsimd.tensor_scalar(f0["hhi"][:, s % RING, :], f0["h"][:, s % HR, :], 1.0, 1.0,
                                                ALU.mult, ALU.mult).then_inc(hi_ready.sem, 1)
                return item

            def f1_item(ph):
                def item(it, par, first, last):
                    nxt = following(ph, it, par, last)
                    for c in range(NC1):
                        if first and ph in PIECES and c % CPP == 0 and P1[0] + 2 + c // CPP < P1[1]:
                            piece_hi(P1[0] + 2 + c // CPP)
                        if c == 7 and nxt:
                            rstd_of(*nxt)
                        if c in POOL_LO:
                            lo_of_pool(ph, it, par, c)
                return item

            def lo_of_pool(ph, it, par, c):
                s = par * NC1 + c
                pool.wait_ge(hi_ready.sem, hi_ready.at(ph, it, c + 1))
                nc.gpsimd.tensor_tensor(f1["hlo"][:, s % RING, :], f1["h"][:, s % HR, :],
                                        f1["hhi"][:, s % RING, :].bitcast(F32), ALU.subtract).then_inc(lo_pool.sem, 1)

            def attention_item(ph):
                def item(it, par, first, last):
                    nxt = following(ph, it, par, last)
                    for u in steps(last):
                        if u == 0 and nxt:
                            rstd_of(*nxt)
                        if last and u == routing(ph, nxt)[2]:
                            sqrt_of(nxt[0], nxt[1])
                        for step, name, i, offset in A1.jobs:
                            if PHASES[ph] == "A1" and name == "QK" and step == u and not (last and offset):
                                parts_of(ph, it + offset, i)
                        if u < HEADS:
                            norm_of(ph, it, u)
                return item

            def parts_of(ph, it, i):
                pool.wait_ge(qk_value.sem, qk_value.at(ph, it, i + 1))
                if qk_ready.past(ph, it, i - 1):
                    pool.wait_ge(qk_ready.sem, qk_ready.at(ph, it, i - 1))
                carry(pool)
                nc.gpsimd.tensor_scalar(qk_h[:, i % 2, :, :], qk_v[:, i % 2, :, :], 1.0, 1.0, ALU.mult,
                                        ALU.mult).then_inc(qk_parts.sem, 1)

            def norm_of(ph, it, u):
                pool.wait_ge(rsum_ready.sem, rsum_ready.at(ph, it, u // 2 + 1))
                carry(pool)
                for t, keys in enumerate((slice(0, 128), slice(192, 384))):
                    p = PROBS[PHASES[ph]][:, u % PR, keys]
                    ins = nc.gpsimd.tensor_scalar(p, p, rsums[:, u % PR, t:t + 1], 1.0, ALU.mult, ALU.mult)
                ins.then_inc(p_ready.sem, 1)

            for ph, kind in enumerate(PHASES):
                enter(pool, ph)
                if ph == 0:
                    rstd_of(ph, 0, 0, GT)
                if ph in PIECES:
                    piece_hi(PIECES[ph][0])
                    piece_hi(PIECES[ph][0] + 1)
                if kind in ("F0", "F1"):
                    if ph == 0:
                        sqrt_of(ph, 0)
                    items(pool, ph, f0_item(ph) if kind == "F0" else f1_item(ph))
                else:
                    nc.gpsimd.memset(PROBS[kind][:, :, 128:192], 0.0).then_inc(probs_zeroed, 1)
                    for i in range(PIECES[ph][0] + 2, PIECES[ph][1]):
                        piece_hi(i)
                    if kind == "A1":
                        pool.wait_ge(dma_a1, 64)
                        for _, name, i, offset in A1.jobs:
                            if name == "QK" and offset == 1:
                                parts_of(ph, 0, i)
                    items(pool, ph, attention_item(ph))
                leave(pool)

        @block.scalar
        def _(act):
            def xt_hi_of(ph, it, par, tiles):
                n = tiles * P
                act.wait_ge(xn_turned.sem, xn_turned.at(ph, it, 1))
                nc.scalar.activation(xthi[:, par, 0:n], bank[MISC][:, 0:n], ACT.Copy).then_inc(xt_hi.sem, 1)

            def acc_out(ph, it, par):
                act.wait_ge(down_done.sem, down_done.at(ph, it + 1, 0))
                if y_turned.past(ph, it, 0):
                    act.wait_ge(y_turned.sem, y_turned.at(ph, it, 0))
                nc.scalar.activation(acc_sb[:], acc_bank(par)[:], ACT.Copy).then_inc(acc_copied.sem, 1)

            def gate_exp_of(ph, it):
                act.wait_ge(gate_dve.sem, gate_dve.at(ph, it, 2))
                nc.scalar.activation(g_x[:], g_e[:], ACT.Exp).then_inc(gate_exp.sem, 1)

            def gate_sig_of(ph, it):
                act.wait_ge(logits_read.sem, logits_read.at(ph, it, 1))
                nc.scalar.activation(e_sig[:], e_a[:], ACT.Sigmoid).then_inc(gate_sig.sem, 1)

            def gate_act_of(ph, it):
                if PHASES[ph] == "F0":
                    gate_exp_of(ph, it)
                else:
                    gate_sig_of(ph, it)

            def cwt_of(ph, it, par):
                act.wait_ge(cw_turned.sem, cw_turned.at(ph, it, 1))
                nc.scalar.activation(cwt[:, par, :, :].rearrange("p h n -> p (h n)"),
                                     bank[MISC][0:96, :].bitcast(BF16), ACT.Copy).then_inc(cwt_ready.sem, 1)

            def xe_hi_of(ph, it, e):
                act.wait_ge(xe_turned.sem, xe_turned.at(ph, it, e + 1))
                used = SH0 + SH0 * (e - 1)
                if e >= 2:
                    act.wait_ge(up_done.sem, up_done.at(ph, it, used))
                elif up_done.past(ph, it, 0):
                    act.wait_ge(up_done.sem, up_done.at(ph, it, 0) - (1 - e) * SH0)
                nc.scalar.activation(xehi[:, e % 2, :], bank[4 + e % 2][:], ACT.Copy).then_inc(xe_hi.sem, 1)

            def act_of(ph, it, par, c, func, f, nch):
                s = par * nch + c
                act.wait_ge(up_done.sem, up_done.at(ph, it, c + 1))
                if h_ready.past(ph, it, c + 1 - RR):
                    act.wait_ge(h_ready.sem, h_ready.at(ph, it, c + 1 - RR))
                nc.scalar.activation(f["r"][:, s % RR, :], bank[s % UPB][:], func).then_inc(act_done.sem, 1)

            def square_of(ph, it, par, c):
                s = par * NC0 + c
                act.wait_ge(act_done.sem, act_done.at(ph, it, c + 1))
                wait_lo(act, ph, it, c - HR)
                nc.scalar.activation(f0["h"][:, s % HR, :], f0["r"][:, s % RR, :], ACT.Square).then_inc(h_ready.sem, 1)

            def f0_item(ph):
                def item(it, par, first, last):
                    nxt = following(ph, it, par, last)
                    for c in range(NC0):
                        act_of(ph, it, par, c, ACT.Relu, f0, NC0)
                        if c >= 1:
                            square_of(ph, it, par, c - 1)
                        if c % 4 == 1 and c // 4 < E0 and not (first and c == 1):
                            xe_hi_of(ph, it, c // 4)
                        if first and c == 2:
                            xe_hi_of(ph, it, 0)
                        if c == 6 and not first:
                            acc_out(ph, it - 1, 1 - par)
                        if c == 13 and nxt:
                            xt_hi_of(*nxt)
                        if c == routing(ph, nxt)[1]:
                            gate_act_of(nxt[0], nxt[1])
                    square_of(ph, it, par, NC0 - 1)
                    if last:
                        acc_out(ph, it, par)
                return item

            def hi_of(ph, it, par, c):
                s = par * NC1 + c
                act.wait_ge(h_ready.sem, h_ready.at(ph, it, c + 1))
                if down_done.past(ph, it, c + 1 - RING):
                    act.wait_ge(down_done.sem, down_done.at(ph, it, c + 1 - RING))
                nc.scalar.activation(f1["hhi"][:, s % RING, :], f1["h"][:, s % HR, :], ACT.Copy).then_inc(hi_ready.sem, 1)

            def f1_item(ph):
                def item(it, par, first, last):
                    nxt = following(ph, it, par, last)
                    for c in range(NC1):
                        act_of(ph, it, par, c, ACT.Silu, f1, NC1)
                        if c >= 1:
                            hi_of(ph, it, par, c - 1)
                        if c == 6 and not first:
                            acc_out(ph, it - 1, 1 - par)
                        if c == 13 and nxt:
                            xt_hi_of(*nxt)
                        if c == routing(ph, nxt)[1]:
                            gate_act_of(nxt[0], nxt[1])
                        if c == 28 and not last:
                            cwt_of(ph, it + 1, 1 - par)
                    hi_of(ph, it, par, NC1 - 1)
                    if last:
                        acc_out(ph, it, par)
                return item

            def exp_of(ph, it, par, u):
                act.wait_ge(masked_ready.sem, masked_ready.at(ph, it, u + 1))
                if p_turned.past(ph, it, u + 1 - PR):
                    act.wait_ge(p_turned.sem, p_turned.at(ph, it, u + 1 - PR))
                for t in range(BT):
                    masked = MASKEDS[PHASES[ph]]
                    src = masked[:, u % 2, 0:128] if t == 0 else masked[:, u % 2, 128:320]
                    dst = PROBS[PHASES[ph]][:, u % PR, slice(0, 128) if t == 0 else slice(192, 384)]
                    ins = nc.scalar.activation(dst, src, ACT.Exp, bias=negmax[:, u % PR, t:t + 1], scale=-1.0,
                                               accum_out=sums[:, u % PR, t:t + 1])
                ins.then_inc(exp_done.sem, 1)

            def job_act(ph, a, it, par, name, i):
                b = bank[6 + a.index(name, i) % 2]
                if name == "QK":
                    act.wait_ge(qk_done.sem, qk_done.at(ph, it, i + 1))
                    if a is A0 and scores.past(ph, it - 1, 0):
                        act.wait_ge(scores.sem, scores.at(ph, it - 1, 0))
                    if a is A0:
                        nc.scalar.activation(qk0[:, par, i, :, :].rearrange("p w n -> p (w n)"), b[:],
                                             ACT.Copy).then_inc(qk_ready.sem, 1)
                    else:
                        if qk_ready.past(ph, it, i - 1):
                            act.wait_ge(qk_ready.sem, qk_ready.at(ph, it, i - 1))
                        for w in range(2):
                            ins = nc.scalar.activation(qk_v[:, i % 2, w, :], b[:, 256 * w:256 * w + 256], ACT.Identity,
                                                       bias=bqk1[:, 2 * i + w:2 * i + w + 1])
                        ins.then_inc(qk_value.sem, 1)
                if name == "V":
                    act.wait_ge(v_done.sem, v_done.at(ph, it, i + 1))
                    if pv_done.past(ph, it - 1, 0):
                        act.wait_ge(pv_done.sem, pv_done.at(ph, it - 1, 0))
                    if a is A0:
                        half, t = divmod(i, 2)
                        nc.scalar.activation(v0[:, par, t, 512 * half:512 * half + 512], b[:], ACT.Copy).then_inc(v_ready.sem, 1)
                    else:
                        nc.scalar.activation(v1[:, par, i, :], b[:, 0:P], ACT.Copy).then_inc(v_ready.sem, 1)
            def o_out(ph, a, it, k):
                act.wait_ge(pv_done.sem, pv_done.at(ph, it, a.group * (k + 1)))
                if k == 0 and y_done.past(ph, it, 0):
                    act.wait_ge(y_done.sem, y_done.at(ph, it, 0))
                nc.scalar.activation(OT[a.kind][:, 2 * k:2 * k + 2, :].rearrange("p c n -> p (c n)"),
                                     bank[4 + k % 2][:], ACT.Copy).then_inc(ot_ready.sem, 1)

            def attention_item(ph, a):
                def item(it, par, first, last):
                    nxt = following(ph, it, par, last)
                    for u in steps(last):
                        if u < HEADS:
                            exp_of(ph, it, par, u)
                        if last and u == routing(ph, nxt)[1]:
                            gate_act_of(nxt[0], nxt[1])
                        out_of = late(u, O_LAG, it, par, first)
                        if out_of and (out_of[2] + 1) % a.group == 0:
                            o_out(ph, a, out_of[0], out_of[2] // a.group)
                        for step, name, i, offset in a.jobs:
                            if step == u and name == "XT" and nxt:
                                if v_done.past(ph, it, 0):
                                    act.wait_ge(v_done.sem, v_done.at(ph, it, 0))
                                    act.wait_ge(qk_done.sem, qk_done.at(ph, it, 0))
                                xt_hi_of(*nxt)
                            if step == u and name in ("QK", "V") and not (last and offset):
                                job_act(ph, a, it + offset, par ^ offset, name, i)
                return item

            for ph, kind in enumerate(PHASES):
                enter(act, ph)
                if kind in ("A0", "A1"):
                    a = A0 if kind == "A0" else A1
                    if a is A1:
                        act.wait_ge(dma_a1, 64)
                    for _, name, i, offset in a.jobs:
                        if name in ("QK", "V") and offset == 1:
                            job_act(ph, a, 0, 0, name, i)
                    items(act, ph, attention_item(ph, a))
                if kind in ("F0", "F1"):
                    if ph == 0:
                        xt_hi_of(ph, 0, 0, GT)
                        gate_act_of(ph, 0)
                    if kind == "F1":
                        cwt_of(ph, 0, 0)
                    items(act, ph, f0_item(ph) if kind == "F0" else f1_item(ph))
                leave(act)

        @block.vector
        def _(dve):
            def piece_lo(i):
                _, hi, lo, n = pieces[i]
                dve.wait_ge(w_hi, i + 1)
                nc.vector.tensor_tensor(lo, stage[:, i % 2, 0:n], hi.bitcast(F32), ALU.subtract).then_inc(w_lo, 1)

            def stats_of(ph, it, par, tiles, step):
                if step == 0:
                    for j in range(tiles):
                        xs = x[:, bass.ds(it * tiles + j, 1), :].rearrange("p a d -> p (a d)")
                        ins = nc.vector.bn_stats(stats[:, j, :], xs)
                    ins.then_inc(stat_step.sem, 1)
                if step == 1:
                    dve.wait_ge(stat_step.sem, stat_step.at(ph, it, 1))
                    carry(dve)
                    for j in range(tiles):
                        ins = nc.vector.bn_aggr(mv[:, j, :], stats[:, j, :])
                    ins.then_inc(stat_step.sem, 1)
                if step == 2:
                    dve.wait_ge(stat_step.sem, stat_step.at(ph, it, 2))
                    nc.vector.tensor_scalar(var[:, 0:tiles], mv[:, 0:tiles, 1], EPS, None, ALU.add).then_inc(var_ready.sem, 1)

            def xn_of(ph, it, par, tiles):
                dve.wait_ge(rstd_ready.sem, rstd_ready.at(ph, it, 1))
                for j in range(tiles):
                    ins = nc.vector.tensor_scalar(xn[:, par, j, :], x[:, bass.ds(it * tiles + j, 1), :].rearrange("p a d -> p (a d)"),
                                                  mv[:, j, 0:1], rstd[:, j:j + 1], ALU.subtract, ALU.mult)
                ins.then_inc(xn_ready.sem, 1)

            def xt_lo_of(ph, it, par, tiles):
                n = tiles * P
                dve.wait_ge(xt_hi.sem, xt_hi.at(ph, it, 1))
                nc.vector.tensor_tensor(xtlo[:, par, 0:n], bank[MISC][:, 0:n], xthi[:, par, 0:n].bitcast(F32),
                                        ALU.subtract).then_inc(xt_lo.sem, 1)

            def x_add(ph, it):
                dve.wait_ge(y_turned.sem, y_turned.at(ph, it, 1))
                xs = x[:, bass.ds(it * GT, GT), :].rearrange("p t d -> p (t d)")
                nc.vector.scalar_tensor_tensor(out=xs, in0=bank[MISC][:], scalar=0.5, in1=xs,
                                               op0=ALU.mult, op1=ALU.add).then_inc(x_added.sem, 1)

            def bc(ap, n):
                return ap.unsqueeze(2).broadcast_to([P, GT, n])

            def gate0(ph, it, par, k):
                step = gate_dve
                if k == 1:
                    dve.wait_ge(logits.sem, logits.at(ph, it, 1))
                elif k == 3:
                    dve.wait_ge(gate_exp.sem, gate_exp.at(ph, it, 1))
                elif k == 15:
                    dve.wait_ge(gate_sqrt.sem, gate_sqrt.at(ph, it, 1))
                if step.past(ph, it, k - 1) or ph:
                    dve.wait_ge(step.sem, step.at(ph, it, k - 1))
                lg = bank[MISC][:, 0:GT * 2 * E0].rearrange("p (t s e) -> p t e s", t=GT, s=2)
                top, total, inv, den, denc, dinv = (g_s[:, i, :] for i in range(6))
                if k == 1:
                    nc.vector.tensor_reduce(g_l[:], lg, AX_X, ALU.add).then_inc(logits_read.sem, 1)
                    dve.wait_ge(logits_read.sem, logits_read.at(ph, it, 1))
                    ins = nc.vector.tensor_reduce(top, g_l[:], AX_X, ALU.max)
                elif k == 2:
                    ins = nc.vector.tensor_tensor(g_e[:], g_l[:], bc(top, E0), ALU.subtract)
                elif k == 3:
                    ins = nc.vector.tensor_reduce(total, g_x[:], AX_X, ALU.add)
                elif k == 4:
                    ins = nc.vector.reciprocal(inv, total)
                elif k == 5:
                    ins = nc.vector.tensor_tensor(g_p[:], g_x[:], bc(inv, E0), ALU.mult)
                elif k == 6:
                    carry(dve)
                    for j in range(GT):
                        ins = nc.vector.max(g_mx[:, j, :], g_p[:, j, :])
                elif k == 7:
                    carry(dve)
                    for j in range(GT):
                        ins = nc.vector.max_index(g_ix[:, j, :], g_mx[:, j, :], g_p[:, j, :])
                elif k == 8:
                    ins = nc.vector.tensor_copy(g_if[:], g_ix[:, :, 0:2])
                elif k == 9:
                    ins = nc.vector.tensor_tensor(den, g_mx[:, :, 0], g_mx[:, :, 1], ALU.add)
                elif k == 10:
                    ins = nc.vector.tensor_scalar(denc, den, 1e-9, None, ALU.max)
                elif k == 11:
                    ins = nc.vector.reciprocal(dinv, denc)
                elif k == 12:
                    ins = nc.vector.tensor_tensor(g_m[:, 0], iota8[:].unsqueeze(1).broadcast_to([P, GT, E0]),
                                                  bc(g_if[:, :, 0], E0), ALU.is_equal)
                elif k == 13:
                    ins = nc.vector.tensor_tensor(g_m[:, 1], iota8[:].unsqueeze(1).broadcast_to([P, GT, E0]),
                                                  bc(g_if[:, :, 1], E0), ALU.is_equal)
                elif k == 14:
                    ins = nc.vector.tensor_tensor(g_w[:], g_mx[:, :, 0:2], bc(dinv, 2), ALU.mult)
                elif k == 15:
                    ins = nc.vector.tensor_tensor(g_m[:, 2], g_m[:, 0], bc(g_sq[:, :, 0], E0), ALU.mult)
                elif k == 16:
                    ins = nc.vector.tensor_tensor(g_m[:, 3], g_m[:, 1], bc(g_sq[:, :, 1], E0), ALU.mult)
                elif k == 17:
                    ins = nc.vector.tensor_tensor(gate[:, par], g_m[:, 2], g_m[:, 3], ALU.add)
                ins.then_inc(step.sem, 1)

            def gate1(ph, it, par, k):
                step = gate_dve
                if k == 1:
                    dve.wait_ge(logits.sem, logits.at(ph, it, 1))
                elif k == 5:
                    dve.wait_ge(gate_sig.sem, gate_sig.at(ph, it, 1))
                if step.past(ph, it, k - 1) or ph:
                    dve.wait_ge(step.sem, step.at(ph, it, k - 1))
                lg = bank[MISC][:].rearrange("p (t s e) -> p t e s", t=GT, s=2)
                total, guard, inv = (e_s[:, i, :] for i in range(3))

                def halves(t):
                    return t[:].rearrange("p t (h e) -> p t h e", h=2)

                if k == 1:
                    nc.vector.tensor_reduce(e_a[:], lg, AX_X, ALU.add).then_inc(logits_read.sem, 1)
                    dve.wait_ge(logits_read.sem, logits_read.at(ph, it, 1))
                    ins = nc.vector.tensor_tensor(e_b[:], e_a[:], e_bias[:].unsqueeze(1).broadcast_to([P, GT, E1]), ALU.add)
                elif k == 2:
                    carry(dve)
                    for j in range(GT):
                        ins = nc.vector.max(e_mx[:, j, :], e_b[:, j, :])
                elif k == 3:
                    carry(dve)
                    for j in range(GT):
                        ins = nc.vector.match_replace(e_rep[:, j, :], e_mx[:, j, :], e_b[:, j, :], -3e38)
                elif k == 4:
                    ins = nc.vector.tensor_tensor(e_m[:], e_b[:], e_rep[:], ALU.not_equal)
                elif k == 5:
                    ins = nc.vector.tensor_tensor(e_w[:], e_sig[:], e_m[:], ALU.mult)
                elif k == 6:
                    ins = nc.vector.tensor_reduce(total, e_w[:], AX_X, ALU.add)
                elif k == 7:
                    ins = nc.vector.tensor_scalar(guard, total, 1e-8, None, ALU.add)
                elif k == 8:
                    ins = nc.vector.reciprocal(inv, guard)
                elif k == 9:
                    ins = nc.vector.tensor_tensor(e_cw[:], e_w[:], bc(inv, E1), ALU.mult)
                elif k == 10:
                    ins = nc.vector.tensor_copy(parts[:, :, :, 0, :], halves(e_cw))
                elif k == 11:
                    ins = nc.vector.tensor_tensor(halves(e_r1), halves(e_cw), parts[:, :, :, 0, :], ALU.subtract)
                elif k == 12:
                    ins = nc.vector.tensor_copy(parts[:, :, :, 1, :], halves(e_r1))
                elif k == 13:
                    ins = nc.vector.tensor_tensor(halves(e_r2), halves(e_r1), parts[:, :, :, 1, :], ALU.subtract)
                elif k == 14:
                    ins = nc.vector.tensor_copy(parts[:, :, :, 2, :], halves(e_r2))
                ins.then_inc(step.sem, 1)

            def gates_of(ph, nxt, step):
                for k in routing(ph, nxt)[3].get(step, ()):
                    (gate0 if PHASES[nxt[0]] == "F0" else gate1)(*nxt[0:3], k)

            def xe_lo_of(ph, it, e):
                dve.wait_ge(xe_hi.sem, xe_hi.at(ph, it, e + 1))
                nc.vector.tensor_tensor(xelo[:, e % 2, :], bank[4 + e % 2][:], xehi[:, e % 2, :].bitcast(F32),
                                        ALU.subtract).then_inc(xe_lo.sem, 1)

            def lo_of(ph, it, par, c, f, nch):
                s = par * nch + c
                dve.wait_ge(hi_ready.sem, hi_ready.at(ph, it, c + 1))
                nc.vector.tensor_tensor(f["hlo"][:, s % RING, :], f["h"][:, s % HR, :], f["hhi"][:, s % RING, :].bitcast(F32),
                                        ALU.subtract).then_inc(lo_ready.sem, 1)

            def f0_item(ph):
                def item(it, par, first, last):
                    nxt = following(ph, it, par, last)
                    for c in range(NC0):
                        if first and ph in PIECES and c % CPP == CPP - 1 and P0[0] + 2 + c // CPP < P0[1]:
                            piece_lo(P0[0] + 2 + c // CPP)
                        if c % 4 == 1 and c // 4 < E0 and not (first and c == 1):
                            xe_lo_of(ph, it, c // 4)
                        if first and c == 2:
                            xe_lo_of(ph, it, 0)
                        if nxt and c in (5, 6, 7):
                            if c == 5 and ph == 0 and first:
                                dve.wait_ge(dma_x, 16 * (GROUPS - 1))
                            if c == 5 and last:
                                dve.wait_ge(x_added.sem, x_added.at(ph, 1, 0))
                            stats_of(*nxt, c - 5)
                        if c == 10 and nxt:
                            xn_of(*nxt)
                        if c == 9 and not first:
                            x_add(ph, it - 1)
                        if c == 13 and nxt:
                            xt_lo_of(*nxt)
                        gates_of(ph, nxt, c)
                        if c >= 1:
                            lo_of(ph, it, par, c - 1, f0, NC0)
                    lo_of(ph, it, par, NC0 - 1, f0, NC0)
                    if last:
                        x_add(ph, it)
                return item

            def mult_of(ph, it, par, c):
                s = par * NC1 + c
                dve.wait_ge(act_done.sem, act_done.at(ph, it, c + 1))
                wait_lo(dve, ph, it, c - HR)
                hb, rb_ = f1["h"][:, s % HR, :], f1["r"][:, s % RR, :]
                if c == 0:
                    ins = nc.vector.tensor_copy(hb, rb_)
                else:
                    dve.wait_ge(cb_done.sem, cb_done.at(ph, it, c))
                    ins = nc.vector.tensor_tensor(hb, bank[4 + (c - 1) % 2][:], rb_, ALU.mult)
                ins.then_inc(h_ready.sem, 1)

            def f1_item(ph):
                def item(it, par, first, last):
                    nxt = following(ph, it, par, last)
                    for c in range(NC1):
                        if first and ph in PIECES and c % CPP == CPP - 1 and P1[0] + 2 + c // CPP < P1[1]:
                            piece_lo(P1[0] + 2 + c // CPP)
                        if nxt and c in (5, 6, 7):
                            if c == 5 and last:
                                dve.wait_ge(x_added.sem, x_added.at(ph, 1, 0))
                            stats_of(*nxt, c - 5)
                        if c == 10 and nxt:
                            xn_of(*nxt)
                        if c == 9 and not first:
                            x_add(ph, it - 1)
                        if c == 13 and nxt:
                            xt_lo_of(*nxt)
                        gates_of(ph, nxt, c)
                        mult_of(ph, it, par, c)
                        if c >= 1 and c - 1 not in POOL_LO:
                            lo_of(ph, it, par, c - 1, f1, NC1)
                    lo_of(ph, it, par, NC1 - 1, f1, NC1)
                    if last:
                        x_add(ph, it)
                return item

            def mask_of(ph, a, it, par, u):
                dve.wait_ge(scores.sem, scores.at(ph, it, u + 1))
                if exp_done.past(ph, it, u - 1):
                    dve.wait_ge(exp_done.sem, exp_done.at(ph, it, u - 1))
                carry(dve)
                for t in range(BT):
                    cols = slice(0, 128) if t == 0 else slice(128, 320)
                    ins = nc.vector.tensor_tensor_reduce(
                        out=MASKEDS[a.kind][:, u % 2, cols], in0=bank[u % 2][:, cols], in1=mask[:, cols], scale=-a.scale,
                        scalar=3e38, op0=ALU.add, op1=ALU.min, accum_out=negmax[:, u % PR, t:t + 1])
                ins.then_inc(masked_ready.sem, 1)

            def pt_of(ph, it, u):
                dve.wait_ge(p_turned.sem, p_turned.at(ph, it, u + 1))
                if pv_done.past(ph, it, u - 3):
                    dve.wait_ge(pv_done.sem, pv_done.at(ph, it, u - 3))
                nc.vector.tensor_copy(PTS[PHASES[ph]][:, u % 4, :], bank[2 + u % 2][:, 0:384]).then_inc(pt_ready.sem, 1)

            def rsum_of(ph, it, u):
                dve.wait_ge(exp_done.sem, exp_done.at(ph, it, u + 1))
                pair = slice(u % PR - 1, u % PR + 1)
                nc.vector.reciprocal(rsums[:, pair, :], sums[:, pair, :]).then_inc(rsum_ready.sem, 1)

            def qk_of(ph, it, par, i):
                dve.wait_ge(qk_parts.sem, qk_parts.at(ph, it, i + 1))
                if scores.past(ph, it - 1, 0):
                    dve.wait_ge(scores.sem, scores.at(ph, it - 1, 0))
                for w in range(2):
                    ins = nc.vector.scalar_tensor_tensor(
                        out=qk1[:, par, i, w, :], in0=qk_h[:, i % 2, w, :].bitcast(F32), scalar=less_hi[:, w:w + 1],
                        in1=qk_v[:, i % 2, w, :], op0=ALU.mult, op1=ALU.add)
                ins.then_inc(qk_ready.sem, 1)

            def y_of(ph, a, it):
                b = bank[6 + a.index("Y", 0) % 2]
                dve.wait_ge(y_done.sem, y_done.at(ph, it, 1))
                xs = x[:, bass.ds(it * BT, BT), :].rearrange("p t d -> p (t d)")
                nc.vector.tensor_tensor(xs, b[:, 0:256], xs, ALU.add).then_inc(x_added.sem, 1)

            def attention_item(ph, a):
                def item(it, par, first, last):
                    nxt = following(ph, it, par, last)
                    for u in steps(last):
                        if u < HEADS:
                            mask_of(ph, a, it, par, u)
                        sum_of = late(u, SUM_LAG, it, par, first)
                        if sum_of and sum_of[2] % 2:
                            rsum_of(ph, sum_of[0], sum_of[2])
                        turned = late(u, TURN_LAG, it, par, first)
                        if turned:
                            pt_of(ph, turned[0], turned[2])
                        if nxt and u == 0:
                            if last:
                                dve.wait_ge(x_added.sem, x_added.at(ph, 2, 0))
                            stats_of(*nxt, 0)
                        if nxt and u == 1:
                            stats_of(*nxt, 1)
                            stats_of(*nxt, 2)
                        if nxt and u == 3:
                            xn_of(*nxt)
                        if nxt and u == a.xt_step + 1:
                            xt_lo_of(*nxt)
                        for step, name, i, offset in a.jobs:
                            if a is A1 and name == "QK" and step + 3 == u and not (last and offset):
                                qk_of(ph, it + offset, par ^ offset, i)
                        if last:
                            gates_of(ph, nxt, u)
                        if u == a.y_step + a.y_steps and not first:
                            y_of(ph, a, it - 1)
                    if last:
                        y_of(ph, a, it)
                return item

            dve.wait_ge(dma_x0, 16)
            for step in range(3):
                stats_of(0, 0, 0, GT, step)
            xn_of(0, 0, 0, GT)
            dve.wait_ge(dma_const, 112)
            for split, cols in ((router0, slice(0, E0)), (router1, slice(E0, E0 + E1))):
                nc.vector.tensor_copy(split[:, 0, :], router[:, cols]).then_inc(router_split, 1)
            dve.wait_ge(router_split, 2)
            for split, cols in ((router0, slice(0, E0)), (router1, slice(E0, E0 + E1))):
                nc.vector.tensor_tensor(split[:, 1, :], router[:, cols], split[:, 0, :].bitcast(F32),
                                        ALU.subtract).then_inc(router_split, 1)
            for ph, kind in enumerate(PHASES):
                enter(dve, ph)
                if ph == 0:
                    xt_lo_of(ph, 0, 0, GT)
                if ph in PIECES:
                    piece_lo(PIECES[ph][0])
                    piece_lo(PIECES[ph][0] + 1)
                if kind in ("A0", "A1"):
                    a = A0 if kind == "A0" else A1
                    for i in range(PIECES[ph][0] + 2, PIECES[ph][1]):
                        piece_lo(i)
                    if a is A1:
                        dve.wait_ge(dma_a1, 64)
                        for _, name, i, offset in a.jobs:
                            if name == "QK" and offset == 1:
                                qk_of(ph, 0, 0, i)
                    items(dve, ph, attention_item(ph, a))
                if kind == "F0":
                    if ph == 0:
                        for k in range(1, gate_dve.per["F0"] + 1):
                            gate0(ph, 0, 0, k)
                    items(dve, ph, f0_item(ph))
                if kind == "F1":
                    items(dve, ph, f1_item(ph))
                leave(dve)

        @block.tensor
        def _(pe):
            def three(o, whi, wlo, vhi, vlo, start=True, stop=True):
                nc.tensor.matmul(o, whi, vhi, start=start, stop=False)
                nc.tensor.matmul(o, whi, vlo, start=False, stop=False)
                return nc.tensor.matmul(o, wlo, vhi, start=False, stop=stop)

            def turn_xn(ph, it, par, tiles):
                pe.wait_ge(xn_ready.sem, xn_ready.at(ph, it, 1))
                for j in range(tiles):
                    mm = nc.tensor.transpose(bank[MISC][:, j * P:(j + 1) * P], xn[:, par, j, :], ident[:])
                mm.then_inc(xn_turned.sem, 1)

            def turn_next(ph, it, nxt):
                if x_added.past(ph, it, 0):
                    pe.wait_ge(x_added.sem, x_added.at(ph, it, 0))
                if PHASES[ph] == "F1":
                    pe.wait_ge(cwt_ready.sem, cwt_ready.at(ph, it + 1, 0))
                turn_xn(*nxt)

            def route(ph, it, par):
                pe.wait_ge(xt_lo.sem, xt_lo.at(ph, it, 1))
                split, ne = (router0, E0) if PHASES[ph] == "F0" else (router1, E1)
                for j in range(GT):
                    o = bank[MISC][:, j * 2 * ne:(j + 1) * 2 * ne]
                    tok, both = slice(j * P, (j + 1) * P), split[:].rearrange("p s e -> p (s e)")
                    nc.tensor.matmul(o, xthi[:, par, tok], both, start=True, stop=False)
                    mm = nc.tensor.matmul(o, xtlo[:, par, tok], both, start=False, stop=True)
                mm.then_inc(logits.sem, 1)

            def turn_xe(ph, it, e):
                pe.wait_ge(xe_ready.sem, xe_ready.at(ph, it, e + 1))
                if xe_lo.past(ph, it, e - 1):
                    pe.wait_ge(xe_lo.sem, xe_lo.at(ph, it, e - 1))
                for j in range(GT):
                    mm = nc.tensor.transpose(bank[4 + e % 2][:, j * P:(j + 1) * P], xe[:, e % 2, j, :], ident[:])
                mm.then_inc(xe_turned.sem, 1)

            def turn_cw(ph, it):
                pe.wait_ge(gate_dve.sem, gate_dve.at(ph, it, gate_dve.per["F1"]))
                turned = bank[MISC][0:96, :].bitcast(BF16)
                for h in range(2):
                    for j in range(GT):
                        mm = nc.tensor.transpose(turned[:, (h * GT + j) * P:(h * GT + j + 1) * P],
                                                 parts[:, j, h, :, :].rearrange("p k e -> p (k e)"), ident_b[:])
                mm.then_inc(cw_turned.sem, 1)

            def turn_acc(ph, it, prepared):
                pe.wait_ge(acc_copied.sem, acc_copied.at(ph, it, 1))
                pe.wait_ge(logits_read.sem, logits_read.at(ph, prepared, 1))
                if PHASES[ph] == "F1":
                    pe.wait_ge(cwt_ready.sem, cwt_ready.at(ph, prepared, 1))
                for j in range(GT):
                    mm = nc.tensor.transpose(bank[MISC][:, j * P:(j + 1) * P], acc_sb[:, j * P:(j + 1) * P], ident[:])
                mm.then_inc(y_turned.sem, 1)

            def up(ph, it, par, c, nch, whi, wlo, vhi, vlo):
                s = par * nch + c
                if act_done.past(ph, it, c + 1 - UPB):
                    pe.wait_ge(act_done.sem, act_done.at(ph, it, c + 1 - UPB))
                three(bank[s % UPB][:], whi[:, c, 0:128], wlo[:, c, 0:128], vhi, vlo).then_inc(up_done.sem, 1)

            def down(ph, it, par, c, nch, whi, wlo, f):
                s = par * nch + c
                wait_lo(pe, ph, it, c)
                if c == 0 and acc_copied.past(ph, it, -1):
                    pe.wait_ge(acc_copied.sem, acc_copied.at(ph, it, -1))
                three(acc_bank(par)[:], whi[:, c, 128:256], wlo[:, c, 128:256], f["hhi"][:, s % RING, :],
                      f["hlo"][:, s % RING, :], start=(c == 0), stop=(c == nch - 1)).then_inc(down_done.sem, 1)

            def lagged_down(ph, it, par, c, first, nch, whi, wlo, f):
                if c >= LAG:
                    down(ph, it, par, c - LAG, nch, whi, wlo, f)
                elif not first:
                    down(ph, it - 1, 1 - par, nch + c - LAG, nch, whi, wlo, f)

            def tail(ph, it, par, nch, whi, wlo, f):
                if PHASES[ph] == "F1":
                    cb(ph, it, par, nch - 1)
                for c in range(nch - LAG, nch):
                    down(ph, it, par, c, nch, whi, wlo, f)
                if ph + 1 < len(PHASES):
                    pe.wait_ge(xt_lo.sem, xt_lo.at(ph + 1, 0, 1))
                    if PHASES[ph + 1] in ("F0", "F1"):
                        pe.wait_ge(logits_read.sem, logits_read.at(ph + 1, 0, 1))
                turn_acc(ph, it, it)

            def f0_item(ph):
                def item(it, par, first, last):
                    nxt = following(ph, it, par, last)
                    for c in range(NC0):
                        if first and ph in PIECES and c % CPP == 0:
                            pe.wait_ge(w_lo, P0[0] + c // CPP + 1)
                        if c % 4 == 1 and c // 4 < E0 and not (first and c == 1):
                            turn_xe(ph, it, c // 4)
                        if first and c == 2:
                            turn_xe(ph, it, 0)
                        if c < SH0:
                            vhi, vlo = xthi[:, par, :], xtlo[:, par, :]
                        else:
                            e = (c - SH0) // SH0
                            if c % SH0 == 0:
                                pe.wait_ge(xe_lo.sem, xe_lo.at(ph, it, e + 1))
                            vhi, vlo = xehi[:, e % 2, :], xelo[:, e % 2, :]
                        up(ph, it, par, c, NC0, w0hi, w0lo, vhi, vlo)
                        lagged_down(ph, it, par, c, first, NC0, w0hi, w0lo, f0)
                        if c == 8 and not first:
                            turn_acc(ph, it - 1, it)
                        if c == 13 and nxt:
                            turn_next(ph, it, nxt)
                        if c == routing(ph, nxt)[0]:
                            route(*nxt[0:3])
                    if last:
                        tail(ph, it, par, NC0, w0hi, w0lo, f0)
                return item

            def cb(ph, it, par, c):
                if c == 1:
                    pe.wait_ge(cwt_ready.sem, cwt_ready.at(ph, it, 1))
                if h_ready.past(ph, it, c - 1):
                    pe.wait_ge(h_ready.sem, h_ready.at(ph, it, c - 1))
                half, j = divmod(c - 1, 16)
                nc.tensor.matmul(bank[4 + (c - 1) % 2][:], sel[:, j, :], cwt[:, par, half, :],
                                 start=True, stop=True).then_inc(cb_done.sem, 1)

            def f1_item(ph):
                def item(it, par, first, last):
                    nxt = following(ph, it, par, last)
                    for c in range(NC1):
                        if first and ph in PIECES and c % CPP == 0:
                            pe.wait_ge(w_lo, P1[0] + c // CPP + 1)
                        up(ph, it, par, c, NC1, w1hi, w1lo, xthi[:, par, :], xtlo[:, par, :])
                        if c == 2 and first:
                            pe.wait_ge(dma_sel, 16)
                        if c >= 2:
                            cb(ph, it, par, c - 1)
                        elif c == 0 and not first:
                            cb(ph, it - 1, 1 - par, NC1 - 1)
                        lagged_down(ph, it, par, c, first, NC1, w1hi, w1lo, f1)
                        if c == 8 and not first:
                            turn_acc(ph, it - 1, it)
                        if c == 13 and nxt:
                            turn_next(ph, it, nxt)
                        if c == routing(ph, nxt)[0]:
                            route(*nxt[0:3])
                        if c == 26 and not last:
                            turn_cw(ph, it + 1)
                    if last:
                        tail(ph, it, par, NC1, w1hi, w1lo, f1)
                return item

            def job_pe(ph, a, item_kind, it, par, name, i, here):
                index = a.index(name, 0 if name == "XT" else i)
                b = bank[6 + index % 2]
                prev = a.before(item_kind, index)
                if prev:
                    back, pname, pi, offset = prev
                    batch = here - back + offset
                    read = job_read(a, pname)
                    pe.wait_ge(read.sem, read.at(ph, batch, pi + 1))
                if name == "XT":
                    turn_xn(*i)
                if name == "QK":
                    if i == 0:
                        pe.wait_ge(xt_lo.sem, xt_lo.at(ph, it, 1))
                    for w in range(2):
                        if a is A0:
                            cols = slice(1024 * w + P * i, 1024 * w + P * i + P)
                            whi, wlo = wqkv_hi[:, cols], wqkv_lo[:, cols]
                        else:
                            cols = slice(P * (2 * i + w), P * (2 * i + w) + P)
                            whi, wlo = wa1_hi[:, cols], wa1_lo[:, cols]
                        mm = three(b[:, 256 * w:256 * w + 256], whi, wlo, xthi[:, par, 0:256], xtlo[:, par, 0:256])
                    mm.then_inc(qk_done.sem, 1)
                if name == "V":
                    if a is A0:
                        half, t = divmod(i, 2)
                        tok = slice(P * t, P * t + P)
                        cols = slice(2048 + 512 * half, 2048 + 512 * half + 512)
                        mm = three(b[:], xthi[:, par, tok], xtlo[:, par, tok], wqkv_hi[:, cols], wqkv_lo[:, cols])
                    else:
                        tok = slice(P * i, P * i + P)
                        cols = slice(1024, 1024 + P)
                        three(b[:, 0:P], xthi[:, par, tok], xtlo[:, par, tok], wa1_hi[:, cols], wa1_lo[:, cols], stop=False)
                        mm = nc.tensor.matmul(b[:, 0:P], brow1[:, 0:P], brow1[:, P + D:P + D + P], start=False, stop=True)
                    mm.then_inc(v_done.sem, 1)
                if name == "Y":
                    pe.wait_ge(ot_ready.sem, ot_ready.at(ph, it + 1, 0))

            def y_part(a, part):
                b = bank[6 + a.index("Y", 0) % 2]
                products = [(t, c) for t in range(BT) for c in range(a.chunks)]
                share = (len(products) + a.y_steps - 1) // a.y_steps
                w = wout if a is A0 else wo1
                for t, c in products[part * share:(part + 1) * share]:
                    o = b[:, t * P:(t + 1) * P]
                    end = c == a.chunks - 1
                    mm = nc.tensor.matmul(o, OT[a.kind][:, c, t * P:(t + 1) * P], w[:, c, :], start=(c == 0), stop=(a is A0 and end))
                    if a is A1 and end:
                        mm = nc.tensor.matmul(o, brow1[:, 0:P], brow1[:, P:P + D], start=False, stop=True)
                if part == a.y_steps - 1:
                    mm.then_inc(y_done.sem, 1)

            def scores_of(ph, a, it, par, u):
                c, r = divmod(u, a.heads_a_chunk)
                if r == 0:
                    pe.wait_ge(qk_ready.sem, qk_ready.at(ph, it, c + 1))
                if masked_ready.past(ph, it, u - 1):
                    pe.wait_ge(masked_ready.sem, masked_ready.at(ph, it, u - 1))
                rows = slice(a.rows * r, a.rows * r + a.rows)
                q, k = QK[a.kind][rows, par, c, 0, :], QK[a.kind][rows, par, c, 1, :]
                nc.tensor.matmul(bank[u % 2][:, 0:128], q[:, 0:128], k[:, 0:128], start=True, stop=True)
                nc.tensor.matmul(bank[u % 2][:, 128:320], q[:, 128:256], k[:, 64:256],
                                 start=True, stop=True).then_inc(scores.sem, 1)

            def turn_p(ph, it, u):
                pe.wait_ge(p_ready.sem, p_ready.at(ph, it, u + 1))
                if pt_ready.past(ph, it, u - 1):
                    pe.wait_ge(pt_ready.sem, pt_ready.at(ph, it, u - 1))
                for c in range(3):
                    keys = slice(c * P, (c + 1) * P)
                    mm = nc.tensor.transpose(bank[2 + u % 2][:, keys], PROBS[PHASES[ph]][:, u % PR, keys], ident[:])
                mm.then_inc(p_turned.sem, 1)

            def pv_of(ph, a, it, par, u):
                k, g = divmod(u, a.group)
                pe.wait_ge(pt_ready.sem, pt_ready.at(ph, it, u + 1))
                if g == 0:
                    pe.wait_ge(v_ready.sem, v_ready.at(ph, it, 2 * (u // 8) + 2 if a is A0 else 2))
                    if ot_ready.past(ph, it, k - 1):
                        pe.wait_ge(ot_ready.sem, ot_ready.at(ph, it, k - 1))
                c, r = divmod(g, a.heads_a_chunk)
                rows = slice(a.rows * r, a.rows * r + a.rows)
                if a is A0:
                    v = [v0[:, par, t, 64 * u:64 * u + 64] for t in range(BT)]
                else:
                    v = [v1[:, par, t, 32 * (u // 4):32 * (u // 4) + 32] for t in range(BT)]
                o, pt = bank[4 + k % 2], PTS[a.kind]
                nc.tensor.matmul(o[rows, 256 * c:256 * c + 256], v[0], pt[:, u % 4, 0:256], start=True, stop=False)
                nc.tensor.matmul(o[rows, 256 * c + 128:256 * c + 256], v[1], pt[:, u % 4, 256:384],
                                 start=False, stop=True).then_inc(pv_done.sem, 1)

            def attention_item(ph, a):
                def item(it, par, first, last):
                    nxt = following(ph, it, par, last)
                    kind = 0 if first else 2 if last else 1
                    for u in steps(last):
                        if u < HEADS:
                            scores_of(ph, a, it, par, u)
                        turned = late(u, TURN_LAG, it, par, first)
                        if turned:
                            turn_p(ph, turned[0], turned[2])
                        summed = late(u, PV_LAG, it, par, first)
                        if summed:
                            pv_of(ph, a, *summed)
                        if last and u == routing(ph, nxt)[0]:
                            pe.wait_ge(v_ready.sem, v_ready.at(ph, it + 1, 0))
                            route(*nxt[0:3])
                        for step, name, i, offset in a.jobs:
                            if step == u and name == "XT" and nxt:
                                job_pe(ph, a, kind, None, None, "XT", nxt, it)
                            if step == u and name in ("QK", "V") and not (last and offset):
                                job_pe(ph, a, kind, it + offset, par ^ offset, name, i, it)
                            if name == "Y" and not first and 0 <= u - step < a.y_steps:
                                if step == u:
                                    job_pe(ph, a, kind, it - 1, 1 - par, name, i, it)
                                y_part(a, u - step)
                    if last:
                        job_pe(ph, a, 3, it, par, "Y", 0, it + 1)
                        for part in range(a.y_steps):
                            y_part(a, part)
                return item

            pe.wait_ge(dma_const, 112)
            for ph, kind in enumerate(PHASES):
                enter(pe, ph)
                if kind in ("A0", "A1"):
                    a = A0 if kind == "A0" else A1
                    if a is A0:
                        pe.wait_ge(dma_wout, 16)
                    else:
                        pe.wait_ge(dma_a1, 64)
                    pe.wait_ge(probs_zeroed, 1 if a is A0 else 2)
                    for _, name, i, offset in a.jobs:
                        if name in ("QK", "V") and offset == 1:
                            cols = 3 * 1024 if name == "V" else (1024 if a is A0 else P * (i + 1)) + P * (i + 1)
                            pe.wait_ge(w_lo, min(PIECES[ph][0] + (cols + PIECE - 1) // PIECE, PIECES[ph][1]))
                            job_pe(ph, a, -1, 0, 0, name, i, -1)
                    items(pe, ph, attention_item(ph, a))
                if ph == 0:
                    turn_xn(ph, 0, 0, GT)
                    pe.wait_ge(router_split, 4)
                    route(ph, 0, 0)
                if kind == "F0":
                    items(pe, ph, f0_item(ph))
                if kind == "F1":
                    turn_cw(ph, 0)
                    items(pe, ph, f1_item(ph))
                leave(pe)


def kernel(**inputs):
    import numpy as np
    import concourse.bacc as bacc
    from concourse.bass_utils import run_bass_kernel_spmd as run

    def f32(name):
        return np.ascontiguousarray(inputs[name])

    def chunks(fc, proj):
        n = fc.shape[0] // P
        up = fc.reshape(n, P, D).transpose(2, 0, 1)
        down = proj.reshape(D, n, P).transpose(2, 1, 0)
        return np.ascontiguousarray(np.concatenate([up, down], axis=2).reshape(P, n * 256))

    fc, proj = f32("L0_ffn_w_fc"), f32("L0_ffn_w_proj")
    w0 = np.concatenate([
        chunks(f32("L0_ffn_shared_fc"), f32("L0_ffn_shared_proj")),
        *[chunks(fc[e], proj[e]) for e in range(E0)]], axis=1)
    up1, down1 = f32("L1_ffn_W_up"), f32("L1_ffn_W_down")
    pad = np.zeros((D, FF1), up1.dtype)
    fc1 = np.concatenate([f32("L1_ffn_Ws_up"), pad, up1.transpose(1, 0, 2).reshape(D, E1 * FF1)], axis=1).T
    proj1 = np.concatenate([f32("L1_ffn_Ws_down"), pad.T, down1.reshape(E1 * FF1, D)], axis=0).T
    w1 = chunks(np.ascontiguousarray(fc1), np.ascontiguousarray(proj1))

    wq, bq = f32("L1_attn_Wq").reshape(D, KV1, 4, 1, DH1), f32("L1_attn_bq").reshape(KV1, 4, 1, DH1)
    wk, bk = f32("L1_attn_Wk").reshape(D, KV1, 1, 1, DH1), f32("L1_attn_bk").reshape(KV1, 1, 1, DH1)
    wa = np.zeros((D, KV1, 2, 4, 4, DH1), np.float32)
    ba = np.zeros((KV1, 2, 4, 4, DH1), np.float32)
    wa[:, :, 0], wa[:, :, 1] = wq, wk
    ba[:, 0], ba[:, 1] = bq, bk
    wv = np.zeros((D, KV1, 32), np.float32)
    wv[:, :, 0:DH1] = f32("L1_attn_Wv").reshape(D, KV1, DH1)
    bv = np.zeros((KV1, 32), np.float32)
    bv[:, 0:DH1] = f32("L1_attn_bv").reshape(KV1, DH1)
    wo = np.zeros((HEADS, 32, D), np.float32)
    wo[:, 0:DH1] = f32("L1_attn_Wo").reshape(HEADS, DH1, D)
    wa1 = np.concatenate([wa.reshape(D, 1024), wv.reshape(D, P)], axis=1)
    is_lo = np.zeros((2, 4, 4, DH1), bool)
    is_lo[0, :, 1::2], is_lo[1, :, 2:4] = True, True
    is_lo = is_lo.reshape(2, P)
    ba = ba.reshape(8, P)
    bqk1 = np.concatenate([ba, np.where(is_lo, -1, 0)]).astype(np.float32).T.copy()
    brow1 = np.concatenate([np.ones(P, np.float32), f32("L1_attn_bo"), bv.reshape(P)])[None, :]

    const = np.zeros((P, 456), np.float32)
    const[:, 0:128] = np.eye(P)
    q = np.arange(P)[:, None]
    k0 = np.arange(128)[None, :]
    const[:, 128:256] = np.where((k0 <= q) & (k0 > q - WINDOW), 0, MASKED)
    k1 = np.arange(64, 256)[None, :]
    const[:, 256:448] = np.where((k1 <= q + P) & (k1 > q + P - WINDOW), 0, MASKED)
    const[:, 448:456] = np.arange(8)[None, :]
    sel = np.zeros((P, 17, P), np.float32)
    for j in range(16):
        for part in range(3):
            sel[part * 32 + 2 * j, j, 0:64] = 1
            sel[part * 32 + 2 * j + 1, j, 64:128] = 1
    sel[:, 16, :] = np.eye(P)
    import ml_dtypes
    sel = sel.reshape(P, 17 * P).astype(ml_dtypes.bfloat16)

    arrays = {
        "x": f32("L0_attn_x"), "w0": w0, "router": np.ascontiguousarray(f32("L0_ffn_router_w").T),
        "wqkv": f32("L0_attn_Wqkv"), "wout": f32("L0_attn_Wout"), "w1": w1,
        "cent": np.ascontiguousarray(f32("L1_ffn_centroids").T), "bias1": f32("L1_ffn_expert_biases"),
        "const": const, "sel": sel,
        "wa1": wa1, "bqk1": bqk1, "wo1": wo.reshape(HEADS * 32, D), "brow1": brow1,
    }
    nc = bacc.Bacc("TRN2", target_bir_lowering=False, num_devices=1, dynamic_dma_scratch_size=1024)
    aps = [nc.dram_tensor("in_" + n, a.shape, mybir.dt.from_np(a.dtype), kind="ExternalInput").ap()
           for n, a in arrays.items()]
    out = nc.dram_tensor("out_0", arrays["x"].shape, F32, kind="ExternalOutput").ap()
    build(nc, *aps, out)
    res = run(nc, [{"in_" + n: a for n, a in arrays.items()}], core_ids=[0])
    return res.results[0]["out_0"]
```
